# Optimizing a Trainium2 kernel written in Bass

```python
import numpy as np
import jax
import jax.numpy as jnp

def _softmax(x, axis=-1):
    return jax.nn.softmax(x, axis=axis)

def _gelu(x):
    return jax.nn.gelu(x, approximate=True)

def _silu(x):
    return jax.nn.silu(x)

def _sigmoid(x):
    return jax.nn.sigmoid(x)

def _layernorm(x, axis=-1, eps=1e-05):
    m = jnp.mean(x, axis=axis, keepdims=True)
    v = jnp.var(x, axis=axis, keepdims=True)
    return (x - m) / jnp.sqrt(v + eps)

def _scatter_add(tgt, idx, src, axis=0):
    return tgt.at[idx].add(src)

def _segment_sum(src, seg, n):
    return jax.ops.segment_sum(src, seg, n)
kernel_name = 'mk_prb_d2_jaxref_r8_e48ce8'

def setup_inputs(seed: int=0):
    np.random.seed(seed)
    _w = jnp.asarray

    def _L0_attn_setup():
        import jax, jax.numpy as jnp
        import numpy as np
        D_MODEL = 128
        N_HEADS = 16
        WINDOW = 128
        TOPK_RATIO = 0.25
        N_GLOBAL = 64
        B, N = (2, 256)
        key = jax.random.key(seed)
        ks = jax.random.split(key, 8)
        s = 0.02
        return {'x': jax.random.normal(ks[0], (B, N, D_MODEL), jnp.float32), 'Wq': jax.random.normal(ks[1], (D_MODEL, D_MODEL), jnp.float32) * s, 'bq': jnp.zeros((D_MODEL,), jnp.float32), 'Wk': jax.random.normal(ks[2], (D_MODEL, D_MODEL), jnp.float32) * s, 'bk': jnp.zeros((D_MODEL,), jnp.float32), 'Wv': jax.random.normal(ks[3], (D_MODEL, D_MODEL), jnp.float32) * s, 'bv': jnp.zeros((D_MODEL,), jnp.float32), 'Wo': jax.random.normal(ks[4], (D_MODEL, D_MODEL), jnp.float32) * s, 'bo': jnp.zeros((D_MODEL,), jnp.float32), 'Ws': jax.random.normal(ks[5], (N_HEADS, D_MODEL), jnp.float32) * s, 'bs': jnp.zeros((N_HEADS,), jnp.float32)}
    _L0_attn_in = _L0_attn_setup()

    def _L0_ffn_setup():
        import jax, jax.numpy as jnp
        import numpy as np
        D = 128
        H = 4
        HD = D // H
        E = 8
        FF = 512
        CAP_FACTOR = 1.0

        def _ln(x, g, b, eps=1e-05):
            mu = jnp.mean(x, -1, keepdims=True)
            v = jnp.mean((x - mu) ** 2, -1, keepdims=True)
            return (x - mu) * jax.lax.rsqrt(v + eps) * g + b

        def _mha(x, w, b, ow, ob):
            L, N, _ = x.shape
            qkv = x @ w.T + b
            q, k, v = jnp.split(qkv, 3, axis=-1)
            rh = lambda t: t.reshape(L, N, H, HD).transpose(1, 2, 0, 3)
            q, k, v = (rh(q), rh(k), rh(v))
            scores = jnp.einsum('nhld,nhmd->nhlm', q, k) / np.float32(np.sqrt(HD))
            attn = jax.nn.softmax(scores, axis=-1)
            o = jnp.einsum('nhlm,nhmd->nhld', attn, v).transpose(2, 0, 1, 3).reshape(L, N, D)
            return o @ ow.T + ob

        def _moe(x, wg, w1, b1, w2, b2):
            L, N, _ = x.shape
            S = L * N
            cap = int(CAP_FACTOR * S) // E
            xf = x.reshape(S, D)
            gates = jax.nn.softmax(xf @ wg, axis=-1)
            idx = jnp.argmax(gates, axis=-1)
            mask1 = jax.nn.one_hot(idx, E, dtype=x.dtype)
            loc = jnp.sum((jnp.cumsum(mask1, 0) - 1.0) * mask1, -1).astype(jnp.int32)
            keep = loc < cap
            gate_val = jnp.take_along_axis(gates, idx[:, None], -1)[:, 0]
            slot = jnp.where(keep, idx.astype(jnp.int32) * cap + loc, E * cap)
            disp = jnp.zeros((E * cap, D), x.dtype).at[slot].set(xf, mode='drop')
            disp = disp.reshape(E, cap, D)
            h = jnp.einsum('ecd,edf->ecf', disp, w1) + b1[:, None, :]
            y = (jnp.einsum('ecf,efd->ecd', h, w2) + b2[:, None, :]).reshape(E * cap, D)
            out = jnp.where(keep[:, None], gate_val[:, None] * y[jnp.minimum(slot, E * cap - 1)], 0.0)
            return out.reshape(L, N, D)
        key = jax.random.key(seed)
        ks = jax.random.split(key, 8)
        L, N = (128, 16)
        s = 0.02
        return {'x': jax.random.normal(ks[0], (L, N, D), jnp.float32), 'in_proj_w': jax.random.normal(ks[1], (3 * D, D), jnp.float32) * s, 'in_proj_b': jnp.zeros((3 * D,), jnp.float32), 'out_proj_w': jax.random.normal(ks[2], (D, D), jnp.float32) * s, 'out_proj_b': jnp.zeros((D,), jnp.float32), 'ln1_g': jnp.ones((D,), jnp.float32), 'ln1_b': jnp.zeros((D,), jnp.float32), 'ln2_g': jnp.ones((D,), jnp.float32), 'ln2_b': jnp.zeros((D,), jnp.float32), 'wg': jax.random.normal(ks[3], (D, E), jnp.float32) * s, 'w1': jax.random.normal(ks[4], (E, D, FF), jnp.float32) * s, 'b1': jnp.zeros((E, FF), jnp.float32), 'w2': jax.random.normal(ks[5], (E, FF, D), jnp.float32) * s, 'b2': jnp.zeros((E, D), jnp.float32)}
    _L0_ffn_in = _L0_ffn_setup()

    def _L1_attn_setup():
        import jax, jax.numpy as jnp
        import numpy as np
        D_MODEL = 128
        N_HEADS = 16
        D_HEAD = D_MODEL // N_HEADS
        RPE_HIDDEN = 32

        def _rpe_bias(T, w1, b1, w2, b2):
            pos = jnp.arange(T, dtype=jnp.float32)
            rel = pos[:, None] - pos[None, :]
            rel = jnp.sign(rel) * jnp.log1p(jnp.abs(rel))
            h = jax.nn.relu(rel[..., None] * w1[0] + b1)
            bias = h @ w2 + b2
            return jnp.transpose(bias, (2, 0, 1))
        key = jax.random.key(seed)
        ks = jax.random.split(key, 8)
        B, T = (2, 256)
        s = lambda fan_in: 1.0 / np.sqrt(fan_in)
        return {'x': jax.random.normal(ks[0], (B, T, D_MODEL), dtype=jnp.float32), 'w_qkv': jax.random.uniform(ks[1], (D_MODEL, 3 * D_MODEL), jnp.float32, -s(D_MODEL), s(D_MODEL)), 'b_qkv': jnp.zeros((3 * D_MODEL,), jnp.float32), 'w_out': jax.random.uniform(ks[2], (D_MODEL, D_MODEL), jnp.float32, -s(D_MODEL), s(D_MODEL)), 'b_out': jnp.zeros((D_MODEL,), jnp.float32), 'w1_rpe': jax.random.uniform(ks[3], (1, RPE_HIDDEN), jnp.float32, -1.0, 1.0), 'b1_rpe': jax.random.uniform(ks[4], (RPE_HIDDEN,), jnp.float32, -1.0, 1.0), 'w2_rpe': jax.random.uniform(ks[5], (RPE_HIDDEN, N_HEADS), jnp.float32, -s(RPE_HIDDEN), s(RPE_HIDDEN)), 'b2_rpe': jnp.zeros((N_HEADS,), jnp.float32)}
    _L1_attn_in = _L1_attn_setup()

    def _L1_ffn_setup():
        import jax, jax.numpy as jnp
        import numpy as np
        DIM = 128
        DEPTH = 6
        HEADS = 16
        DIM_HEAD = 64
        WINDOW = 32
        INNER = HEADS * DIM_HEAD
        DIM_INNER = int(DIM * 4 * 2 / 3)
        QK_SCALE = 8.0

        def shift_tokens(t):
            a, s = jnp.split(t, 2, -1)
            s = jnp.pad(s, ((0, 0), (1, 0), (0, 0)))[:, :-1]
            return jnp.concatenate([a, s], -1)

        def l2norm(t):
            return t / jnp.maximum(jnp.linalg.norm(t, axis=-1, keepdims=True), 1e-12)

        def rotate_half(x):
            x1, x2 = jnp.split(x, 2, -1)
            return jnp.concatenate([-x2, x1], -1)

        def rotary_tables(n):
            half = jnp.arange(0, DIM_HEAD, 2, dtype=jnp.float32)
            inv_freq = 1.0 / 10000.0 ** (half / DIM_HEAD)
            t = jnp.arange(n, dtype=jnp.float32)
            freqs = t[:, None] * inv_freq[None, :]
            freqs = jnp.concatenate([freqs, freqs], -1)
            base_scale = (half + 0.4 * DIM_HEAD) / (1.4 * DIM_HEAD)
            power = (t - n // 2) / (WINDOW // 2)
            scale = base_scale[None, :] ** power[:, None]
            scale = jnp.concatenate([scale, scale], -1)
            return (freqs, scale)

        def local_attention(q, k, v):
            b, h, n, d = q.shape
            w = WINDOW
            nw = n // w
            bq = q.reshape(b, h, nw, w, d)
            bk = k.reshape(b, h, nw, w, d)
            bv = v.reshape(b, h, nw, w, d)

            def look(t):
                p = jnp.pad(t, ((0, 0), (0, 0), (1, 0), (0, 0), (0, 0)))
                return jnp.concatenate([p[:, :, :nw], p[:, :, 1:]], axis=3)
            bk2, bv2 = (look(bk), look(bv))
            seq = jnp.arange(n).reshape(nw, w)
            seq_p = jnp.pad(seq, ((1, 0), (0, 0)), constant_values=-1)
            jt = jnp.concatenate([seq_p[:nw], seq_p[1:]], axis=1)
            it = seq[:, :, None]
            jb = jt[:, None, :]
            mask = (it < jb) | (it > jb + w) | (jb == -1)
            sim = jnp.einsum('bhwie,bhwje->bhwij', bq, bk2) * QK_SCALE
            sim = jnp.where(mask, -jnp.finfo(sim.dtype).max, sim)
            attn = jax.nn.softmax(sim, -1)
            out = jnp.einsum('bhwij,bhwje->bhwie', attn, bv2)
            return out.reshape(b, h, n, d)

        def attn_layer(x, Wqkv, qs, ksc, Wo):
            b, n, _ = x.shape
            qkv = x @ Wqkv
            q, k, v = jnp.split(qkv, 3, -1)
            sh = lambda t: t.reshape(b, n, HEADS, DIM_HEAD).transpose(0, 2, 1, 3)
            q, k, v = (sh(q), sh(k), sh(v))
            q = l2norm(q) * qs
            k = l2norm(k) * ksc
            freqs, scale = rotary_tables(n)
            cos, sin = (jnp.cos(freqs), jnp.sin(freqs))
            q = q * cos * scale + rotate_half(q) * sin * scale
            inv = 1.0 / scale
            k = k * cos * inv + rotate_half(k) * sin * inv
            out = local_attention(q, k, v)
            out = out.transpose(0, 2, 1, 3).reshape(b, n, INNER)
            return out @ Wo

        def ffn_layer(x, g, bln, W1, b1, W2, b2):
            mu = x.mean(-1, keepdims=True)
            var = ((x - mu) ** 2).mean(-1, keepdims=True)
            xn = (x - mu) / jnp.sqrt(var + 1e-05) * g + bln
            hg = xn @ W1 + b1
            a, gate = jnp.split(hg, 2, -1)
            return a * jax.nn.gelu(gate, approximate=False) @ W2 + b2
        key = jax.random.key(seed)
        ks = jax.random.split(key, 8)
        B, N = (2, 256)
        init = lambda k, shape: jax.random.normal(k, shape, jnp.float32) * 0.02
        return {'x': jax.random.normal(ks[0], (B, N, DIM), jnp.float32), 'Wqkv': init(ks[1], (DEPTH, DIM, 3 * INNER)), 'q_scale': jnp.ones((DEPTH, DIM_HEAD), jnp.float32), 'k_scale': jnp.ones((DEPTH, DIM_HEAD), jnp.float32), 'Wo': init(ks[2], (DEPTH, INNER, DIM)), 'ln_g': jnp.ones((DEPTH, DIM), jnp.float32), 'ln_b': jnp.zeros((DEPTH, DIM), jnp.float32), 'W1': init(ks[3], (DEPTH, DIM, 2 * DIM_INNER)), 'b1': jnp.zeros((DEPTH, 2 * DIM_INNER), jnp.float32), 'W2': init(ks[4], (DEPTH, DIM_INNER, DIM)), 'b2': jnp.zeros((DEPTH, DIM), jnp.float32)}
    _L1_ffn_in = _L1_ffn_setup()
    _d = {'L0_attn_x': _L0_attn_in['x'], 'L0_attn_Wq': _L0_attn_in['Wq'], 'L0_attn_bq': _L0_attn_in['bq'], 'L0_attn_Wk': _L0_attn_in['Wk'], 'L0_attn_bk': _L0_attn_in['bk'], 'L0_attn_Wv': _L0_attn_in['Wv'], 'L0_attn_bv': _L0_attn_in['bv'], 'L0_attn_Wo': _L0_attn_in['Wo'], 'L0_attn_bo': _L0_attn_in['bo'], 'L0_attn_Ws': _L0_attn_in['Ws'], 'L0_attn_bs': _L0_attn_in['bs'], 'L0_ffn_in_proj_w': _L0_ffn_in['in_proj_w'], 'L0_ffn_in_proj_b': _L0_ffn_in['in_proj_b'], 'L0_ffn_out_proj_w': _L0_ffn_in['out_proj_w'], 'L0_ffn_out_proj_b': _L0_ffn_in['out_proj_b'], 'L0_ffn_ln1_g': _L0_ffn_in['ln1_g'], 'L0_ffn_ln1_b': _L0_ffn_in['ln1_b'], 'L0_ffn_ln2_g': _L0_ffn_in['ln2_g'], 'L0_ffn_ln2_b': _L0_ffn_in['ln2_b'], 'L0_ffn_wg': _L0_ffn_in['wg'], 'L0_ffn_w1': _L0_ffn_in['w1'], 'L0_ffn_b1': _L0_ffn_in['b1'], 'L0_ffn_w2': _L0_ffn_in['w2'], 'L0_ffn_b2': _L0_ffn_in['b2'], 'L1_attn_w_qkv': _L1_attn_in['w_qkv'], 'L1_attn_b_qkv': _L1_attn_in['b_qkv'], 'L1_attn_w_out': _L1_attn_in['w_out'], 'L1_attn_b_out': _L1_attn_in['b_out'], 'L1_attn_w1_rpe': _L1_attn_in['w1_rpe'], 'L1_attn_b1_rpe': _L1_attn_in['b1_rpe'], 'L1_attn_w2_rpe': _L1_attn_in['w2_rpe'], 'L1_attn_b2_rpe': _L1_attn_in['b2_rpe'], 'L1_ffn_Wqkv': _L1_ffn_in['Wqkv'], 'L1_ffn_q_scale': _L1_ffn_in['q_scale'], 'L1_ffn_k_scale': _L1_ffn_in['k_scale'], 'L1_ffn_Wo': _L1_ffn_in['Wo'], 'L1_ffn_ln_g': _L1_ffn_in['ln_g'], 'L1_ffn_ln_b': _L1_ffn_in['ln_b'], 'L1_ffn_W1': _L1_ffn_in['W1'], 'L1_ffn_b1': _L1_ffn_in['b1'], 'L1_ffn_W2': _L1_ffn_in['W2'], 'L1_ffn_b2': _L1_ffn_in['b2']}
    _x0 = _d['L0_attn_x']
    _d['L0_attn_x'] = jax.random.normal(jax.random.fold_in(jax.random.key(seed), 1), (4, 1024, 128), dtype=_x0.dtype)
    del _x0
    return _d

def reference(L0_attn_x, L0_attn_Wq, L0_attn_bq, L0_attn_Wk, L0_attn_bk, L0_attn_Wv, L0_attn_bv, L0_attn_Wo, L0_attn_bo, L0_attn_Ws, L0_attn_bs, L0_ffn_in_proj_w, L0_ffn_in_proj_b, L0_ffn_out_proj_w, L0_ffn_out_proj_b, L0_ffn_ln1_g, L0_ffn_ln1_b, L0_ffn_ln2_g, L0_ffn_ln2_b, L0_ffn_wg, L0_ffn_w1, L0_ffn_b1, L0_ffn_w2, L0_ffn_b2, L1_attn_w_qkv, L1_attn_b_qkv, L1_attn_w_out, L1_attn_b_out, L1_attn_w1_rpe, L1_attn_b1_rpe, L1_attn_w2_rpe, L1_attn_b2_rpe, L1_ffn_Wqkv, L1_ffn_q_scale, L1_ffn_k_scale, L1_ffn_Wo, L1_ffn_ln_g, L1_ffn_ln_b, L1_ffn_W1, L1_ffn_b1, L1_ffn_W2, L1_ffn_b2):

    def _L0_attn_ref(x, Wq, bq, Wk, bk, Wv, bv, Wo, bo, Ws, bs):
        import jax, jax.numpy as jnp
        import numpy as np
        D_MODEL = 128
        N_HEADS = 16
        WINDOW = 128
        TOPK_RATIO = 0.25
        N_GLOBAL = 64
        B, N = (2, 256)
        Bx, Nx, C = x.shape
        H, D = (N_HEADS, C // N_HEADS)
        scale = 1.0 / jnp.sqrt(jnp.asarray(D, x.dtype))

        def heads(t):
            return t.reshape(Bx, Nx, H, D).transpose(0, 2, 1, 3)
        q = heads(x @ Wq.T + bq)
        k = heads(x @ Wk.T + bk)
        v = heads(x @ Wv.T + bv)
        attn = jnp.einsum('bhnd,bhmd->bhnm', q, k) * scale
        idx = jnp.arange(Nx)
        band = jnp.abs(idx[:, None] - idx[None, :]) <= WINDOW
        attn = jnp.where(band[None, None], attn, -jnp.inf)
        local_out = jnp.einsum('bhnm,bhmd->bhnd', jax.nn.softmax(attn, axis=-1), v)
        k_tokens = max(int(Nx * TOPK_RATIO), 1)
        scores = (x @ Ws.T + bs).transpose(0, 2, 1)
        top_idx = jax.lax.top_k(scores, k_tokens)[1]
        gather = lambda t: jnp.take_along_axis(t, top_idx[..., None], axis=2)
        k_t, v_t = (gather(k), gather(v))
        attn_t = jnp.einsum('bhnd,bhkd->bhnk', q, k_t) * scale
        topk_out = jnp.einsum('bhnk,bhkd->bhnd', jax.nn.softmax(attn_t, axis=-1), v_t)
        k_g, v_g = (k[:, :, :N_GLOBAL], v[:, :, :N_GLOBAL])
        attn_g = jnp.einsum('bhnd,bhgd->bhng', q, k_g) * scale
        global_out = jnp.einsum('bhng,bhgd->bhnd', jax.nn.softmax(attn_g, axis=-1), v_g)
        out = (local_out + topk_out + global_out) / 3.0
        out = out.transpose(0, 2, 1, 3).reshape(Bx, Nx, C)
        return out @ Wo.T + bo

    def _L0_ffn_ref(x, in_proj_w, in_proj_b, out_proj_w, out_proj_b, ln1_g, ln1_b, ln2_g, ln2_b, wg, w1, b1, w2, b2):
        import jax, jax.numpy as jnp
        import numpy as np
        D = 128
        H = 4
        HD = D // H
        E = 8
        FF = 512
        CAP_FACTOR = 1.0

        def _ln(x, g, b, eps=1e-05):
            mu = jnp.mean(x, -1, keepdims=True)
            v = jnp.mean((x - mu) ** 2, -1, keepdims=True)
            return (x - mu) * jax.lax.rsqrt(v + eps) * g + b

        def _mha(x, w, b, ow, ob):
            L, N, _ = x.shape
            qkv = x @ w.T + b
            q, k, v = jnp.split(qkv, 3, axis=-1)
            rh = lambda t: t.reshape(L, N, H, HD).transpose(1, 2, 0, 3)
            q, k, v = (rh(q), rh(k), rh(v))
            scores = jnp.einsum('nhld,nhmd->nhlm', q, k) / np.float32(np.sqrt(HD))
            attn = jax.nn.softmax(scores, axis=-1)
            o = jnp.einsum('nhlm,nhmd->nhld', attn, v).transpose(2, 0, 1, 3).reshape(L, N, D)
            return o @ ow.T + ob

        def _moe(x, wg, w1, b1, w2, b2):
            L, N, _ = x.shape
            S = L * N
            cap = int(CAP_FACTOR * S) // E
            xf = x.reshape(S, D)
            gates = jax.nn.softmax(xf @ wg, axis=-1)
            idx = jnp.argmax(gates, axis=-1)
            mask1 = jax.nn.one_hot(idx, E, dtype=x.dtype)
            loc = jnp.sum((jnp.cumsum(mask1, 0) - 1.0) * mask1, -1).astype(jnp.int32)
            keep = loc < cap
            gate_val = jnp.take_along_axis(gates, idx[:, None], -1)[:, 0]
            slot = jnp.where(keep, idx.astype(jnp.int32) * cap + loc, E * cap)
            disp = jnp.zeros((E * cap, D), x.dtype).at[slot].set(xf, mode='drop')
            disp = disp.reshape(E, cap, D)
            h = jnp.einsum('ecd,edf->ecf', disp, w1) + b1[:, None, :]
            y = (jnp.einsum('ecf,efd->ecd', h, w2) + b2[:, None, :]).reshape(E * cap, D)
            out = jnp.where(keep[:, None], gate_val[:, None] * y[jnp.minimum(slot, E * cap - 1)], 0.0)
            return out.reshape(L, N, D)
        y1 = _ln(x + _mha(x, in_proj_w, in_proj_b, out_proj_w, out_proj_b), ln1_g, ln1_b)
        y2 = _ln(y1 + _moe(y1, wg, w1, b1, w2, b2), ln2_g, ln2_b)
        return y2

    def _L1_attn_ref(x, w_qkv, b_qkv, w_out, b_out, w1_rpe, b1_rpe, w2_rpe, b2_rpe):
        import jax, jax.numpy as jnp
        import numpy as np
        D_MODEL = 128
        N_HEADS = 16
        D_HEAD = D_MODEL // N_HEADS
        RPE_HIDDEN = 32

        def _rpe_bias(T, w1, b1, w2, b2):
            pos = jnp.arange(T, dtype=jnp.float32)
            rel = pos[:, None] - pos[None, :]
            rel = jnp.sign(rel) * jnp.log1p(jnp.abs(rel))
            h = jax.nn.relu(rel[..., None] * w1[0] + b1)
            bias = h @ w2 + b2
            return jnp.transpose(bias, (2, 0, 1))
        B, T, C = x.shape
        qkv = x @ w_qkv + b_qkv
        q, k, v = jnp.split(qkv, 3, axis=-1)

        def heads(t):
            return jnp.transpose(t.reshape(B, T, N_HEADS, D_HEAD), (0, 2, 1, 3))
        q, k, v = (heads(q), heads(k), heads(v))
        scores = jnp.einsum('bhtd,bhsd->bhts', q, k) / np.sqrt(D_HEAD)
        scores = scores + _rpe_bias(T, w1_rpe, b1_rpe, w2_rpe, b2_rpe)[None]
        attn = jax.nn.softmax(scores, axis=-1)
        out = jnp.einsum('bhts,bhsd->bhtd', attn, v)
        out = jnp.transpose(out, (0, 2, 1, 3)).reshape(B, T, C)
        return out @ w_out + b_out

    def _L1_ffn_ref(x, Wqkv, q_scale, k_scale, Wo, ln_g, ln_b, W1, b1, W2, b2):
        import jax, jax.numpy as jnp
        import numpy as np
        DIM = 128
        DEPTH = 6
        HEADS = 16
        DIM_HEAD = 64
        WINDOW = 32
        INNER = HEADS * DIM_HEAD
        DIM_INNER = int(DIM * 4 * 2 / 3)
        QK_SCALE = 8.0

        def shift_tokens(t):
            a, s = jnp.split(t, 2, -1)
            s = jnp.pad(s, ((0, 0), (1, 0), (0, 0)))[:, :-1]
            return jnp.concatenate([a, s], -1)

        def l2norm(t):
            return t / jnp.maximum(jnp.linalg.norm(t, axis=-1, keepdims=True), 1e-12)

        def rotate_half(x):
            x1, x2 = jnp.split(x, 2, -1)
            return jnp.concatenate([-x2, x1], -1)

        def rotary_tables(n):
            half = jnp.arange(0, DIM_HEAD, 2, dtype=jnp.float32)
            inv_freq = 1.0 / 10000.0 ** (half / DIM_HEAD)
            t = jnp.arange(n, dtype=jnp.float32)
            freqs = t[:, None] * inv_freq[None, :]
            freqs = jnp.concatenate([freqs, freqs], -1)
            base_scale = (half + 0.4 * DIM_HEAD) / (1.4 * DIM_HEAD)
            power = (t - n // 2) / (WINDOW // 2)
            scale = base_scale[None, :] ** power[:, None]
            scale = jnp.concatenate([scale, scale], -1)
            return (freqs, scale)

        def local_attention(q, k, v):
            b, h, n, d = q.shape
            w = WINDOW
            nw = n // w
            bq = q.reshape(b, h, nw, w, d)
            bk = k.reshape(b, h, nw, w, d)
            bv = v.reshape(b, h, nw, w, d)

            def look(t):
                p = jnp.pad(t, ((0, 0), (0, 0), (1, 0), (0, 0), (0, 0)))
                return jnp.concatenate([p[:, :, :nw], p[:, :, 1:]], axis=3)
            bk2, bv2 = (look(bk), look(bv))
            seq = jnp.arange(n).reshape(nw, w)
            seq_p = jnp.pad(seq, ((1, 0), (0, 0)), constant_values=-1)
            jt = jnp.concatenate([seq_p[:nw], seq_p[1:]], axis=1)
            it = seq[:, :, None]
            jb = jt[:, None, :]
            mask = (it < jb) | (it > jb + w) | (jb == -1)
            sim = jnp.einsum('bhwie,bhwje->bhwij', bq, bk2) * QK_SCALE
            sim = jnp.where(mask, -jnp.finfo(sim.dtype).max, sim)
            attn = jax.nn.softmax(sim, -1)
            out = jnp.einsum('bhwij,bhwje->bhwie', attn, bv2)
            return out.reshape(b, h, n, d)

        def attn_layer(x, Wqkv, qs, ksc, Wo):
            b, n, _ = x.shape
            qkv = x @ Wqkv
            q, k, v = jnp.split(qkv, 3, -1)
            sh = lambda t: t.reshape(b, n, HEADS, DIM_HEAD).transpose(0, 2, 1, 3)
            q, k, v = (sh(q), sh(k), sh(v))
            q = l2norm(q) * qs
            k = l2norm(k) * ksc
            freqs, scale = rotary_tables(n)
            cos, sin = (jnp.cos(freqs), jnp.sin(freqs))
            q = q * cos * scale + rotate_half(q) * sin * scale
            inv = 1.0 / scale
            k = k * cos * inv + rotate_half(k) * sin * inv
            out = local_attention(q, k, v)
            out = out.transpose(0, 2, 1, 3).reshape(b, n, INNER)
            return out @ Wo

        def ffn_layer(x, g, bln, W1, b1, W2, b2):
            mu = x.mean(-1, keepdims=True)
            var = ((x - mu) ** 2).mean(-1, keepdims=True)
            xn = (x - mu) / jnp.sqrt(var + 1e-05) * g + bln
            hg = xn @ W1 + b1
            a, gate = jnp.split(hg, 2, -1)
            return a * jax.nn.gelu(gate, approximate=False) @ W2 + b2
        for i in range(DEPTH):
            x = attn_layer(shift_tokens(x), Wqkv[i], q_scale[i], k_scale[i], Wo[i]) + x
            x = ffn_layer(shift_tokens(x), ln_g[i], ln_b[i], W1[i], b1[i], W2[i], b2[i]) + x
        return x
    x = L0_attn_x
    xn = _layernorm(x, axis=-1)
    x = x + _L0_attn_ref(xn, L0_attn_Wq, L0_attn_bq, L0_attn_Wk, L0_attn_bk, L0_attn_Wv, L0_attn_bv, L0_attn_Wo, L0_attn_bo, L0_attn_Ws, L0_attn_bs) + _L0_ffn_ref(xn, L0_ffn_in_proj_w, L0_ffn_in_proj_b, L0_ffn_out_proj_w, L0_ffn_out_proj_b, L0_ffn_ln1_g, L0_ffn_ln1_b, L0_ffn_ln2_g, L0_ffn_ln2_b, L0_ffn_wg, L0_ffn_w1, L0_ffn_b1, L0_ffn_w2, L0_ffn_b2)
    xn = _layernorm(x, axis=-1)
    x = x + _L1_attn_ref(xn, L1_attn_w_qkv, L1_attn_b_qkv, L1_attn_w_out, L1_attn_b_out, L1_attn_w1_rpe, L1_attn_b1_rpe, L1_attn_w2_rpe, L1_attn_b2_rpe) + _L1_ffn_ref(xn, L1_ffn_Wqkv, L1_ffn_q_scale, L1_ffn_k_scale, L1_ffn_Wo, L1_ffn_ln_g, L1_ffn_ln_b, L1_ffn_W1, L1_ffn_b1, L1_ffn_W2, L1_ffn_b2)
    return x

_drawn_inputs = setup_inputs


def setup_inputs(seed=0):
    import zlib

    import numpy as np

    out = dict(_drawn_inputs(seed))
    spreads = {'L0_attn_bq': (0.0, 0.8),
     'L0_attn_bk': (0.0, 2.0),
     'L0_attn_bv': (0.0, 0.752),
     'L0_attn_bo': (0.0, 0.1),
     'L0_attn_bs': (0.0, 0.1),
     'L0_ffn_in_proj_b': (0.0, 0.599),
     'L0_ffn_out_proj_b': (0.0, 0.1),
     'L0_ffn_ln1_g': (1.0, 0.2),
     'L0_ffn_ln1_b': (0.0, 0.1),
     'L0_ffn_ln2_g': (1.0, 0.2),
     'L0_ffn_ln2_b': (0.0, 0.1),
     'L0_ffn_b1': (0.0, 0.8),
     'L0_ffn_b2': (0.0, 0.8),
     'L1_attn_b_qkv': (0.0, 1.22),
     'L1_attn_b_out': (0.0, 0.8),
     'L1_attn_b2_rpe': (0.0, 2.0),
     'L1_ffn_q_scale': (1.0, 0.6),
     'L1_ffn_k_scale': (1.0, 0.6),
     'L1_ffn_ln_g': (1.0, 0.6),
     'L1_ffn_ln_b': (0.0, 0.8),
     'L1_ffn_b1': (0.0, 0.8),
     'L1_ffn_b2': (0.0, 0.1)}
    factors = {'L0_attn_Wq': 8.0,
     'L0_attn_Wk': 8.0,
     'L0_attn_Wv': 8.0,
     'L0_attn_Wo': 5.159,
     'L0_attn_Ws': 8.0,
     'L0_ffn_in_proj_w': 4.335,
     'L0_ffn_out_proj_w': 3.243,
     'L0_ffn_wg': 5.025,
     'L0_ffn_w1': 6.494,
     'L0_ffn_w2': 5.968,
     'L1_attn_w_qkv': 4.823,
     'L1_attn_w1_rpe': 8.0,
     'L1_attn_b1_rpe': 39.72,
     'L1_attn_w2_rpe': 8.0,
     'L1_ffn_W1': 5.433,
     'L1_ffn_W2': 5.327}
    for name, (base, spread) in spreads.items():
        noise = np.random.default_rng([zlib.crc32(name.encode()), seed]).standard_normal(out[name].shape)
        drawn = base * np.exp(spread * noise) if base else spread * noise
        out[name] = jnp.asarray(drawn.astype(out[name].dtype))
    for name, factor in factors.items():
        out[name] = (out[name] * factor).astype(out[name].dtype)
    return out
```

```python
from contextlib import ExitStack

import numpy as np

import concourse.bass as bass
from concourse import mybir

F32 = mybir.dt.float32
BF16 = mybir.dt.bfloat16
ACT = mybir.ActivationFunctionType
ALU = mybir.AluOpType
AX = mybir.AxisListType

P = 128
B, N, D = 4, 1024, 128
NT = B * N // P
TB = N // P
NEG = -1.0e30
EPS = 1e-5

DEPTH, WH, WD, WIN = 6, 16, 64, 32
INNER = WH * WD
GH = 4
NG = WH // GH
GW = GH * WD
KW = P + WIN
FI = int(D * 4 * 2 / 3)
FC = [(c, min(P, FI - c)) for c in range(0, FI, P)]


class Memory:

    def __init__(self, nc, ctx, prefix):
        self.nc, self.ctx, self.prefix, self.sems = nc, ctx, prefix, []
        ctx.callback(self.close)

    def sb(self, name, shape, dt=F32):
        return self.ctx.enter_context(self.nc.sbuf_tensor(self.prefix + name, shape, dt))

    def ps(self, name, shape, dt=F32):
        return self.ctx.enter_context(self.nc.psum_tensor(self.prefix + name, shape, dt))

    def sem(self, name):
        self.sems.append(self.nc.alloc_semaphore(self.prefix + name))
        return self.sems[-1]

    def close(self):
        self.nc.clear_and_free_semaphores(self.sems)
        self.nc.all_engine_barrier()


def wait_apart(eng, sem, value, passed):
    eng.wait_ge(sem, value)
    eng.sem_inc(passed, 1)


def tokens(ap):
    return ap.rearrange("b (t p) f -> p (b t) f", p=P)


def load_and_normalize(nc, x_dram, ident_dram, X, XN, ident):
    with ExitStack() as ctx:
        m = Memory(nc, ctx, "ln_")
        loaded, normed = m.sem("loaded"), m.sem("normed")
        block = ctx.enter_context(nc.Block())

        @block.sync
        def _(sp):
            sp.dma_start(X[:], tokens(x_dram)).then_inc(loaded, 16)
            sp.dma_start(ident[:], ident_dram).then_inc(loaded, 16)
            sp.wait_ge(loaded, 32)

    layer_norm(nc, X, XN, "ln0_")


def layer_norm(nc, X, XN, prefix):
    with ExitStack() as ctx:
        m = Memory(nc, ctx, prefix)
        stats, mv1, mv = m.sb("stats", [P, 6]), m.sb("mv1", [P, 2]), m.sb("mv", [P, NT, 2])
        rstd, var, half = m.sb("rstd", [P, NT]), m.sb("var", [P, NT]), m.sb("half", [P, NT])
        s_passed, s_stats, s_mv1, s_mv, s_const, s_var, s_rstd = (m.sem(n) for n in ("passed", "stats", "mv1", "mv", "const", "var", "rstd"))
        block = ctx.enter_context(nc.Block())

        @block.vector
        def _(dve):
            with dve.Fori(0, NT) as t:
                dve.bn_stats(stats[:], X[:, bass.ds(t, 1), :].rearrange("p a f -> p (a f)")).then_inc(s_stats, 1)
                wait_apart(dve, s_stats, t + 1, s_passed)
                dve.bn_aggr(mv1[:], stats[:]).then_inc(s_mv1, 1)
                dve.wait_ge(s_mv1, t + 1)
                dve.tensor_copy(mv[:, bass.ds(t, 1), :].rearrange("p a s -> p (a s)"), mv1[:]).then_inc(s_mv, 1)
            dve.wait_ge(s_rstd, 1)
            dve.wait_ge(s_mv, NT)
            with dve.Fori(0, NT) as t:
                dve.tensor_scalar(XN[:, bass.ds(t, 1), :].rearrange("p a f -> p (a f)"),
                                  X[:, bass.ds(t, 1), :].rearrange("p a f -> p (a f)"),
                                  mv[:, bass.ds(t, 1), 0:1].rearrange("p a s -> p (a s)"),
                                  rstd[:, bass.ds(t, 1)], ALU.subtract, ALU.mult)

        @block.gpsimd
        def _(pool):
            pool.memset(half[:], -0.5).then_inc(s_const, 1)
            pool.wait_ge(s_mv, NT)
            pool.tensor_scalar(var[:], mv[:, :, 1], EPS, None, ALU.add).then_inc(s_var, 1)
            pool.wait_ge(s_var, 1)
            pool.wait_ge(s_const, 1)
            pool.tensor_tensor(rstd[:], var[:], half[:], ALU.pow).then_inc(s_rstd, 1)


def add_into(nc, X, Y):
    with ExitStack() as ctx:
        block = ctx.enter_context(nc.Block())

        @block.vector
        def _(dve):
            dve.tensor_tensor(X[:], X[:], Y[:], ALU.add)


def windowed_layers(nc, XF, ident, w):
    with ExitStack() as ctx:
        m = Memory(nc, ctx, "w_")
        wqkv = m.sb("wqkv", [P, NG, 3 * GW])
        wo = m.sb("wo", [P, INNER // P, D])
        w1 = m.sb("w1", [P, 2 * FI])
        w2 = m.sb("w2", [P, len(FC), D])
        b1 = m.sb("b1", [P, 2, len(FC)])
        b2 = m.sb("b2", [1, D])
        lng, lnb = m.sb("lng", [P, 1]), m.sb("lnb", [P, 1])
        scales = m.sb("scales", [P, 2, 2, WD])
        rot0 = m.sb("rot0", [P, TB, 2, 2, WD])
        rot = m.sb("rot", [P, TB, 2, 2, WD])
        masks = m.sb("masks", [P, TB, 2, KW], BF16)
        identb = m.sb("identb", [P, P], BF16)
        flag = m.sb("flag", [P, TB])
        ones = m.sb("ones", [1, P])
        half = m.sb("half", [P, 2 * GH])
        xcur = m.sb("xcur", [P, D])
        xsT = m.sb("xsT", [P, P])
        carryA, carryF = m.sb("carryA", [P, 1]), m.sb("carryF", [P, 1])
        sq = m.sb("sq", [P, 2, GH, WD])
        ss = m.sb("ss", [P, 2 * GH])
        ssm = m.sb("ssm", [P, 2 * GH])
        rn = m.sb("rn", [P, 2, 2 * GH])
        tc = m.sb("tc", [P, 2, GH, WD])
        tsn = m.sb("tsn", [P, 2, GH, WD])
        tadd = m.sb("tadd", [P, 2, GH, WD])
        qk = m.sb("qk", [P, 2, 2 * GH * WD])
        vcur = m.sb("vcur", [P, INNER])
        vprev = m.sb("vprev", [P, INNER])
        qT = m.sb("qT", [P, 2, P])
        kT = m.sb("kT", [P, NG, 2, KW])
        nmax = m.sb("nmax", [P, 2, GH])
        zsum = m.sb("zsum", [P, 2, GH])
        rz = m.sb("rz", [P, GH])
        pr = m.sb("pr", [P, 2, GH, KW])
        prT = m.sb("prT", [P, GH, P])
        prH = m.sb("prH", [P, GH, WIN])
        o = m.sb("o", [P, GW])
        oT = m.sb("oT", [P, INNER // P, P])
        x1 = m.sb("x1", [P, D])
        fsT = m.sb("fsT", [P, P])
        st6, mv = m.sb("st6", [P, 6]), m.sb("mv", [P, 2])
        vr, rstd = m.sb("vr", [P, 1]), m.sb("rstd", [P, 1])
        fn, fnT = m.sb("fn", [P, D]), m.sb("fnT", [P, P])
        gl, hT = m.sb("gl", [P, len(FC), P]), m.sb("hT", [P, len(FC), P])

        psQK = m.ps("psQK", [P, 512])
        psVb = m.ps("psV", [P, 512])
        psOb = m.ps("psO", [P, 512])
        psT = m.ps("psT", [P, 512])
        psS = m.ps("psS", [P, 2, 512])
        psP = m.ps("psP", [P, 512])
        psX = m.ps("psX", [P, 512])
        psV, psO = psVb[:, 0:GW], psOb[:, 0:GW]
        psHalo, psOT = psT[0:WIN, 0:GH * WIN], psP[:, 0:GW]

        names = """const weights layer_done tables x_full xT xsT_hi xsT_full carryA
            qk_full v_full squares norms qk_free rot_c rot_s sums rinv_a rinv qk_added qk_rot v_sb
            qkT qkT_sb scores maxes probs prT_ps prT_sb prH_sb pv rz o_sb oT_ps oT_sb vprev kprev
            y x1_full f_xT fsT_hi fsT_full carryF f_tok f_stats f_mv f_var f_rstd fn fnT_ps fnT_sb
            gates gelu hidden y2 x2_full passed_pe passed_dve passed_pool""".split()
        s = {n: m.sem(n) for n in names}
        block = ctx.enter_context(nc.Block())

        NW = 20

        @block.sync
        def _(sp):
            sp.dma_start(rot0[:], w["rot"]).then_inc(s["const"], 16)
            sp.dma_start(masks[:], w["wmask"]).then_inc(s["const"], 16)
            sp.dma_start(identb[:], w["identb"]).then_inc(s["const"], 16)
            sp.dma_start(flag[:], w["flag"]).then_inc(s["const"], 16)
            with sp.Fori(0, DEPTH) as l:
                sp.wait_ge(s["layer_done"], l + 1)
                one = lambda name: w[name][bass.ds(l, 1)]
                sp.dma_start(wqkv[:], one("Wqkv").rearrange("a p g c -> p (a g) c")).then_inc(s["weights"], 16)
                sp.dma_start(wo[:], one("Wo").rearrange("a (c p) d -> p (a c) d", p=P)).then_inc(s["weights"], 16)
                sp.dma_start(w1[:], one("W1").rearrange("a p f -> p (a f)")).then_inc(s["weights"], 16)
                for c, (f0, fn_) in enumerate(FC):
                    sp.dma_start(w2[0:fn_, c, :], one("W2")[:, f0:f0 + fn_, :].rearrange("a p d -> p (a d)"))\
                        .then_inc(s["weights"], 16)
                    sp.dma_start(b1[0:fn_, :, c], one("b1").rearrange("a (j f) -> f (a j)", j=2)[f0:f0 + fn_],
                                 allow_slow_non_contiguous=True).then_inc(s["weights"], 16)
                sp.dma_start(b2[:], one("b2")).then_inc(s["weights"], 16)
                sp.dma_start(lng[:], one("ln_g").rearrange("a p -> p a"), allow_slow_non_contiguous=True)\
                    .then_inc(s["weights"], 16)
                sp.dma_start(lnb[:], one("ln_b").rearrange("a p -> p a"), allow_slow_non_contiguous=True)\
                    .then_inc(s["weights"], 16)
                for j, name in enumerate(("q_scale", "k_scale")):
                    for k in range(2):
                        for hh in range(2):
                            src = (hh + k) % 2
                            sp.dma_start(scales[:, j, k, hh * 32:hh * 32 + 32],
                                         one(name)[:, src * 32:src * 32 + 32].broadcast_to([P, 32]))\
                                .then_inc(s["weights"], 16)

        @block.tensor
        def _(pe):
            pe.sem_inc(s["scores"], 1)
            pe.sem_inc(s["prT_ps"], 2)
            pe.sem_inc(s["pv"], 1)
            pe.sem_inc(s["oT_ps"], 1)
            pe.wait_ge(s["const"], 64)
            with pe.Fori(0, DEPTH) as l:
                wait_apart(pe, s["weights"], (l + 1) * (NW * 16), s["passed_pe"])
                with pe.Fori(0, B) as b:
                    with pe.Fori(0, TB) as i:
                        t = l * NT + b * TB + i
                        pe.wait_ge(s["x_full"], t + 1)
                        pe.transpose(psX[:, 0:P], xcur[:], ident[:]).then_inc(s["xT"], 1)
                        pe.wait_ge(s["xsT_hi"], t + 1)
                        pe.wait_ge(s["carryA"], t + 2)

                        def project(u):
                            pe.wait_ge(s["qk_free"], t * (2 * NG) + 2 * u + 2)
                            pe.wait_ge(s["squares"], t * NG + u + 1)
                            pe.matmul(psQK[:], xsT[:], wqkv[:, u, 0:2 * GW], start=True, stop=True)\
                                .then_inc(s["qk_full"], 1)
                            pe.wait_ge(s["v_sb"], t * NG + u + 1)
                            pe.matmul(psV, xsT[:], wqkv[:, u, 2 * GW:3 * GW], start=True, stop=True)\
                                .then_inc(s["v_full"], 1)

                        def score(u):
                            pe.wait_ge(s["qk_rot"], t * NG + u + 1)
                            pe.wait_ge(s["qkT_sb"], t * NG + u + 1)
                            for j in range(4):
                                mm = pe.transpose(psT[:, j * P:(j + 1) * P], qk[:, u % 2, j * P:(j + 1) * P], ident[:])
                            mm.then_inc(s["qkT"], 1)
                            pe.wait_ge(s["qkT_sb"], t * NG + u + 2)
                            pe.wait_ge(s["probs"], t * NG + u + 1)
                            pe.wait_ge(s["kprev"], t + 1)
                            for c in range(2):
                                pe.matmul(psS[:, c, 0:2 * KW], identb[:],
                                          masks[:, bass.ds(i, 1), :, :].rearrange("p a h k -> p (a h k)"),
                                          start=True, stop=False, skip_group_check=True)
                            for a in range(2):
                                for c in range(2):
                                    r = slice(c * WD, (c + 1) * WD)
                                    mm = pe.matmul(psS[:, c, a * KW:(a + 1) * KW], qT[r, a, :], kT[r, u, a, :],
                                                   start=False, stop=(a == 1), skip_group_check=True)
                            mm.then_inc(s["scores"], 1)

                        def weigh(u):
                            pe.wait_ge(s["probs"], t * NG + u + 2)
                            pe.wait_ge(s["prT_sb"], t * NG + u + 1)
                            pe.wait_ge(s["prH_sb"], t * NG + u + 1)
                            pe.wait_ge(s["oT_sb"], t * NG + u + 1)
                            for h in range(GH):
                                pe.transpose(psP[:, h * P:(h + 1) * P], pr[:, u % 2, h, 0:P], ident[:])
                            for h in range(GH):
                                mm = pe.transpose(psHalo[:, h * WIN:(h + 1) * WIN], pr[0:WIN, u % 2, h, P:KW],
                                                  ident[0:WIN, 0:WIN])
                            mm.then_inc(s["prT_ps"], 1)
                            pe.wait_ge(s["prT_sb"], t * NG + u + 2)
                            pe.wait_ge(s["prH_sb"], t * NG + u + 2)
                            pe.wait_ge(s["o_sb"], t * NG + u + 1)
                            pe.wait_ge(s["vprev"], t + 1)
                            pe.wait_ge(s["v_sb"], t * NG + u + 2)
                            for h in range(GH):
                                c = u * GW + h * WD
                                pe.matmul(psO[:, h * WD:(h + 1) * WD], prT[:, h, :], vcur[:, c:c + WD],
                                          start=True, stop=False, skip_group_check=True)
                                mm = pe.matmul(psO[0:WIN, h * WD:(h + 1) * WD], prH[P - WIN:P, h, :],
                                               vprev[P - WIN:P, c:c + WD], start=False, stop=True,
                                               skip_group_check=True)
                            mm.then_inc(s["pv"], 1)

                        def turn(u):
                            pe.wait_ge(s["o_sb"], t * NG + u + 2)
                            for a in range(2):
                                mm = pe.transpose(psOT[:, a * P:(a + 1) * P], o[:, a * P:(a + 1) * P], ident[:])
                            mm.then_inc(s["oT_ps"], 1)

                        for k in range(NG + 2):
                            if k < NG:
                                project(k)
                            if 1 <= k <= NG:
                                score(k - 1)
                            if k >= 2:
                                weigh(k - 2)
                                turn(k - 2)
                        pe.wait_ge(s["oT_sb"], t * NG + NG + 1)
                        for c in range(INNER // P):
                            mm = pe.matmul(psX[:, P:2 * P], oT[:, c, :], wo[:, c, :], start=(c == 0),
                                           stop=(c == INNER // P - 1))
                        mm.then_inc(s["y"], 1)
                        pe.wait_ge(s["x1_full"], t + 1)
                        pe.transpose(psX[:, 0:P], x1[:], ident[:]).then_inc(s["f_xT"], 1)
                        pe.wait_ge(s["fsT_hi"], t + 1)
                        pe.wait_ge(s["carryF"], t + 2)
                        pe.transpose(psX[:, P:2 * P], fsT[:], ident[:]).then_inc(s["f_tok"], 1)
                        pe.wait_ge(s["fn"], t + 1)
                        pe.transpose(psX[:, 0:P], fn[:], ident[:]).then_inc(s["fnT_ps"], 1)
                        pe.wait_ge(s["fnT_sb"], t + 1)
                        for j, bank in ((1, psT), (0, psP)):
                            for c, (f0, fw) in enumerate(FC):
                                mm = pe.matmul(bank[0:fw, c * P:(c + 1) * P], w1[:, j * FI + f0:j * FI + f0 + fw],
                                               fnT[:], start=True, stop=True)
                            mm.then_inc(s["gates"], 1)
                        pe.wait_ge(s["hidden"], t + 1)
                        for c, (f0, fw) in enumerate(FC):
                            pe.matmul(psX[:, P:2 * P], hT[0:fw, c, :], w2[0:fw, c, :], start=(c == 0), stop=False)
                        pe.matmul(psX[:, P:2 * P], ones[:], b2[:], start=False, stop=True).then_inc(s["y2"], 1)

        def shifted(act, dst, src, hi):
            act.activation(dst[0:64, :], src[0:64, 0:P], ACT.Copy)
            act.activation(dst[64:P, 1:P], src[64:P, 0:P - 1], ACT.Copy).then_inc(hi, 1)

        @block.scalar
        def _(act):
            act.sem_inc(s["squares"], 1)
            act.sem_inc(s["v_sb"], 1)
            act.sem_inc(s["qkT_sb"], 1)
            act.sem_inc(s["probs"], 1)
            act.sem_inc(s["prT_sb"], 1)
            act.sem_inc(s["oT_sb"], 1)
            with act.Fori(0, DEPTH) as l:
                act.wait_ge(s["weights"], (l + 1) * (NW * 16))
                with act.Fori(0, B) as b:
                    with act.Fori(0, TB) as i:
                        t = l * NT + b * TB + i
                        act.wait_ge(s["xT"], t + 1)
                        shifted(act, xsT, psX, s["xsT_hi"])

                        def evacuate_qkv(u):
                            act.wait_ge(s["qk_full"], t * NG + u + 1)
                            act.wait_ge(s["norms"], t * NG + u + 1)
                            act.activation(sq[:].rearrange("p j h d -> p (j h d)"), psQK[:], ACT.Square)\
                                .then_inc(s["squares"], 1)
                            act.wait_ge(s["v_full"], t * NG + u + 1)
                            act.wait_ge(s["vprev"], t + 1)
                            act.activation(vcur[:, u * GW:(u + 1) * GW], psV, ACT.Copy).then_inc(s["v_sb"], 1)

                        def evacuate_T(u):
                            act.wait_ge(s["qkT"], t * NG + u + 1)
                            act.wait_ge(s["kprev"], t + 1)
                            act.wait_ge(s["scores"], t * NG + u + 1)
                            act.activation(qT[:].rearrange("p a c -> p (a c)"), psT[:, 0:2 * P], ACT.Copy)
                            act.activation(kT[:, u, :, 0:P], psT[:, 2 * P:4 * P].rearrange("p (a c) -> p a c", a=2),
                                           ACT.Copy).then_inc(s["qkT_sb"], 1)

                        def exponentials(u):
                            act.wait_ge(s["maxes"], t * NG + u + 1)
                            act.wait_ge(s["prT_ps"], t * NG + u + 1)
                            act.wait_ge(s["rz"], t * NG + u + 1)
                            for h in range(GH):
                                e = act.activation(pr[:, u % 2, h, :], psS[:, h % 2, (h // 2) * KW:(h // 2 + 1) * KW],
                                                   ACT.Exp, bias=nmax[:, u % 2, h:h + 1],
                                                   accum_out=zsum[:, u % 2, h:h + 1])
                            e.then_inc(s["probs"], 1)

                        def evacuate_P(u):
                            act.wait_ge(s["prT_ps"], t * NG + u + 3)
                            act.wait_ge(s["pv"], t * NG + u + 1)
                            act.activation(prT[:].rearrange("p h c -> p (h c)"), psP[:], ACT.Copy)\
                                .then_inc(s["prT_sb"], 1)

                        def evacuate_oT(u):
                            act.wait_ge(s["oT_ps"], t * NG + u + 2)
                            act.activation(oT[:, 2 * u:2 * u + 2, :].rearrange("p a c -> p (a c)"), psOT, ACT.Copy)\
                                .then_inc(s["oT_sb"], 1)

                        for k in range(NG + 2):
                            if k < NG:
                                evacuate_qkv(k)
                            if 1 <= k <= NG:
                                evacuate_T(k - 1)
                            if k >= 2:
                                evacuate_P(k - 2)
                            if 1 <= k <= NG:
                                exponentials(k - 1)
                            if k >= 2:
                                evacuate_oT(k - 2)
                        act.wait_ge(s["f_xT"], t + 1)
                        shifted(act, fsT, psX, s["fsT_hi"])
                        act.wait_ge(s["gates"], 2 * t + 1)
                        for c, (f0, fw) in enumerate(FC):
                            g = act.activation(gl[0:fw, c, :], psT[0:fw, c * P:(c + 1) * P], ACT.Gelu,
                                               bias=b1[0:fw, 1, c:c + 1])
                        g.then_inc(s["gelu"], 1)

        def carry_over(dve, dst, carry, psum, i, mine, chain, n):
            dve.tensor_copy(dst[64:P, 0:1], carry[64:P, :]).then_inc(mine, 1)
            dve.wait_ge(mine, n)
            dve.tensor_tensor(carry[64:P, :], psum[64:P, P - 1:P], flag[64:P, bass.ds(i, 1)], ALU.mult)\
                .then_inc(chain, 1)

        @block.vector
        def _(dve):
            dve.memset(carryA[:], 0.0).then_inc(s["carryA"], 1)
            dve.memset(carryF[:], 0.0).then_inc(s["carryF"], 1)
            dve.memset(ones[:], 1.0)
            dve.memset(half[:], -0.5)
            dve.sem_inc(s["norms"], 1)
            dve.sem_inc(s["qk_free"], 2)
            dve.sem_inc(s["prH_sb"], 1)
            dve.sem_inc(s["o_sb"], 1)
            dve.sem_inc(s["rz"], 2)
            dve.wait_ge(s["const"], 64)
            with dve.Fori(0, DEPTH) as l:
                dve.wait_ge(s["weights"], (l + 1) * (NW * 16))
                for j in range(2):
                    for k in range(2):
                        dve.tensor_tensor(rot[:, :, j, k, :], rot0[:, :, j, k, :],
                                          scales[:, j, k:k + 1, :].broadcast_to([P, TB, WD]), ALU.mult)\
                            .then_inc(s["tables"], 1)
                wait_apart(dve, s["tables"], 4 * l + 4, s["passed_dve"])
                with dve.Fori(0, B) as b:
                    with dve.Fori(0, TB) as i:
                        t = l * NT + b * TB + i
                        dve.wait_ge(s["xsT_hi"], t + 1)
                        dve.wait_ge(s["carryA"], t + 1)
                        carry_over(dve, xsT, carryA, psX, i, s["xsT_full"], s["carryA"], t + 1)
                        table = lambda k: rot[:, bass.ds(i, 1), :, k, :].rearrange("p a j d -> p (a j) d")

                        def rotate(u):
                            qkv = psQK[:].rearrange("p (j h d) -> p j h d", j=2, h=GH)
                            dve.wait_ge(s["squares"], t * NG + u + 2)
                            dve.wait_ge(s["qk_added"], t * NG + u + 1)
                            for j in range(2):
                                dve.tensor_tensor(
                                    tc[:, j], qkv[:, j],
                                    rot[:, bass.ds(i, 1), j, 0, :].broadcast_to([P, GH, WD]), ALU.mult)
                                for hh in range(2):
                                    a = slice(hh * 32, hh * 32 + 32)
                                    z = slice(32 - hh * 32, 64 - hh * 32)
                                    r = dve.tensor_tensor(
                                        tsn[:, j, :, a], qkv[:, j, :, z],
                                        rot[:, bass.ds(i, 1), j, 1, a].broadcast_to([P, GH, 32]), ALU.mult)
                                r.then_inc(s["qk_free"], 1)
                            dve.wait_ge(s["rinv_a"], t * NG + u + 1)
                            dve.tensor_reduce(ss[:], sq[:].rearrange("p j h d -> p (j h) d"), AX.X, ALU.add)\
                                .then_inc(s["norms"], 1)

                        def maxima(u):
                            dve.wait_ge(s["scores"], t * NG + u + 2)
                            dve.wait_ge(s["probs"], t * NG + u + 1)
                            dve.tensor_reduce(nmax[:, u % 2, :].rearrange("p (a c) -> p c a", a=2),
                                              psS[:, :, 0:2 * KW].rearrange("p c (a k) -> p c a k", a=2),
                                              AX.X, ALU.max, negate=True).then_inc(s["maxes"], 1)

                        def halo(u):
                            dve.wait_ge(s["prT_ps"], t * NG + u + 3)
                            dve.wait_ge(s["pv"], t * NG + u + 1)
                            dve.tensor_copy(prH[P - WIN:P].rearrange("p h c -> p (h c)"), psHalo)\
                                .then_inc(s["prH_sb"], 1)

                        def normalize(u):
                            dve.wait_ge(s["probs"], t * NG + u + 2)
                            dve.reciprocal(rz[:], zsum[:, u % 2, :]).then_inc(s["rz"], 1)
                            dve.wait_ge(s["rz"], t * NG + u + 3)
                            dve.wait_ge(s["pv"], t * NG + u + 2)
                            dve.wait_ge(s["oT_ps"], t * NG + u + 1)
                            dve.tensor_tensor(o[:].rearrange("p (h d) -> p h d", h=GH),
                                              psO.rearrange("p (h d) -> p h d", h=GH),
                                              rz[:].rearrange("p (h a) -> p h a", a=1).broadcast_to([P, GH, WD]), ALU.mult).then_inc(s["o_sb"], 1)

                        for k in range(NG + 2):
                            if k < NG:
                                rotate(k)
                            if k >= 2:
                                halo(k - 2)
                            if 1 <= k <= NG:
                                maxima(k - 1)
                            if k >= 2:
                                normalize(k - 2)
                        dve.wait_ge(s["y"], t + 1)
                        dve.tensor_tensor(x1[:], psX[:, P:2 * P], xcur[:], ALU.add).then_inc(s["x1_full"], 1)
                        dve.wait_ge(s["fsT_hi"], t + 1)
                        dve.wait_ge(s["carryF"], t + 1)
                        carry_over(dve, fsT, carryF, psX, i, s["fsT_full"], s["carryF"], t + 1)
                        dve.wait_ge(s["f_tok"], t + 1)
                        dve.bn_stats(st6[:], psX[:, P:2 * P]).then_inc(s["f_stats"], 1)
                        wait_apart(dve, s["f_stats"], t + 1, s["passed_dve"])
                        dve.bn_aggr(mv[:], st6[:]).then_inc(s["f_mv"], 1)
                        dve.wait_ge(s["f_mv"], t + 1)
                        dve.wait_ge(s["f_rstd"], t + 1)
                        dve.tensor_scalar(fn[:], psX[:, P:2 * P], mv[:, 0:1], rstd[:], ALU.subtract, ALU.mult)\
                            .then_inc(s["fn"], 1)
                        dve.wait_ge(s["fnT_ps"], t + 1)
                        dve.tensor_scalar(fnT[:], psX[:, 0:P], lng[:], lnb[:], ALU.mult, ALU.add)\
                            .then_inc(s["fnT_sb"], 1)
                        dve.wait_ge(s["gates"], 2 * t + 2)
                        dve.wait_ge(s["gelu"], t + 1)
                        for c, (f0, fw) in enumerate(FC):
                            h = dve.scalar_tensor_tensor(hT[0:fw, c, :], psP[0:fw, c * P:(c + 1) * P],
                                                         b1[0:fw, 0, c:c + 1], gl[0:fw, c, :], ALU.add, ALU.mult)
                        h.then_inc(s["hidden"], 1)
                        dve.wait_ge(s["y2"], t + 1)
                        dve.tensor_tensor(XF[:, bass.ds(b * TB + i, 1), :].rearrange("p a f -> p (a f)"),
                                          psX[:, P:2 * P], x1[:], ALU.add).then_inc(s["x2_full"], 1)

        @block.gpsimd
        def _(pool):
            pool.memset(kT[:], 0.0).then_inc(s["kprev"], 1)
            pool.wait_ge(s["kprev"], 1)
            pool.memset(vprev[:], 0.0).then_inc(s["vprev"], 1)
            pool.sem_inc(s["qk_added"], 1)
            pool.sem_inc(s["rinv_a"], 1)
            pool.sem_inc(s["layer_done"], 1)
            pool.sem_inc(s["x2_full"], 1)
            with pool.Fori(0, DEPTH) as l:
                with pool.Fori(0, B) as b:
                    with pool.Fori(0, TB) as i:
                        t = l * NT + b * TB + i
                        pool.wait_ge(s["x2_full"], t + 1)
                        pool.tensor_copy(xcur[:], XF[:, bass.ds(b * TB + i, 1), :].rearrange("p a f -> p (a f)"))\
                            .then_inc(s["x_full"], 1)
                        for u in range(NG):
                            wait_apart(pool, s["norms"], t * NG + u + 2, s["passed_pool"])
                            pool.tensor_scalar(ssm[:], ss[:], 1e-24, None, ALU.max).then_inc(s["rinv_a"], 1)
                            pool.wait_ge(s["rinv_a"], t * NG + u + 2)
                            pool.tensor_tensor(rn[:, u % 2, :], ssm[:], half[:], ALU.pow).then_inc(s["rinv"], 1)
                            pool.wait_ge(s["qk_free"], t * (2 * NG) + 2 * u + 4)
                            pool.tensor_tensor(tadd[:], tc[:], tsn[:], ALU.add).then_inc(s["qk_added"], 1)
                            pool.wait_ge(s["qk_added"], t * NG + u + 2)
                            pool.wait_ge(s["rinv"], t * NG + u + 1)
                            if u >= 2:
                                pool.wait_ge(s["qkT"], t * NG + u - 1)
                            pool.tensor_tensor(qk[:, u % 2, :].rearrange("p (g d) -> p g d", d=WD),
                                               tadd[:].rearrange("p j h d -> p (j h) d"),
                                               rn[:, u % 2, :].rearrange("p (g a) -> p g a", a=1).broadcast_to([P, 2 * GH, WD]), ALU.mult)\
                                .then_inc(s["qk_rot"], 1)
                        wait_apart(pool, s["scores"], t * NG + NG + 1, s["passed_pool"])
                        pool.tensor_tensor(kT[:, :, :, P:KW].rearrange("p u a k -> p (u a) k"),
                                           kT[:, :, :, P - WIN:P].rearrange("p u a k -> p (u a) k"),
                                           flag[:, bass.ds(i, 1)].rearrange("p (a b) -> p a b", a=1)
                                           .broadcast_to([P, 2 * NG, WIN]), ALU.mult).then_inc(s["kprev"], 1)
                        wait_apart(pool, s["pv"], t * NG + NG + 1, s["passed_pool"])
                        wait_apart(pool, s["kprev"], t + 2, s["passed_pool"])
                        pool.tensor_copy(vprev[P - WIN:P, :], vcur[P - WIN:P, :]).then_inc(s["vprev"], 1)
                        wait_apart(pool, s["vprev"], t + 2, s["passed_pool"])
                        wait_apart(pool, s["f_mv"], t + 1, s["passed_pool"])
                        pool.tensor_scalar(vr[:], mv[:, 1:2], EPS, None, ALU.add).then_inc(s["f_var"], 1)
                        pool.wait_ge(s["f_var"], t + 1)
                        pool.tensor_tensor(rstd[:], vr[:], half[:, 0:1], ALU.pow).then_inc(s["f_rstd"], 1)
                pool.wait_ge(s["x2_full"], (l + 1) * NT + 1)
                pool.sem_inc(s["layer_done"], 1)


H, HD = 16, 8
CH = 512
NC_ = B * N // CH
TC = CH // P
SP3 = 3
Q_PARTS = (0, 0, 0, 1, 1, 2)
K_PARTS = (0, 1, 2, 0, 1, 0)
KS = HD * len(Q_PARTS)
KEEP = N // 4
NGLOB = 64
BW = N + (TB - 1) * P


def flipped(tile, tiles):
    a = tile.rearrange("p (t c) -> p t c", c=P)[:, :, P - 1:P]
    return bass.AP(a.tensor, a.offset, [list(a.ap[0]), [P, tiles], [-1, P]])


def project_heads(nc, XN, ident, V, w, pre, qk_parts, scores, flip):
    with ExitStack() as ctx:
        m = Memory(nc, ctx, pre + "p_")
        wq, wk, wv = (m.sb(n, [P, D]) for n in ("wq", "wk", "wv"))
        bq, bqs, bk, bv = m.sb("bq", [P, 1]), m.sb("bqs", [P, 1]), m.sb("bk", [P, 1]), m.sb("bv", [P, D])
        xcur, xT = m.sb("xcur", [P, CH]), m.sb("xT", [P, CH])
        qk, rest = m.sb("qk", [P, 2, CH]), m.sb("rest", [P, 2, CH])
        parts = m.sb("parts", [P, SP3, 2, CH], BF16)
        psX, psQ, psK, psV, psS = (m.ps(n, [P, CH]) for n in ("psX", "psQ", "psK", "psV", "psS"))
        names = """weights bias x xT_ps xT q k v qk_sb high r1 mid low v_sb stored sc sc_sb sc_stored passed"""
        s = {n: m.sem(n) for n in names.split()}
        if scores is not None:
            ws, bs, sc = m.sb("ws", [P, H]), m.sb("bs", [H, 1]), m.sb("sc", [H, CH])
        block = ctx.enter_context(nc.Block())
        scale = 1.0 / float(np.sqrt(np.float32(HD)))
        NWT = 16 * (6 + (2 if scores is not None else 0))

        @block.sync
        def _(sp):
            for dst, name in ((wq, "wq"), (wk, "wk"), (wv, "wv"), (bq, "bq"), (bk, "bk")):
                sp.dma_start(dst[:], w[pre + name]).then_inc(s["weights"], 16)
            sp.dma_start(bv[:], w[pre + "bv"].broadcast_to([P, D])).then_inc(s["weights"], 16)
            if scores is not None:
                sp.dma_start(ws[:], w[pre + "ws"]).then_inc(s["weights"], 16)
                sp.dma_start(bs[:], w[pre + "bs"]).then_inc(s["weights"], 16)
            with sp.Fori(0, NC_) as c:
                sp.wait_ge(s["low"], c + 2)
                for part in range(SP3):
                    sp.dma_start(qk_parts[part, :, :, bass.ds(c * CH, CH)].rearrange("j p t -> p j t"),
                                 parts[:, part]).then_inc(s["stored"], 16)
                if scores is not None:
                    wait_apart(sp, s["sc_sb"], c + 1, s["passed"])
                    sp.dma_start(scores[:, bass.ds(c * CH, CH)], sc[:]).then_inc(s["sc_stored"], 16)
            sp.wait_ge(s["stored"], 48 * (NC_ + 1))
            if scores is not None:
                sp.wait_ge(s["sc_stored"], 16 * (NC_ + 1))

        @block.gpsimd
        def _(pool):
            pool.sem_inc(s["x"], 1)
            with pool.Fori(0, NC_) as c:
                pool.wait_ge(s["xT"], c + 1)
                pool.tensor_copy(xcur[:].rearrange("p (t f) -> p t f", t=TC), XN[:, bass.ds(c * TC, TC), :])\
                    .then_inc(s["x"], 1)

        @block.tensor
        def _(pe):
            pe.wait_ge(s["weights"], NWT)
            with pe.Fori(0, NC_) as c:
                pe.wait_ge(s["x"], c + 2)
                for j in range(TC):
                    mm = pe.transpose(psX[:, j * P:(j + 1) * P], xcur[:, j * P:(j + 1) * P], ident[:])
                mm.then_inc(s["xT_ps"], 1)
                pe.wait_ge(s["xT"], c + 2)
                pe.wait_ge(s["qk_sb"], c + 1)
                pe.matmul(psQ[:], wq[:], xT[:], start=True, stop=True).then_inc(s["q"], 1)
                pe.matmul(psK[:], wk[:], xT[:], start=True, stop=True).then_inc(s["k"], 1)
                if scores is not None:
                    pe.matmul(psS[0:H, :], ws[:], xT[:], start=True, stop=True).then_inc(s["sc"], 1)
                pe.wait_ge(s["v_sb"], c + 1)
                for j in range(TC):
                    mm = pe.matmul(psV[:, j * P:(j + 1) * P], xT[:, j * P:(j + 1) * P], wv[:], start=True, stop=True)
                mm.then_inc(s["v"], 1)

        @block.scalar
        def _(act):
            act.sem_inc(s["xT"], 1)
            act.sem_inc(s["qk_sb"], 1)
            act.wait_ge(s["weights"], NWT)
            act.activation(bqs[:], bq[:], ACT.Copy, scale=scale).then_inc(s["bias"], 1)
            act.wait_ge(s["bias"], 1)
            with act.Fori(0, NC_) as c:
                act.wait_ge(s["xT_ps"], c + 1)
                act.wait_ge(s["v"], c + 1)
                act.activation(xT[:], psX[:], ACT.Copy).then_inc(s["xT"], 1)
                act.wait_ge(s["q"], c + 1)
                act.wait_ge(s["low"], c + 1)
                if flip:
                    act.activation(flipped(qk[:, 0], TC), psQ[:].rearrange("p (t c) -> p t c", c=P), ACT.Identity,
                                   bias=bqs[:], scale=scale)
                else:
                    act.activation(qk[:, 0], psQ[:], ACT.Identity, bias=bqs[:], scale=scale)
                act.wait_ge(s["k"], c + 1)
                act.activation(qk[:, 1], psK[:], ACT.Identity, bias=bk[:]).then_inc(s["qk_sb"], 1)
                if scores is not None:
                    act.wait_ge(s["sc"], c + 1)
                    act.wait_ge(s["sc_stored"], 16 * c + 16)
                    act.activation(sc[:], psS[0:H, :], ACT.Identity, bias=bs[:]).then_inc(s["sc_sb"], 1)

        @block.vector
        def _(dve):
            dve.sem_inc(s["low"], 1)
            dve.sem_inc(s["v_sb"], 1)
            dve.sem_inc(s["v"], 1)
            dve.sem_inc(s["stored"], 48)
            dve.sem_inc(s["sc_stored"], 16)
            dve.wait_ge(s["weights"], NWT)
            with dve.Fori(0, NC_) as c:
                dve.wait_ge(s["qk_sb"], c + 2)
                dve.wait_ge(s["stored"], 48 * c + 48)
                dve.tensor_copy(parts[:, 0], qk[:]).then_inc(s["high"], 1)
                dve.wait_ge(s["high"], c + 1)
                dve.tensor_tensor(rest[:], qk[:], parts[:, 0], ALU.subtract).then_inc(s["r1"], 1)
                dve.wait_ge(s["r1"], c + 1)
                dve.tensor_copy(parts[:, 1], rest[:]).then_inc(s["mid"], 1)
                dve.wait_ge(s["mid"], c + 1)
                dve.tensor_tensor(parts[:, 2], rest[:], parts[:, 1], ALU.subtract).then_inc(s["low"], 1)
                dve.wait_ge(s["v"], c + 2)
                dve.tensor_tensor(V[:, bass.ds(c * TC, TC), :], psV[:].rearrange("p (t f) -> p t f", t=TC),
                                  bv[:].rearrange("p (a f) -> p a f", a=1).broadcast_to([P, TC, D]), ALU.add)\
                    .then_inc(s["v_sb"], 1)


def select_keys(nc, scores, topmask):
    with ExitStack() as ctx:
        m = Memory(nc, ctx, "top_")
        sc, work = m.sb("sc", [B * H, N]), m.sb("work", [B * H, N])
        best = m.sb("best", [B * H, 8])
        left, mask = m.sb("left", [B * H, N]), m.sb("mask", [B * H, N], BF16)
        loaded, s_best, s_work, s_left, s_mask, stored, passed = (
            m.sem(n) for n in ("loaded", "best", "work", "left", "mask", "stored", "passed"))
        block = ctx.enter_context(nc.Block())

        @block.sync
        def _(sp):
            for b in range(B):
                sp.dma_start(sc[b * H:(b + 1) * H, :], scores[:, b * N:(b + 1) * N]).then_inc(loaded, 16)
            sp.wait_ge(s_mask, 1)
            sp.dma_start(topmask, mask[:]).then_inc(stored, 16)
            sp.wait_ge(stored, 16)

        @block.vector
        def _(dve):
            dve.wait_ge(loaded, 16 * B)
            dve.tensor_copy(work[:], sc[:]).then_inc(s_work, 1)
            for k in range(KEEP // 8):
                dve.wait_ge(s_work, k + 1)
                dve.max(best[:], work[:]).then_inc(s_best, 1)
                dve.wait_ge(s_best, k + 1)
                dve.match_replace(work[:], best[:], work[:], -3.0e38).then_inc(s_work, 1)
            dve.wait_ge(s_work, KEEP // 8 + 1)
            dve.tensor_tensor(left[:], work[:], sc[:], ALU.is_equal).then_inc(s_left, 1)
            dve.wait_ge(s_left, 1)
            dve.tensor_scalar(mask[:], left[:], NEG, None, ALU.mult).then_inc(s_mask, 1)


def relative_bias(nc, w, bias):
    R, HID = 2 * N, 32
    with ExitStack() as ctx:
        m = Memory(nc, ctx, "rpe_")
        rel, hid = m.sb("rel", [HID, R]), m.sb("hid", [HID, R])
        w1, b1, w2, b2 = m.sb("w1", [HID, 1]), m.sb("b1", [HID, 1]), m.sb("w2", [HID, H]), m.sb("b2", [H, 1])
        o = m.sb("o", [H, R])
        ps = m.ps("ps", [H, R])
        loaded, hidden, ready, done, stored = (m.sem(n) for n in ("loaded", "hidden", "ready", "done", "stored"))
        block = ctx.enter_context(nc.Block())

        @block.sync
        def _(sp):
            sp.dma_start(rel[:], w["rel"].broadcast_to([HID, R])).then_inc(loaded, 16)
            for dst, name in ((w1, "rpe_w1"), (b1, "rpe_b1"), (w2, "rpe_w2"), (b2, "rpe_b2")):
                sp.dma_start(dst[:], w[name]).then_inc(loaded, 16)
            sp.wait_ge(done, 1)
            sp.dma_start(bias, o[:]).then_inc(stored, 16)
            sp.wait_ge(stored, 16)

        @block.scalar
        def _(act):
            act.wait_ge(loaded, 80)
            act.activation(hid[:], rel[:], ACT.Relu, bias=b1[:], scale=w1[:]).then_inc(hidden, 1)
            act.wait_ge(ready, 1)
            act.activation(o[:], ps[:], ACT.Identity, bias=b2[:]).then_inc(done, 1)

        @block.tensor
        def _(pe):
            pe.wait_ge(loaded, 80)
            pe.wait_ge(hidden, 1)
            for c in range(0, R, 512):
                mm = pe.matmul(ps[:, c:c + 512], w2[:], hid[:, c:c + 512], start=True, stop=True)
            mm.then_inc(ready, 1)


def attend(nc, V, ident, O, qk_parts, pre, bias=None, topmask=None, w=None):
    mixed = topmask is not None
    NR = 3 if mixed else 2
    NTY = 3 if mixed else 1
    KT = 16
    NL = 16 * 13
    with ExitStack() as ctx:
        m = Memory(nc, ctx, pre + "a_")
        qst, kst = m.sb("qst", [64, 2, N], BF16), m.sb("kst", [64, 2, N], BF16)
        vh = m.sb("vh", [P, 2, TB, HD])
        if mixed:
            band = m.sb("band", [P, 3 * P])
        else:
            bt = m.sb("bt", [P, 2, BW])
        z = m.sb("z", [P, 2, 3 * P if mixed else N])
        pr = m.sb("pr", [P, 2, N + (3 * P + NGLOB if mixed else 0)])
        prT = m.sb("prT", [P, NR, 4 * P])
        nmax = m.sb("nmax", [P, 2, 4])
        zs = m.sb("zs", [P, 2, TB, NTY])
        rz = m.sb("rz", [P, TB, NTY])
        ot, osum = m.sb("ot", [P, TB * NTY, HD]), m.sb("osum", [P, TB, HD])
        psS = [m.ps(f"psS{j}", [P, N]) for j in range(2)]
        psG = [m.ps(f"psG{j}", [P, 512]) for j in range(2)] if mixed else None
        psT = [m.ps(f"psT{j}", [P, 512]) for j in range(1 if mixed else 2)]
        psO = [m.ps(f"psO{j}", [P, 512]) for j in range(1 if mixed else 2)]
        s = {n: m.sem(n) for n in """const ones load0 load1 vcopy scores z probs norm rz ot osum passed""".split()}
        turned, turned_sb, pv = ([m.sem(f"{n}{r}") for r in range(NR)] for n in ("turned", "turned_sb", "pv"))
        block = ctx.enter_context(nc.Block())

        def plan(qt, r):
            if not mixed or r < 2:
                return [((4 * r + j) * P, 4 * r + j, P, 0) for j in range(4)]
            lo, hi = max(qt - 1, 0), min(qt + 1, TB - 1)
            return [(N + (j - lo) * P, j, P, 1) for j in range(lo, hi + 1)] + [(N + 3 * P, 0, NGLOB, 2)]

        def band_of(qt):
            lo, hi = max(qt - 1, 0), min(qt + 1, TB - 1)
            return lo * P, (lo - qt + 1) * P, (hi - lo + 1) * P

        @block.sync
        def _(sp):
            if mixed:
                sp.dma_start(band[:], w["band"]).then_inc(s["const"], 16)
            sp.wait_ge(s["ones"], 1)
            with sp.Fori(0, B) as b:
                with sp.Fori(0, H // 2) as hp:
                    for par in range(2):
                        it = b * (H // 2) + hp
                        wait_apart(sp, s["z"], it * KT + (par + 1) * TB, s["passed"])
                        load = s[f"load{par}"]

                        def rows(j, part):
                            return qk_parts[part:part + 1, j, bass.ds(hp * (2 * HD) + par * HD, HD),
                                            bass.ds(b * N, N)]

                        for row, part in enumerate(Q_PARTS):
                            sp.dma_start(qst[row * HD:(row + 1) * HD, par, :],
                                         rows(0, part).rearrange("a d t -> (a d) t")).then_inc(load, 16)
                        for row, part in enumerate(K_PARTS):
                            sp.dma_start(kst[row * HD:(row + 1) * HD, par, :],
                                         rows(1, part).rearrange("a d t -> (a d) t")).then_inc(load, 16)
                        if mixed:
                            sp.dma_start(kst[KS:KS + 1, par, :], topmask[bass.ds(b * H + hp * 2 + par, 1), :])\
                                .then_inc(load, 16)
                        else:
                            a = bias[bass.ds(hp * 2 + par, 1), 0:BW]
                            sp.dma_start(bt[:, par, :], bass.AP(a.tensor, a.offset, [[1, P], [1, BW]]))\
                                .then_inc(load, 16)

        @block.gpsimd
        def _(pool):
            pool.memset(qst[:], 1.0).then_inc(s["ones"], 1)
            with pool.Fori(0, B) as b:
                with pool.Fori(0, H // 2) as hp:
                    for par in range(2):
                        it = b * (H // 2) + hp
                        pool.wait_ge(s["norm"], 2 * it + par + 1)
                        pool.tensor_copy(vh[:, par], V[:, bass.ds(b * TB, TB), bass.ds(hp * (2 * HD) + par * HD, HD)])\
                            .then_inc(s["vcopy"], 1)

        @block.tensor
        def _(pe):
            pe.sem_inc(turned[NR - 1], 2)
            for r in range(NR):
                pe.sem_inc(pv[r], 1)
            pe.wait_ge(s["ones"], 1)
            with pe.Fori(0, B * H // 2) as it:

                def score(k):
                    n, par, qt = it * KT + k, k // TB, k % TB
                    if qt == 0:
                        pe.wait_ge(s[f"load{par}"], NL * it + NL)
                    pe.wait_ge(s["z"], n + 15)
                    if mixed:
                        pe.wait_ge(s["probs"], n + 1)
                    q = slice(qt * P, (qt + 1) * P)
                    rows = KS + 1 if mixed else KS
                    for c in range(2):
                        mm = pe.matmul(psS[k % 2][:, c * 512:(c + 1) * 512], qst[0:rows, par, q],
                                       kst[0:rows, par, c * 512:(c + 1) * 512], start=True, stop=True)
                    if mixed:
                        k0, _, width = band_of(qt)
                        pe.matmul(psG[k % 2][:, 0:width], qst[0:KS, par, q], kst[0:KS, par, k0:k0 + width],
                                  start=True, stop=True)
                        mm = pe.matmul(psG[k % 2][:, 3 * P:3 * P + NGLOB], qst[0:KS, par, q], kst[0:KS, par, 0:NGLOB],
                                       start=True, stop=True)
                    mm.then_inc(s["scores"], 1)

                def weigh(k):
                    n, par, qt = it * KT + k, k // TB, k % TB
                    pe.wait_ge(s["probs"], n + 3)

                    def times_v(r):
                        pe.wait_ge(turned_sb[r], n + 2)
                        blocks = plan(qt, r)
                        for j, (_, kb, keys, kind) in enumerate(blocks):
                            c = (qt * NTY + kind) * HD
                            first = kb == 0 if kind == 0 else (kind == 2 or j == 0)
                            last = kb == TB - 1 if kind == 0 else (kind == 2 or blocks[j + 1][3] == 2)
                            mm = pe.matmul(psO[par % len(psO)][:, c:c + HD], prT[0:keys, r, j * P:(j + 1) * P],
                                           vh[0:keys, par, kb, :], start=first, stop=last)
                        mm.then_inc(pv[r], 1)

                    for r in range(NR):
                        if mixed and r > 0:
                            pe.wait_ge(turned_sb[r - 1], n + 2)
                        else:
                            pe.wait_ge(turned_sb[NR - 1 if mixed else r], n + 1)
                        for j, (c0, _, keys, _) in enumerate(plan(qt, r)):
                            mm = pe.transpose(psT[r % len(psT)][0:keys, j * P:(j + 1) * P],
                                              pr[:, k % 2, c0:c0 + keys], ident[:])
                        mm.then_inc(turned[r], 1)
                        if r == 0 and qt == 0:
                            pe.wait_ge(s["vcopy"], 2 * it + par + 1)
                            pe.wait_ge(s["norm"], 2 * it + par + (2 if mixed else 1))
                        if r > 0:
                            times_v(r - 1)
                    times_v(NR - 1)

                for k in range(KT + 1):
                    if k < KT:
                        score(k)
                    if k >= 1:
                        weigh(k - 1)

        def copy_round(eng, copy, n, qt, r):
            eng.wait_ge(turned[r], n + (3 if r == NR - 1 else 1))
            eng.wait_ge(pv[r], n + 1)
            blocks = plan(qt, r)
            full = sum(keys == P for _, _, keys, _ in blocks)
            c = copy(prT[:, r, 0:full * P], psT[r % len(psT)][:, 0:full * P])
            if full < len(blocks):
                c = copy(prT[0:NGLOB, r, full * P:(full + 1) * P], psT[r % len(psT)][0:NGLOB, full * P:(full + 1) * P])
            c.then_inc(turned_sb[r], 1)

        @block.scalar
        def _(act):
            act.sem_inc(s["probs"], 2)
            act.sem_inc(turned_sb[1], 1)
            with act.Fori(0, B * H // 2) as it:
                for k in range(KT + 1):
                    if k < KT:
                        n, par, qt = it * KT + k, k // TB, k % TB
                        act.wait_ge(s["z"], n + 17)
                        act.wait_ge(turned[NR - 1], n + 1)
                        if qt == 0:
                            act.wait_ge(s["norm"], 2 * it + par + 1)
                        nm = nmax[:, k % 2, :]
                        if mixed:
                            _, _, width = band_of(qt)
                            act.activation(pr[:, k % 2, 0:N], psS[k % 2][:], ACT.Exp, bias=nm[:, 0:1],
                                           accum_out=zs[:, par, qt, 0:1])
                            act.activation(pr[:, k % 2, N:N + width], z[:, k % 2, 0:width], ACT.Exp, bias=nm[:, 1:2],
                                           scale=-1.0, accum_out=zs[:, par, qt, 1:2])
                            e = act.activation(pr[:, k % 2, N + 3 * P:N + 3 * P + NGLOB],
                                               psG[k % 2][:, 3 * P:3 * P + NGLOB], ACT.Exp, bias=nm[:, 2:3],
                                               accum_out=zs[:, par, qt, 2:3])
                        else:
                            e = act.activation(pr[:, k % 2, :], z[:, k % 2, :], ACT.Exp, bias=nm[:, 0:1], scale=-1.0,
                                               accum_out=zs[:, par, qt, 0:1])
                        e.then_inc(s["probs"], 1)
                    if k >= 1:
                        copy_round(act, lambda o, i: act.activation(o, i, ACT.Copy), it * KT + k - 1, (k - 1) % TB, 1)

        @block.vector
        def _(dve):
            dve.sem_inc(s["z"], 16)
            dve.sem_inc(s["norm"], 2)
            dve.sem_inc(turned_sb[0], 1)
            if mixed:
                dve.sem_inc(turned_sb[2], 1)
                dve.wait_ge(s["const"], 16)
            with dve.Fori(0, B) as b:
                with dve.Fori(0, H // 2) as hp:
                    it = b * (H // 2) + hp

                    def maxima(k):
                        n, par, qt = it * KT + k, k // TB, k % TB
                        dve.wait_ge(s["scores"], n + 1)
                        dve.wait_ge(s["probs"], n + 1)
                        nm = nmax[:, k % 2, :]
                        if mixed:
                            _, c0, width = band_of(qt)
                            dve.tensor_reduce(nm[:, 0:1], psS[k % 2][:], AX.X, ALU.max, negate=True)
                            dve.tensor_tensor_reduce(z[:, k % 2, 0:width], psG[k % 2][:, 0:width],
                                                     band[:, c0:c0 + width], -1.0, 3.0e38, ALU.add, ALU.min, nm[:, 1:2])
                            dve.tensor_reduce(nm[:, 2:3], psG[k % 2][:, 3 * P:3 * P + NGLOB], AX.X, ALU.max,
                                              negate=True).then_inc(s["z"], 1)
                        else:
                            c0 = (TB - 1 - qt) * P
                            wait_apart(dve, s[f"load{par}"], NL * it + NL, s["passed"])
                            dve.tensor_tensor_reduce(z[:, k % 2, :], psS[k % 2][:], bt[:, par, c0:c0 + N], -1.0, 3.0e38,
                                                     ALU.add, ALU.min, nm[:, 0:1]).then_inc(s["z"], 1)

                    def normalize(par):
                        n = it * KT + par * TB + TB - 1
                        nh = 2 * it + par
                        dve.wait_ge(s["probs"], n + 3)
                        dve.reciprocal(rz[:], zs[:, par]).then_inc(s["rz"], 1)
                        dve.wait_ge(pv[NR - 1], n + 2)
                        dve.wait_ge(s["rz"], nh + 1)
                        sums = psO[par % len(psO)][:, 0:TB * NTY * HD].rearrange("p (q d) -> p q d", d=HD)
                        rzb = rz[:].rearrange("p q (k a) -> p (q k) a", a=1).broadcast_to([P, TB * NTY, HD])
                        dst = O[:, bass.ds(b * TB, TB), bass.ds(hp * (2 * HD) + par * HD, HD)]
                        if mixed:
                            dve.tensor_tensor(ot[:], sums, rzb, ALU.mult).then_inc(s["ot"], 1)
                            dve.wait_ge(s["ot"], nh + 1)
                            dve.tensor_reduce(osum[:], ot[:].rearrange("p (q k) d -> p q d k", k=NTY), AX.X, ALU.add)\
                                .then_inc(s["osum"], 1)
                            dve.wait_ge(s["osum"], nh + 1)
                            dve.tensor_scalar(dst, osum[:], 1.0 / 3.0, None, ALU.mult).then_inc(s["norm"], 1)
                        else:
                            dve.tensor_tensor(dst, sums, rzb, ALU.mult).then_inc(s["norm"], 1)

                    for k in range(KT + 1):
                        if k < KT:
                            maxima(k)
                        if k >= 1:
                            copy_round(dve, dve.tensor_copy, it * KT + k - 1, (k - 1) % TB, 0)
                            if mixed:
                                copy_round(dve, dve.tensor_copy, it * KT + k - 1, (k - 1) % TB, 2)
                            if k % TB == 0:
                                normalize(k // TB - 1)


def project_out(nc, O, X, ident, w, pre, flip):
    with ExitStack() as ctx:
        m = Memory(nc, ctx, pre + "o_")
        wo, bo, ones = m.sb("wo", [P, D]), m.sb("bo", [1, D]), m.sb("ones", [1, P])
        ocur, oT = m.sb("ocur", [P, D]), m.sb("oT", [P, D])
        psT, psY = m.ps("psT", [P, 512]), m.ps("psY", [P, 512])
        s = {n: m.sem(n) for n in "weights one cur turned oT y added".split()}
        block = ctx.enter_context(nc.Block())

        @block.sync
        def _(sp):
            sp.dma_start(wo[:], w[pre + "wo"]).then_inc(s["weights"], 16)
            sp.dma_start(bo[:], w[pre + "bo"]).then_inc(s["weights"], 16)
            sp.wait_ge(s["weights"], 32)

        @block.gpsimd
        def _(pool):
            pool.memset(ones[:], 1.0).then_inc(s["one"], 1)
            with pool.Fori(0, NT) as t:
                pool.wait_ge(s["turned"], t + 1)
                pool.tensor_copy(ocur[:], O[:, bass.ds(t, 1), :].rearrange("p a f -> p (a f)")).then_inc(s["cur"], 1)

        @block.tensor
        def _(pe):
            pe.sem_inc(s["turned"], 1)
            pe.wait_ge(s["weights"], 32)
            pe.wait_ge(s["one"], 1)
            with pe.Fori(0, NT) as t:
                pe.wait_ge(s["cur"], t + 1)
                pe.wait_ge(s["oT"], t + 1)
                pe.transpose(psT[:, 0:P], ocur[:], ident[:]).then_inc(s["turned"], 1)
                pe.wait_ge(s["oT"], t + 2)
                pe.wait_ge(s["added"], t + 1)
                pe.matmul(psY[:, 0:D], oT[:], wo[:], start=True, stop=False)
                pe.matmul(psY[:, 0:D], ones[:], bo[:], start=False, stop=True).then_inc(s["y"], 1)

        @block.scalar
        def _(act):
            act.sem_inc(s["oT"], 1)
            act.sem_inc(s["y"], 1)
            with act.Fori(0, NT) as t:
                act.wait_ge(s["turned"], t + 2)
                act.wait_ge(s["y"], t + 1)
                if flip:
                    act.activation(flipped(oT[:], 1), psT[:, 0:P].rearrange("p (t c) -> p t c", c=P), ACT.Copy)\
                        .then_inc(s["oT"], 1)
                else:
                    act.activation(oT[:], psT[:, 0:P], ACT.Copy).then_inc(s["oT"], 1)

        @block.vector
        def _(dve):
            dve.sem_inc(s["added"], 1)
            with dve.Fori(0, NT) as t:
                dve.wait_ge(s["y"], t + 2)
                x = X[:, bass.ds(t, 1), :].rearrange("p a f -> p (a f)")
                dve.tensor_tensor(x, psY[:, 0:D], x, ALU.add).then_inc(s["added"], 1)


L, MH = B, 4
MD = D // MH
E, FF = 8, 512
CAP = B * N // E


def cross_attention(nc, XN, Y, ident, w):
    with ExitStack() as ctx:
        m = Memory(nc, ctx, "m_")
        win, bin_ = m.sb("win", [P, 3 * D]), m.sb("bin", [P, 3 * D])
        wout, bout = m.sb("wout", [P, D]), m.sb("bout", [P, D])
        xcur, xT = m.sb("xcur", [P, L, D]), m.sb("xT", [P, L, P])
        qkv = m.sb("qkv", [P, L, 3 * D])
        prod = m.sb("prod", [P, L, L, D])
        sc, sub, ex, pn = (m.sb(n, [P, L * L * MH]) for n in ("sc", "sub", "ex", "pn"))
        mx, zs, rz = (m.sb(n, [P, L * MH]) for n in ("mx", "zs", "rz"))
        o, oT = m.sb("o", [P, L, D]), m.sb("oT", [P, L, P])
        yb = m.sb("yb", [P, L, D])
        psX, psQ, psY = m.ps("psX", [P, 512]), m.ps("psQ", [P, L, 512]), m.ps("psY", [P, 512])
        s = {n: m.sem(n) for n in """weights x xT_ps xT qkv_ps qkv prod sc mx sub ex zs rz pn pv o oT_ps oT
            y_ps yb y""".split()}
        block = ctx.enter_context(nc.Block())
        scale = 1.0 / float(np.sqrt(MD))

        @block.sync
        def _(sp):
            sp.dma_start(win[:], w["m_win"]).then_inc(s["weights"], 16)
            sp.dma_start(bin_[:], w["m_bin"].broadcast_to([P, 3 * D])).then_inc(s["weights"], 16)
            sp.dma_start(wout[:], w["m_wout"]).then_inc(s["weights"], 16)
            sp.dma_start(bout[:], w["m_bout"].broadcast_to([P, D])).then_inc(s["weights"], 16)
            sp.wait_ge(s["weights"], 64)

        @block.gpsimd
        def _(pool):
            with pool.Fori(0, TB) as j:
                pool.wait_ge(s["y"], j + 1)
                pool.tensor_copy(xcur[:], XN[:].rearrange("p (l j) f -> p l j f", l=L)[:, :, bass.ds(j, 1), :]
                                 .rearrange("p l a f -> p l (a f)")).then_inc(s["x"], 1)

        @block.tensor
        def _(pe):
            pe.wait_ge(s["weights"], 64)
            with pe.Fori(0, TB) as j:
                pe.wait_ge(s["x"], j + 1)
                for l in range(L):
                    mm = pe.transpose(psX[:, l * P:(l + 1) * P], xcur[:, l, :], ident[:])
                mm.then_inc(s["xT_ps"], 1)
                pe.wait_ge(s["xT"], j + 1)
                for l in range(L):
                    mm = pe.matmul(psQ[:, l, 0:3 * D], xT[:, l, :], win[:], start=True, stop=True)
                mm.then_inc(s["qkv_ps"], 1)
                pe.wait_ge(s["o"], j + 1)
                for l in range(L):
                    mm = pe.transpose(psX[:, l * P:(l + 1) * P], o[:, l, :], ident[:])
                mm.then_inc(s["oT_ps"], 1)
                pe.wait_ge(s["oT"], j + 1)
                for l in range(L):
                    mm = pe.matmul(psY[:, l * P:(l + 1) * P], oT[:, l, :], wout[:], start=True, stop=True)
                mm.then_inc(s["y_ps"], 1)

        @block.scalar
        def _(act):
            with act.Fori(0, TB) as j:
                act.wait_ge(s["xT_ps"], j + 1)
                act.activation(xT[:].rearrange("p l c -> p (l c)"), psX[:], ACT.Copy).then_inc(s["xT"], 1)
                act.wait_ge(s["sub"], j + 1)
                act.activation(ex[:], sub[:], ACT.Exp, scale=scale).then_inc(s["ex"], 1)
                act.wait_ge(s["oT_ps"], j + 1)
                act.activation(oT[:].rearrange("p l c -> p (l c)"), psX[:], ACT.Copy).then_inc(s["oT"], 1)

        @block.vector
        def _(dve):
            dve.sem_inc(s["y"], 1)
            dve.wait_ge(s["weights"], 64)
            with dve.Fori(0, TB) as j:
                dve.wait_ge(s["qkv_ps"], j + 1)
                dve.tensor_tensor(qkv[:], psQ[:, :, 0:3 * D],
                                  bin_[:].rearrange("p (a f) -> p a f", a=1).broadcast_to([P, L, 3 * D]), ALU.add)\
                    .then_inc(s["qkv"], 1)
                dve.wait_ge(s["qkv"], j + 1)
                for l in range(L):
                    d = dve.tensor_tensor(prod[:, l], qkv[:, l:l + 1, 0:D].broadcast_to([P, L, D]), qkv[:, :, D:2 * D],
                                          ALU.mult)
                d.then_inc(s["prod"], 1)
                dve.wait_ge(s["prod"], j + 1)
                dve.tensor_reduce(sc[:], prod[:].rearrange("p l m (h d) -> p (l m h) d", d=MD), AX.X, ALU.add)\
                    .then_inc(s["sc"], 1)
                dve.wait_ge(s["sc"], j + 1)
                by_key = "p (l m h) -> p l h m"
                dve.tensor_reduce(mx[:].rearrange("p (l h) -> p l h", l=L), sc[:].rearrange(by_key, l=L, m=L), AX.X,
                                  ALU.max).then_inc(s["mx"], 1)
                dve.wait_ge(s["mx"], j + 1)
                over = lambda t: t[:].rearrange("p (l a h) -> p l a h", l=L, a=1).broadcast_to([P, L, L, MH])
                lmh = lambda t: t[:].rearrange("p (l m h) -> p l m h", l=L, m=L)
                dve.tensor_tensor(lmh(sub), lmh(sc), over(mx), ALU.subtract).then_inc(s["sub"], 1)
                dve.wait_ge(s["ex"], j + 1)
                dve.tensor_reduce(zs[:].rearrange("p (l h) -> p l h", l=L), ex[:].rearrange(by_key, l=L, m=L), AX.X,
                                  ALU.add).then_inc(s["zs"], 1)
                dve.wait_ge(s["zs"], j + 1)
                dve.reciprocal(rz[:], zs[:]).then_inc(s["rz"], 1)
                dve.wait_ge(s["rz"], j + 1)
                dve.tensor_tensor(lmh(pn), lmh(ex), over(rz), ALU.mult).then_inc(s["pn"], 1)
                dve.wait_ge(s["pn"], j + 1)
                for l in range(L):
                    d = dve.tensor_tensor(
                        prod[:, l].rearrange("p m (h d) -> p m h d", h=MH),
                        pn[:, l * L * MH:(l + 1) * L * MH].rearrange("p (m h a) -> p m h a", m=L, a=1)
                        .broadcast_to([P, L, MH, MD]),
                        qkv[:, :, 2 * D:3 * D].rearrange("p m (h d) -> p m h d", h=MH), ALU.mult)
                d.then_inc(s["pv"], 1)
                dve.wait_ge(s["pv"], j + 1)
                dve.tensor_reduce(o[:], prod[:].rearrange("p l m f -> p l f m"), AX.X, ALU.add).then_inc(s["o"], 1)
                dve.wait_ge(s["y_ps"], j + 1)
                dve.tensor_tensor(yb[:], psY[:].rearrange("p (l f) -> p l f", l=L),
                                  bout[:].rearrange("p (a f) -> p a f", a=1).broadcast_to([P, L, D]), ALU.add)\
                    .then_inc(s["yb"], 1)
                dve.wait_ge(s["yb"], j + 1)
                dve.tensor_tensor(Y[:].rearrange("p (l j) f -> p l j f", l=L)[:, :, bass.ds(j, 1), :]
                                  .rearrange("p l a f -> p l (a f)"), yb[:], xcur[:], ALU.add).then_inc(s["y"], 1)


def scale_shift(nc, Y, w, g, b, X=None):
    with ExitStack() as ctx:
        m = Memory(nc, ctx, g + "_")
        gb, bb = m.sb("g", [P, D]), m.sb("b", [P, D])
        loaded, scaled, shifted_, = (m.sem(n) for n in ("loaded", "scaled", "shifted"))
        block = ctx.enter_context(nc.Block())

        @block.sync
        def _(sp):
            sp.dma_start(gb[:], w[g].broadcast_to([P, D])).then_inc(loaded, 16)
            sp.dma_start(bb[:], w[b].broadcast_to([P, D])).then_inc(loaded, 16)
            sp.wait_ge(loaded, 32)

        @block.vector
        def _(dve):
            row = lambda t: t[:].rearrange("p (a f) -> p a f", a=1).broadcast_to([P, NT, D])
            dve.wait_ge(loaded, 32)
            dve.tensor_tensor(Y[:], Y[:], row(gb), ALU.mult).then_inc(scaled, 1)
            dve.wait_ge(scaled, 1)
            dve.tensor_tensor(Y[:], Y[:], row(bb), ALU.add).then_inc(shifted_, 1)
            if X is not None:
                dve.wait_ge(shifted_, 1)
                dve.tensor_tensor(X[:], X[:], Y[:], ALU.add)


def experts(nc, Y, YS, ident, w):
    FK = FF // P
    with ExitStack() as ctx:
        m = Memory(nc, ctx, "e_")
        w1T, w2 = m.sb("w1T", [P, E * FK, D]), m.sb("w2", [P, E * FK, D])
        b1 = m.sb("b1", [P, E * FK])
        w12, b12, b2 = m.sb("w12", [P, E * D]), m.sb("b12", [1, E * D]), m.sb("b2", [1, E * D])
        wg, ones, first = m.sb("wg", [P, E]), m.sb("ones", [P, P]), m.sb("first", [P, E])
        upper = m.sb("upper", [P, P])
        ycur, yT = m.sb("ycur", [P, D]), m.sb("yT", [P, P])
        nmx, mx, eq, best, z, ex = (m.sb(n, [P, k]) for n, k in
                                    (("nmx", 1), ("mx", 1), ("eq", E), ("best", 1), ("z", 1), ("ex", E)))
        one = m.sb("one", [P, E])
        prod = m.sb("prod", [P, E, D])
        hot, gate = m.sb("hot", [P, NT, E]), m.sb("gate", [P, NT])
        before = [m.sb(f"before{k}", [P, NT, E]) for k in range(2)]
        rank, mine, keep = m.sb("rank", [P, NT, E]), m.sb("mine", [P, NT]), m.sb("keep", [P, NT])
        psT, psG = m.ps("psT", [P, 512]), m.ps("psG", [P, 512])
        psE, psW = m.ps("psE", [P, E * D]), m.ps("psW", [P, E * D])
        psC, psA = m.ps("psC", [P, 512]), m.ps("psA", [P, 512])
        s = {n: m.sem(n) for n in """weights const w12_ps w12 b12_ps b12 y yT_ps yT logits picked_e nmx mx eq best
            one ex rz prod picked hot counts chain kept""".split()}
        block = ctx.enter_context(nc.Block())
        NW = 16 * 8

        @block.sync
        def _(sp):
            for dst, name in ((w1T, "e_w1T"), (w2, "e_w2"), (b1, "e_b1"), (b2, "e_b2"), (wg, "e_wg"),
                              (first, "first"), (upper, "upper"), (ones, "ones")):
                sp.dma_start(dst[:], w[name]).then_inc(s["weights"], 16)
            sp.wait_ge(s["weights"], NW)

        @block.gpsimd
        def _(pool):
            with pool.Fori(0, NT) as t:
                pool.wait_ge(s["yT_ps"], t + 1)
                pool.tensor_copy(ycur[:], Y[:, bass.ds(t, 1), :].rearrange("p a f -> p (a f)")).then_inc(s["y"], 1)

        @block.tensor
        def _(pe):
            pe.sem_inc(s["yT_ps"], 1)
            pe.wait_ge(s["weights"], NW)
            for e in range(E):
                for k in range(FK):
                    mm = pe.matmul(psW[:, e * D:(e + 1) * D], w1T[:, e * FK + k, :], w2[:, e * FK + k, :],
                                   start=(k == 0), stop=(k == FK - 1))
            mm.then_inc(s["w12_ps"], 1)
            for e in range(E):
                for k in range(FK):
                    mm = pe.matmul(psE[0:1, e * D:(e + 1) * D], b1[:, e * FK + k:e * FK + k + 1],
                                   w2[:, e * FK + k, :], start=(k == 0), stop=(k == FK - 1))
            mm.then_inc(s["b12_ps"], 1)
            pe.wait_ge(s["w12"], 1)
            pe.wait_ge(s["b12"], 1)
            with pe.Fori(0, NT) as t:
                pe.wait_ge(s["y"], t + 1)
                pe.wait_ge(s["yT"], t + 1)
                pe.transpose(psT[:, 0:P], ycur[:], ident[:]).then_inc(s["yT_ps"], 1)
                pe.wait_ge(s["yT"], t + 2)
                pe.wait_ge(s["ex"], t + 1)
                pe.matmul(psG[:, 0:E], yT[:], wg[:], start=True, stop=True).then_inc(s["logits"], 1)
                pe.wait_ge(s["prod"], t + 1)
                for c in range(0, E * D, 512):
                    pe.matmul(psE[:, c:c + 512], yT[:], w12[:, c:c + 512], start=True, stop=False)
                    mm = pe.matmul(psE[:, c:c + 512], ones[0:1, :], b12[:, c:c + 512], start=False, stop=True)
                mm.then_inc(s["picked_e"], 1)
            pe.wait_ge(s["hot"], NT)
            hots = hot[:].rearrange("p t e -> p (t e)")
            pe.matmul(psC[:, 0:NT * E], upper[:], hots, start=True, stop=True)
            pe.matmul(psA[:, 0:NT * E], ones[:], hots, start=True, stop=True).then_inc(s["counts"], 1)

        @block.scalar
        def _(act):
            act.sem_inc(s["yT"], 1)
            act.sem_inc(s["ex"], 1)
            act.wait_ge(s["w12_ps"], 1)
            act.activation(w12[:], psW[:], ACT.Copy).then_inc(s["w12"], 1)
            with act.Fori(0, NT) as t:
                act.wait_ge(s["yT_ps"], t + 2)
                act.wait_ge(s["logits"], t + 1)
                act.activation(yT[:], psT[:, 0:P], ACT.Copy).then_inc(s["yT"], 1)
                act.wait_ge(s["eq"], t + 1)
                act.wait_ge(s["rz"], t + 1)
                act.activation(ex[:], psG[:, 0:E], ACT.Exp, bias=nmx[:], accum_out=z[:]).then_inc(s["ex"], 1)

        @block.vector
        def _(dve):
            dve.sem_inc(s["prod"], 1)
            dve.sem_inc(s["logits"], 1)
            dve.sem_inc(s["rz"], 1)
            dve.wait_ge(s["weights"], NW)
            dve.wait_ge(s["b12_ps"], 1)
            dve.tensor_tensor(b12[:], psE[0:1, :], b2[:], ALU.add).then_inc(s["b12"], 1)
            with dve.Fori(0, NT) as t:
                dve.wait_ge(s["logits"], t + 2)
                dve.tensor_reduce(nmx[:], psG[:, 0:E], AX.X, ALU.max, negate=True)
                dve.tensor_reduce(mx[:], psG[:, 0:E], AX.X, ALU.max).then_inc(s["mx"], 1)
                dve.wait_ge(s["mx"], t + 1)
                dve.scalar_tensor_tensor(eq[:], psG[:, 0:E], mx[:], first[:], ALU.is_equal, ALU.mult)\
                    .then_inc(s["eq"], 1)
                dve.wait_ge(s["eq"], t + 1)
                dve.tensor_reduce(best[:], eq[:], AX.X, ALU.max).then_inc(s["best"], 1)
                dve.wait_ge(s["best"], t + 1)
                dve.tensor_scalar(one[:], eq[:], best[:], None, ALU.is_equal).then_inc(s["one"], 1)
                dve.wait_ge(s["one"], t + 1)
                dve.tensor_copy(hot[:, bass.ds(t, 1), :].rearrange("p a e -> p (a e)"), one[:]).then_inc(s["hot"], 1)
                dve.wait_ge(s["picked_e"], t + 1)
                dve.tensor_tensor(prod[:], psE[:].rearrange("p (e f) -> p e f", e=E),
                                  one[:].rearrange("p (e a) -> p e a", a=1).broadcast_to([P, E, D]), ALU.mult)\
                    .then_inc(s["prod"], 1)
                dve.wait_ge(s["prod"], t + 2)
                dve.tensor_reduce(YS[:, bass.ds(t, 1), :].rearrange("p a f -> p (a f)"),
                                  prod[:].rearrange("p e f -> p f e"), AX.X, ALU.add).then_inc(s["picked"], 1)
                dve.wait_ge(s["ex"], t + 2)
                dve.reciprocal(gate[:, bass.ds(t, 1)], z[:]).then_inc(s["rz"], 1)
            dve.wait_ge(s["counts"], 1)
            n = 0
            dve.memset(before[0][:, 0:1, :], 0.0)
            dve.tensor_copy(before[0][:, 1:NT, :], psA[:, 0:(NT - 1) * E].rearrange("p (t e) -> p t e", e=E))\
                .then_inc(s["chain"], 1)
            for k in range(5):
                a, z_, step = before[k % 2], before[(k + 1) % 2], 1 << k
                dve.wait_ge(s["chain"], k + 1)
                dve.tensor_copy(z_[:, 0:step, :], a[:, 0:step, :])
                dve.tensor_tensor(z_[:, step:NT, :], a[:, step:NT, :], a[:, 0:NT - step, :], ALU.add)\
                    .then_inc(s["chain"], 1)
            dve.wait_ge(s["chain"], 6)
            dve.tensor_tensor(rank[:].rearrange("p t e -> p (t e)"), psC[:, 0:NT * E],
                              before[1][:].rearrange("p t e -> p (t e)"), ALU.add).then_inc(s["chain"], 1)
            dve.wait_ge(s["chain"], 7)
            dve.tensor_tensor(rank[:], rank[:], hot[:], ALU.mult).then_inc(s["chain"], 1)
            dve.wait_ge(s["chain"], 8)
            dve.tensor_reduce(mine[:], rank[:], AX.X, ALU.add).then_inc(s["chain"], 1)
            dve.wait_ge(s["chain"], 9)
            dve.tensor_scalar(mine[:], mine[:], float(CAP), None, ALU.is_le).then_inc(s["chain"], 1)
            dve.wait_ge(s["chain"], 10)
            dve.wait_ge(s["rz"], NT + 1)
            dve.tensor_tensor(keep[:], mine[:], gate[:], ALU.mult).then_inc(s["chain"], 1)
            dve.wait_ge(s["chain"], 11)
            dve.wait_ge(s["picked"], NT)
            dve.tensor_tensor(YS[:], YS[:], keep[:].rearrange("p (t a) -> p t a", a=1).broadcast_to([P, NT, D]),
                              ALU.mult).then_inc(s["chain"], 1)
            dve.wait_ge(s["chain"], 12)
            dve.tensor_tensor(Y[:], Y[:], YS[:], ALU.add).then_inc(s["kept"], 1)


def constants():
    bf16 = np.dtype("bfloat16")
    c = {}
    c["ident"] = np.eye(P, dtype=np.float32)
    c["identb"] = np.eye(P).astype(bf16)
    hd = np.arange(0, WD, 2, dtype=np.float32)
    inv_freq = (1.0 / np.float32(10000.0) ** (hd / np.float32(WD))).astype(np.float32)
    pos = np.arange(N, dtype=np.float32)
    freqs = (pos[:, None] * inv_freq[None, :]).astype(np.float32)
    freqs = np.concatenate([freqs, freqs], -1).astype(np.float64)
    base = (hd + 0.4 * WD) / (1.4 * WD)
    power = (pos - N // 2) / (WIN // 2)
    scale = base.astype(np.float64)[None, :] ** power.astype(np.float64)[:, None]
    scale = np.concatenate([scale, scale], -1)
    sign = np.where(np.arange(WD) < WD // 2, -1.0, 1.0)[None, :]
    rot = np.empty((N, 2, 2, WD), np.float64)
    rot[:, 0, 0], rot[:, 0, 1] = 8 * np.cos(freqs) * scale, 8 * np.sin(freqs) * scale * sign
    rot[:, 1, 0], rot[:, 1, 1] = np.cos(freqs) / scale, np.sin(freqs) / scale * sign
    c["rot"] = rot.reshape(TB, P, 2, 2, WD).transpose(1, 0, 2, 3, 4).astype(np.float32)
    key = np.concatenate([np.arange(P), np.arange(-WIN, 0)])
    back = np.arange(P)[:, None] - key[None, :]
    m = np.where((back >= 0) & (back <= WIN), 0.0, NEG)
    m = np.repeat(m[:, None, None, :], TB, 1).repeat(2, 2)
    m[:, 0, :, P:] = NEG
    c["wmask"] = m.astype(bf16)
    f = np.ones((P, TB), np.float32)
    f[:, TB - 1] = 0.0
    c["flag"] = f
    off = np.arange(3 * P)[None, :] - P - np.arange(P)[:, None]
    c["band"] = np.where(np.abs(off) <= P, 0.0, NEG).astype(np.float32)
    c["first"] = np.tile(np.arange(E, 0, -1, dtype=np.float32), (P, 1))
    c["upper"] = np.triu(np.ones((P, P), np.float32))
    c["ones"] = np.ones((P, P), np.float32)
    d = (N - 1 - np.arange(2 * N)).astype(np.float32)
    c["rel"] = (np.sign(d) * np.log1p(np.abs(d))).astype(np.float32)[None, :]
    return c

def layout(inputs):
    a = {k: np.asarray(v) for k, v in inputs.items()}
    w = {"x": a["L0_attn_x"]}
    pre = "L1_ffn_"
    for name in ("Wo", "W1", "W2", "b1", "b2", "ln_g", "ln_b", "q_scale", "k_scale"):
        w[name] = a[pre + name]
    w["Wqkv"] = a[pre + "Wqkv"].reshape(DEPTH, D, 3, NG, GW).transpose(0, 1, 3, 2, 4).reshape(DEPTH, D, NG, 3 * GW)
    pre = "L0_attn_"
    for n in "qkv":
        w["A" + "w" + n] = a[pre + "W" + n].T
    w["Awo"], w["Aws"] = a[pre + "Wo"].T, a[pre + "Ws"].T
    w["Abq"], w["Abk"], w["Abs"] = (a[pre + n].reshape(-1, 1) for n in ("bq", "bk", "bs"))
    w["Abv"], w["Abo"] = a[pre + "bv"].reshape(1, -1), a[pre + "bo"].reshape(1, -1)
    pre = "L1_attn_"
    for j, n in enumerate("qkv"):
        w["Cw" + n] = a[pre + "w_qkv"][:, j * D:(j + 1) * D]
        w["Cb" + n] = a[pre + "b_qkv"][j * D:(j + 1) * D].reshape((1, -1) if n == "v" else (-1, 1))
    w["Cwo"], w["Cbo"] = a[pre + "w_out"], a[pre + "b_out"].reshape(1, -1)
    w["rpe_w1"], w["rpe_b1"] = a[pre + "w1_rpe"].reshape(-1, 1), a[pre + "b1_rpe"].reshape(-1, 1)
    w["rpe_w2"], w["rpe_b2"] = a[pre + "w2_rpe"], a[pre + "b2_rpe"].reshape(-1, 1)
    pre = "L0_ffn_"
    w["m_win"], w["m_bin"] = a[pre + "in_proj_w"].T, a[pre + "in_proj_b"].reshape(1, -1)
    w["m_wout"], w["m_bout"] = a[pre + "out_proj_w"].T, a[pre + "out_proj_b"].reshape(1, -1)
    for n in ("ln1_g", "ln1_b", "ln2_g", "ln2_b"):
        w[n] = a[pre + n].reshape(1, -1)
    w["e_w1T"] = a[pre + "w1"].reshape(E, D, FF // P, P).transpose(3, 0, 2, 1).reshape(P, -1, D)
    w["e_w2"] = a[pre + "w2"].reshape(E, FF // P, P, D).transpose(2, 0, 1, 3).reshape(P, -1, D)
    w["e_b1"] = a[pre + "b1"].reshape(E * (FF // P), P).T
    w["e_b2"], w["e_wg"] = a[pre + "b2"].reshape(1, -1), a[pre + "wg"]
    w.update(constants())
    return {k: np.ascontiguousarray(v) for k, v in w.items()}


def build(nc, w, out):
    with ExitStack() as ctx:
        X = ctx.enter_context(nc.sbuf_tensor("X", [P, NT, D], F32))
        XN = ctx.enter_context(nc.sbuf_tensor("XN", [P, NT, D], F32))
        ident = ctx.enter_context(nc.sbuf_tensor("ident", [P, P], F32))
        qk_parts = nc.dram_tensor("qk_parts", (SP3, 2, P, B * N), BF16, kind="Internal").ap()
        scores = nc.dram_tensor("scores", (H, B * N), F32, kind="Internal").ap()
        topmask = nc.dram_tensor("topmask", (B * H, N), BF16, kind="Internal").ap()
        bias = nc.dram_tensor("bias", (H, 2 * N), F32, kind="Internal").ap()
        load_and_normalize(nc, w["x"], w["ident"], X, XN, ident)
        with ExitStack() as inner:
            V = inner.enter_context(nc.sbuf_tensor("V", [P, NT, D], F32))
            O = inner.enter_context(nc.sbuf_tensor("O", [P, NT, D], F32))
            project_heads(nc, XN, ident, V, w, "A", qk_parts, scores, False)
            select_keys(nc, scores, topmask)
            attend(nc, V, ident, O, qk_parts, "A", topmask=topmask, w=w)
            project_out(nc, O, X, ident, w, "A", False)
            cross_attention(nc, XN, V, ident, w)
            layer_norm(nc, V, V, "ln1_")
            scale_shift(nc, V, w, "ln1_g", "ln1_b")
            experts(nc, V, O, ident, w)
            layer_norm(nc, V, V, "ln2_")
            scale_shift(nc, V, w, "ln2_g", "ln2_b", X)
            layer_norm(nc, X, XN, "ln3_")
            relative_bias(nc, w, bias)
            project_heads(nc, XN, ident, V, w, "C", qk_parts, None, True)
            attend(nc, V, ident, O, qk_parts, "C", bias=bias)
            project_out(nc, O, X, ident, w, "C", True)
        windowed_layers(nc, XN, ident, w)
        add_into(nc, X, XN)
        stored = ctx.enter_context(nc.semaphore("stored"))
        block = ctx.enter_context(nc.Block())

        @block.sync
        def _(sp):
            sp.dma_start(tokens(out), X[:]).then_inc(stored, 16)
            sp.wait_ge(stored, 16)


def kernel(**inputs):
    import concourse.bacc as _bacc
    from concourse import mybir as _mybir
    from concourse.bass_utils import run_bass_kernel_spmd as _run
    nc = _bacc.Bacc("TRN2", target_bir_lowering=False, num_devices=1)
    arrays = layout(inputs)
    w = {k: nc.dram_tensor(k + "_dram", v.shape, _mybir.dt.from_np(v.dtype), kind="ExternalInput").ap()
         for k, v in arrays.items()}
    o = nc.dram_tensor("out", (B, N, D), F32, kind="ExternalOutput").ap()
    build(nc, w, o)
    r = _run(nc, [{k + "_dram": v for k, v in arrays.items()}], core_ids=[0])
    return r.results[0]["out"]
```

```python
from contextlib import ExitStack

import numpy as np

import concourse.bass as bass
from concourse import mybir

F32 = mybir.dt.float32
BF16 = mybir.dt.bfloat16
ACT = mybir.ActivationFunctionType
ALU = mybir.AluOpType
AX = mybir.AxisListType

P = 128
B, N, D = 4, 1024, 128
NT = B * N // P
TB = N // P
NEG = -1.0e30
EPS = 1e-5

DEPTH, WH, WD, WIN = 6, 16, 64, 32
INNER = WH * WD
GH = 4
NG = WH // GH
GW = GH * WD
KW = P + WIN
FI = int(D * 4 * 2 / 3)
FC = [(c, min(P, FI - c)) for c in range(0, FI, P)]


class Memory:

    def __init__(self, nc, ctx, prefix):
        self.nc, self.ctx, self.prefix, self.sems = nc, ctx, prefix, []
        ctx.callback(self.close)

    def sb(self, name, shape, dt=F32):
        return self.ctx.enter_context(self.nc.sbuf_tensor(self.prefix + name, shape, dt))

    def ps(self, name, shape, dt=F32):
        return self.ctx.enter_context(self.nc.psum_tensor(self.prefix + name, shape, dt))

    def sem(self, name):
        self.sems.append(self.nc.alloc_semaphore(self.prefix + name))
        return self.sems[-1]

    def close(self):
        self.nc.clear_and_free_semaphores(self.sems)
        self.nc.all_engine_barrier()


def wait_apart(eng, sem, value, passed):
    eng.wait_ge(sem, value)
    eng.sem_inc(passed, 1)


def tokens(ap):
    return ap.rearrange("b (t p) f -> p (b t) f", p=P)


def load_and_normalize(nc, x_dram, ident_dram, X, XN, ident):
    with ExitStack() as ctx:
        m = Memory(nc, ctx, "ln_")
        loaded, normed = m.sem("loaded"), m.sem("normed")
        block = ctx.enter_context(nc.Block())

        @block.sync
        def _(sp):
            sp.dma_start(X[:], tokens(x_dram)).then_inc(loaded, 16)
            sp.dma_start(ident[:], ident_dram).then_inc(loaded, 16)
            sp.wait_ge(loaded, 32)

    layer_norm(nc, X, XN, "ln0_")


def layer_norm(nc, X, XN, prefix):
    with ExitStack() as ctx:
        m = Memory(nc, ctx, prefix)
        stats, mv1, mv = m.sb("stats", [P, 6]), m.sb("mv1", [P, 2]), m.sb("mv", [P, NT, 2])
        rstd, var, half = m.sb("rstd", [P, NT]), m.sb("var", [P, NT]), m.sb("half", [P, NT])
        s_passed, s_stats, s_mv1, s_mv, s_const, s_var, s_rstd = (m.sem(n) for n in ("passed", "stats", "mv1", "mv", "const", "var", "rstd"))
        block = ctx.enter_context(nc.Block())

        @block.vector
        def _(dve):
            with dve.Fori(0, NT) as t:
                dve.bn_stats(stats[:], X[:, bass.ds(t, 1), :].rearrange("p a f -> p (a f)")).then_inc(s_stats, 1)
                wait_apart(dve, s_stats, t + 1, s_passed)
                dve.bn_aggr(mv1[:], stats[:]).then_inc(s_mv1, 1)
                dve.wait_ge(s_mv1, t + 1)
                dve.tensor_copy(mv[:, bass.ds(t, 1), :].rearrange("p a s -> p (a s)"), mv1[:]).then_inc(s_mv, 1)
            dve.wait_ge(s_rstd, 1)
            dve.wait_ge(s_mv, NT)
            with dve.Fori(0, NT) as t:
                dve.tensor_scalar(XN[:, bass.ds(t, 1), :].rearrange("p a f -> p (a f)"),
                                  X[:, bass.ds(t, 1), :].rearrange("p a f -> p (a f)"),
                                  mv[:, bass.ds(t, 1), 0:1].rearrange("p a s -> p (a s)"),
                                  rstd[:, bass.ds(t, 1)], ALU.subtract, ALU.mult)

        @block.gpsimd
        def _(pool):
            pool.memset(half[:], -0.5).then_inc(s_const, 1)
            pool.wait_ge(s_mv, NT)
            pool.tensor_scalar(var[:], mv[:, :, 1], EPS, None, ALU.add).then_inc(s_var, 1)
            pool.wait_ge(s_var, 1)
            pool.wait_ge(s_const, 1)
            pool.tensor_tensor(rstd[:], var[:], half[:], ALU.pow).then_inc(s_rstd, 1)


def add_into(nc, X, Y):
    with ExitStack() as ctx:
        block = ctx.enter_context(nc.Block())

        @block.vector
        def _(dve):
            dve.tensor_tensor(X[:], X[:], Y[:], ALU.add)


def windowed_layers(nc, XF, ident, w):
    with ExitStack() as ctx:
        m = Memory(nc, ctx, "w_")
        wqkv = m.sb("wqkv", [P, NG, 3 * GW])
        wo = m.sb("wo", [P, INNER // P, D])
        w1 = m.sb("w1", [P, 2 * FI])
        w2 = m.sb("w2", [P, len(FC), D])
        b1 = m.sb("b1", [P, 2, len(FC)])
        b2 = m.sb("b2", [1, D])
        lng, lnb = m.sb("lng", [P, 1]), m.sb("lnb", [P, 1])
        scales = m.sb("scales", [P, 2, 2, WD])
        rot0 = m.sb("rot0", [P, TB, 2, 2, WD])
        rot = m.sb("rot", [P, TB, 2, 2, WD])
        masks = m.sb("masks", [P, TB + 2, 2, KW], BF16)
        identb = m.sb("identb", [P, P], BF16)
        flag = m.sb("flag", [P, TB + 2])
        ones = m.sb("ones", [1, P])
        half = m.sb("half", [P, 2 * GH])
        xcur = m.sb("xcur", [P, D])
        xnT, xsT = m.sb("xnT", [P, P]), m.sb("xsT", [P, P])
        carryA, carryF = m.sb("carryA", [P, 1]), m.sb("carryF", [P, 1])
        sq = m.sb("sq", [P, 2, GH, WD])
        ss = m.sb("ss", [P, 2 * GH])
        ssm = m.sb("ssm", [P, 2 * GH])
        rn = m.sb("rn", [P, 2, 2 * GH])
        tc = m.sb("tc", [P, 2, GH, WD])
        tsn = m.sb("tsn", [P, 2, GH, WD])
        tadd = m.sb("tadd", [P, 2, GH, WD])
        qk = m.sb("qk", [P, 2, 2 * GH * WD])
        vcur = m.sb("vcur", [P, INNER])
        vprev = m.sb("vprev", [P, INNER])
        qT = m.sb("qT", [P, 2, P])
        kT = m.sb("kT", [P, NG, 2, KW])
        nmax = m.sb("nmax", [P, 2, GH])
        zsum = m.sb("zsum", [P, 2, GH])
        rz = m.sb("rz", [P, GH])
        pr = m.sb("pr", [P, 2, GH, KW])
        prT = m.sb("prT", [P, GH, P])
        prH = m.sb("prH", [P, GH, WIN])
        o = m.sb("o", [P, GW])
        oT = m.sb("oT", [P, INNER // P, P])
        x1 = m.sb("x1", [P, D])
        fsT = m.sb("fsT", [P, P])
        st6, mv = m.sb("st6", [P, 6]), m.sb("mv", [P, 2])
        vr, rstd = m.sb("vr", [P, 1]), m.sb("rstd", [P, 1])
        fn, fnT = m.sb("fn", [P, D]), m.sb("fnT", [P, P])
        gl, hT = m.sb("gl", [P, len(FC), P]), m.sb("hT", [P, len(FC), P])

        psQK = m.ps("psQK", [P, 512])
        psVb = m.ps("psV", [P, 512])
        psOb = m.ps("psO", [P, 512])
        psT = m.ps("psT", [P, 512])
        psS = m.ps("psS", [P, 2, 512])
        psP = m.ps("psP", [P, 512])
        psX = m.ps("psX", [P, 512])
        psV, psO = psVb[:, 0:GW], psOb[:, 0:GW]
        psHalo, psOT = psT[0:WIN, 0:GH * WIN], psOb[:, GW:2 * GW]

        names = """const weights layer_done tables x_full xT xnT_hi xnT_full carryA xsT_sb
            qk_full v_full squares norms qk_free rot_c rot_s sums rinv_a rinv qk_added qk_rot v_sb
            qkT qkT_sb scores maxes probs prT_ps prT_sb prH_sb pv rz o_sb oT_ps oT_sb vprev kprev
            y x1_full f_xT fsT_hi fsT_full carryF f_tok f_stats f_mv f_var f_rstd fn fnT_ps fnT_sb
            gates gelu hidden y2 x2_full passed_pe passed_dve passed_pool""".split()
        s = {n: m.sem(n) for n in names}
        block = ctx.enter_context(nc.Block())

        NW = 20

        @block.sync
        def _(sp):
            sp.dma_start(rot0[:], w["rot"]).then_inc(s["const"], 16)
            sp.dma_start(masks[:], w["wmask"]).then_inc(s["const"], 16)
            sp.dma_start(identb[:], w["identb"]).then_inc(s["const"], 16)
            sp.dma_start(flag[:], w["flag"]).then_inc(s["const"], 16)
            with sp.Fori(0, DEPTH) as l:
                sp.wait_ge(s["layer_done"], l + 1)
                one = lambda name: w[name][bass.ds(l, 1)]
                sp.dma_start(wqkv[:], one("Wqkv").rearrange("a p g c -> p (a g) c")).then_inc(s["weights"], 16)
                sp.dma_start(wo[:], one("Wo").rearrange("a (c p) d -> p (a c) d", p=P)).then_inc(s["weights"], 16)
                sp.dma_start(w1[:], one("W1").rearrange("a p f -> p (a f)")).then_inc(s["weights"], 16)
                for c, (f0, fn_) in enumerate(FC):
                    sp.dma_start(w2[0:fn_, c, :], one("W2")[:, f0:f0 + fn_, :].rearrange("a p d -> p (a d)"))\
                        .then_inc(s["weights"], 16)
                    sp.dma_start(b1[0:fn_, :, c], one("b1").rearrange("a (j f) -> f (a j)", j=2)[f0:f0 + fn_],
                                 allow_slow_non_contiguous=True).then_inc(s["weights"], 16)
                sp.dma_start(b2[:], one("b2")).then_inc(s["weights"], 16)
                sp.dma_start(lng[:], one("ln_g").rearrange("a p -> p a"), allow_slow_non_contiguous=True)\
                    .then_inc(s["weights"], 16)
                sp.dma_start(lnb[:], one("ln_b").rearrange("a p -> p a"), allow_slow_non_contiguous=True)\
                    .then_inc(s["weights"], 16)
                for j, name in enumerate(("q_scale", "k_scale")):
                    for k in range(2):
                        for hh in range(2):
                            src = (hh + k) % 2
                            sp.dma_start(scales[:, j, k, hh * 32:hh * 32 + 32],
                                         one(name)[:, src * 32:src * 32 + 32].broadcast_to([P, 32]))\
                                .then_inc(s["weights"], 16)


        def over_tiles(eng, l, tile):
            tile(l * NT, 0, True, False)
            with eng.Fori(1, NT) as t:
                tile(l * NT + t, t, True, True)
            tile(l * NT + NT, NT, False, True)

        def before(k, cur, prev):
            return (cur if k >= 1 else prev), (cur if k >= 2 else prev)

        def position(t):
            return t % TB

        @block.tensor
        def _(pe):
            pe.sem_inc(s["scores"], 1)
            pe.sem_inc(s["prT_ps"], 2)
            pe.sem_inc(s["pv"], 1)
            pe.sem_inc(s["oT_ps"], 1)
            pe.sem_inc(s["xT"], 1)
            pe.sem_inc(s["qkT"], 2)
            pe.wait_ge(s["const"], 64)

            def features_of_x(T):
                pe.wait_ge(s["x_full"], T + 1)
                pe.transpose(psX[:, 0:P], xcur[:], ident[:]).then_inc(s["xT"], 1)

            def project(n, u):
                pe.wait_ge(s["qk_free"], 2 * n + 2)
                pe.matmul(psQK[:], xsT[:], wqkv[:, u, 0:2 * GW], start=True, stop=True).then_inc(s["qk_full"], 1)
                pe.wait_ge(s["v_sb"], n + 1)
                pe.matmul(psV, xsT[:], wqkv[:, u, 2 * GW:3 * GW], start=True, stop=True).then_inc(s["v_full"], 1)

            def turn_qk(n, u):
                pe.wait_ge(s["qk_rot"], n + 1)
                pe.wait_ge(s["qkT_sb"], n + 1)
                for j in range(4):
                    mm = pe.transpose(psT[:, j * P:(j + 1) * P], qk[:, u % 2, j * P:(j + 1) * P], ident[:])
                mm.then_inc(s["qkT"], 1)

            def score(n, u, at):
                pe.wait_ge(s["qkT_sb"], n + 2)
                pe.wait_ge(s["probs"], n + 1)
                pe.wait_ge(s["kprev"], n + 1)
                for c in range(2):
                    pe.matmul(psS[:, c, 0:2 * KW], identb[:],
                              masks[:, bass.ds(at, 1), :, :].rearrange("p a h k -> p (a h k)"),
                              start=True, stop=False, skip_group_check=True)
                for a in range(2):
                    for c in range(2):
                        r = slice(c * WD, (c + 1) * WD)
                        mm = pe.matmul(psS[:, c, a * KW:(a + 1) * KW], qT[r, a, :], kT[r, u, a, :],
                                       start=False, stop=(a == 1), skip_group_check=True)
                mm.then_inc(s["scores"], 1)

            def turn_p(n, u, last_turned):
                pe.wait_ge(s["probs"], n + 2)
                pe.wait_ge(s["prT_sb"], n + 1)
                for h in range(GH):
                    pe.transpose(psP[:, h * P:(h + 1) * P], pr[:, u % 2, h, 0:P], ident[:])
                wait_apart(pe, s["qkT_sb"], last_turned + 2, s["passed_pe"])
                for h in range(GH):
                    mm = pe.transpose(psHalo[:, h * WIN:(h + 1) * WIN], pr[0:WIN, u % 2, h, P:KW],
                                      ident[0:WIN, 0:WIN])
                mm.then_inc(s["prT_ps"], 1)

            def weigh(n, u):
                pe.wait_ge(s["prT_sb"], n + 2)
                pe.wait_ge(s["prH_sb"], n + 2)
                pe.wait_ge(s["o_sb"], n + 1)
                pe.wait_ge(s["oT_sb"], n + 1)
                pe.wait_ge(s["vprev"], n + 1)
                pe.wait_ge(s["v_sb"], n + 2)
                for h in range(GH):
                    c = u * GW + h * WD
                    pe.matmul(psO[:, h * WD:(h + 1) * WD], prT[:, h, :], vcur[:, c:c + WD],
                              start=True, stop=False, skip_group_check=True)
                    mm = pe.matmul(psO[0:WIN, h * WD:(h + 1) * WD], prH[P - WIN:P, h, :],
                                   vprev[P - WIN:P, c:c + WD], start=False, stop=True, skip_group_check=True)
                mm.then_inc(s["pv"], 1)

            def turn_o(n, u):
                pe.wait_ge(s["o_sb"], n + 2)
                for a in range(2):
                    mm = pe.transpose(psOT[:, a * P:(a + 1) * P], o[:, a * P:(a + 1) * P], ident[:])
                mm.then_inc(s["oT_ps"], 1)

            def ffn(F, part):
                if part == "y":
                    pe.wait_ge(s["oT_sb"], F * NG + NG + 1)
                    for c in range(INNER // P):
                        mm = pe.matmul(psX[:, P:2 * P], oT[:, c, :], wo[:, c, :], start=(c == 0),
                                       stop=(c == INNER // P - 1))
                    mm.then_inc(s["y"], 1)
                elif part == "turn":
                    pe.wait_ge(s["x1_full"], F + 1)
                    pe.transpose(psX[:, 0:P], x1[:], ident[:]).then_inc(s["f_xT"], 1)
                elif part == "back":
                    pe.wait_ge(s["fsT_hi"], F + 1)
                    pe.wait_ge(s["carryF"], F + 2)
                    pe.transpose(psX[:, P:2 * P], fsT[:], ident[:]).then_inc(s["f_tok"], 1)
                elif part == "normed":
                    pe.wait_ge(s["fn"], F + 1)
                    pe.transpose(psX[:, 0:P], fn[:], ident[:]).then_inc(s["fnT_ps"], 1)
                elif part == "gates":
                    pe.wait_ge(s["fnT_sb"], F + 1)
                    for j, bank in ((1, psVb), (0, psP)):
                        for c, (f0, fw) in enumerate(FC):
                            mm = pe.matmul(bank[0:fw, c * P:(c + 1) * P], w1[:, j * FI + f0:j * FI + f0 + fw],
                                           fnT[:], start=True, stop=True)
                        mm.then_inc(s["gates"], 1)
                elif part == "y2":
                    pe.wait_ge(s["hidden"], F + 1)
                    for c, (f0, fw) in enumerate(FC):
                        pe.matmul(psX[:, P:2 * P], hT[0:fw, c, :], w2[0:fw, c, :], start=(c == 0), stop=False)
                    pe.matmul(psX[:, P:2 * P], ones[:], b2[:], start=False, stop=True).then_inc(s["y2"], 1)

            features_of_x(0)
            with pe.Fori(0, DEPTH) as l:
                wait_apart(pe, s["weights"], (l + 1) * (NW * 16), s["passed_pe"])

                def tile(T, t, cur, prev):
                    i = position(t)
                    for k in range(NG):
                        n, (one, two) = T * NG + k, before(k, cur, prev)
                        if k == 0 and cur:
                            pe.wait_ge(s["xsT_sb"], T + 1)
                        if cur:
                            project(n, k)
                        if k == 1 and cur:
                            pe.wait_ge(s["x2_full"], T + NT - 1 if prev else T + NT)
                            pe.wait_ge(s["carryA"], T + 2)
                            features_of_x(T + 1)
                        if k == 2 and prev:
                            if cur:
                                pe.wait_ge(s["xnT_hi"], T + 2)
                                pe.wait_ge(s["carryA"], T + 3)
                            ffn(T - 1, "y")
                        if k == 3 and prev:
                            ffn(T - 1, "normed")
                        if one:
                            turn_qk(n - 1, (k - 1) % NG)
                        if two:
                            turn_p(n - 2, (k - 2) % NG, n - 1 if one else n - 2)
                        if k == 2 and prev:
                            ffn(T - 1, "turn")
                        if k == 3 and prev:
                            pe.wait_ge(s["v_sb"], n + 2 if cur else T * NG + 1)
                            pe.wait_ge(s["prT_sb"], n if cur else T * NG + 1)
                            ffn(T - 1, "gates")
                        if one:
                            score(n - 1, (k - 1) % NG, i + (1 if k else 0))
                        if two:
                            weigh(n - 2, (k - 2) % NG)
                        if k == 2 and prev:
                            ffn(T - 1, "back")
                        if two:
                            turn_o(n - 2, (k - 2) % NG)
                        if k == 3 and prev:
                            ffn(T - 1, "y2")

                over_tiles(pe, l, tile)

        def shifted(act, dst, src, hi):
            act.activation(dst[0:64, :], src[0:64, 0:P], ACT.Copy)
            act.activation(dst[64:P, 1:P], src[64:P, 0:P - 1], ACT.Copy).then_inc(hi, 1)

        @block.scalar
        def _(act):
            act.sem_inc(s["squares"], 1)
            act.sem_inc(s["v_sb"], 1)
            act.sem_inc(s["qkT_sb"], 1)
            act.sem_inc(s["probs"], 1)
            act.sem_inc(s["prT_sb"], 1)
            act.sem_inc(s["oT_sb"], 1)
            def evacuate_qkv(n, u):
                act.wait_ge(s["qk_full"], n + 1)
                act.wait_ge(s["norms"], n + 1)
                act.activation(sq[:].rearrange("p j h d -> p (j h d)"), psQK[:], ACT.Square)\
                    .then_inc(s["squares"], 1)
                act.wait_ge(s["v_full"], n + 1)
                act.wait_ge(s["vprev"], n + 1)
                act.activation(vcur[:, u * GW:(u + 1) * GW], psV, ACT.Copy).then_inc(s["v_sb"], 1)

            def evacuate_T(n, u):
                act.wait_ge(s["qkT"], n + 3)
                act.wait_ge(s["kprev"], n + 1)
                act.wait_ge(s["scores"], n + 1)
                act.activation(qT[:].rearrange("p a c -> p (a c)"), psT[:, 0:2 * P], ACT.Copy)
                act.activation(kT[:, u, :, 0:P], psT[:, 2 * P:4 * P].rearrange("p (a c) -> p a c", a=2),
                               ACT.Copy).then_inc(s["qkT_sb"], 1)

            def exponentials(n, u):
                act.wait_ge(s["maxes"], n + 1)
                act.wait_ge(s["prT_ps"], n + 1)
                act.wait_ge(s["rz"], n + 1)
                for h in range(GH):
                    e = act.activation(pr[:, u % 2, h, :], psS[:, h % 2, (h // 2) * KW:(h // 2 + 1) * KW],
                                       ACT.Exp, bias=nmax[:, u % 2, h:h + 1],
                                       accum_out=zsum[:, u % 2, h:h + 1])
                e.then_inc(s["probs"], 1)

            def evacuate_P(n, u):
                act.wait_ge(s["prT_ps"], n + 3)
                act.wait_ge(s["pv"], n + 1)
                act.activation(prT[:].rearrange("p h c -> p (h c)"), psP[:], ACT.Copy)\
                    .then_inc(s["prT_sb"], 1)

            def evacuate_oT(n, u):
                act.wait_ge(s["oT_ps"], n + 2)
                act.activation(oT[:, 2 * u:2 * u + 2, :].rearrange("p a c -> p (a c)"), psOT, ACT.Copy)\
                    .then_inc(s["oT_sb"], 1)

            def gates(F):
                act.wait_ge(s["gates"], 2 * F + 1)
                for c, (f0, fw) in enumerate(FC):
                    g = act.activation(gl[0:fw, c, :], psVb[0:fw, c * P:(c + 1) * P], ACT.Gelu,
                                       bias=b1[0:fw, 1, c:c + 1])
                g.then_inc(s["gelu"], 1)

            def use_next_x(T):
                act.wait_ge(s["xnT_full"], T + 1)
                act.activation(xsT[:], xnT[:], ACT.Copy).then_inc(s["xsT_sb"], 1)

            act.wait_ge(s["xT"], 2)
            shifted(act, xnT, psX, s["xnT_hi"])
            use_next_x(0)
            with act.Fori(0, DEPTH) as l:
                act.wait_ge(s["weights"], (l + 1) * (NW * 16))

                def tile(T, t, cur, prev):
                    for k in range(NG):
                        n, (one, two) = T * NG + k, before(k, cur, prev)
                        if cur:
                            evacuate_qkv(n, k)
                        if k == 1 and cur:
                            act.wait_ge(s["xT"], T + 3)
                            shifted(act, xnT, psX, s["xnT_hi"])
                        if k == 3 and cur:
                            use_next_x(T + 1)
                        if one:
                            evacuate_T(n - 1, (k - 1) % NG)
                        if two:
                            evacuate_P(n - 2, (k - 2) % NG)
                        if k == 2 and prev:
                            act.wait_ge(s["f_xT"], T)
                            shifted(act, fsT, psX, s["fsT_hi"])
                        if k == 3 and prev:
                            gates(T - 1)
                        if one:
                            exponentials(n - 1, (k - 1) % NG)
                        if two:
                            evacuate_oT(n - 2, (k - 2) % NG)

                over_tiles(act, l, tile)

        def carry_over(dve, dst, carry, psum, i, mine, chain, n):
            dve.tensor_copy(dst[64:P, 0:1], carry[64:P, :]).then_inc(mine, 1)
            dve.wait_ge(mine, n)
            dve.tensor_tensor(carry[64:P, :], psum[64:P, P - 1:P], flag[64:P, bass.ds(i, 1)], ALU.mult)\
                .then_inc(chain, 1)

        @block.vector
        def _(dve):
            dve.memset(carryA[:], 0.0).then_inc(s["carryA"], 1)
            dve.memset(carryF[:], 0.0).then_inc(s["carryF"], 1)
            dve.memset(ones[:], 1.0)
            dve.memset(half[:], -0.5)
            dve.sem_inc(s["norms"], 1)
            dve.sem_inc(s["qk_free"], 2)
            dve.sem_inc(s["prH_sb"], 1)
            dve.sem_inc(s["o_sb"], 1)
            dve.sem_inc(s["rz"], 2)
            dve.wait_ge(s["const"], 64)
            def rotate(n, u, i):
                qkv = psQK[:].rearrange("p (j h d) -> p j h d", j=2, h=GH)
                dve.wait_ge(s["squares"], n + 2)
                dve.wait_ge(s["qk_added"], n + 1)
                for j in range(2):
                    dve.tensor_tensor(
                        tc[:, j], qkv[:, j],
                        rot[:, bass.ds(i, 1), j, 0, :].broadcast_to([P, GH, WD]), ALU.mult)
                    for hh in range(2):
                        a = slice(hh * 32, hh * 32 + 32)
                        z = slice(32 - hh * 32, 64 - hh * 32)
                        r = dve.tensor_tensor(
                            tsn[:, j, :, a], qkv[:, j, :, z],
                            rot[:, bass.ds(i, 1), j, 1, a].broadcast_to([P, GH, 32]), ALU.mult)
                    r.then_inc(s["qk_free"], 1)
                dve.wait_ge(s["rinv_a"], n + 1)
                dve.tensor_reduce(ss[:], sq[:].rearrange("p j h d -> p (j h) d"), AX.X, ALU.add)\
                    .then_inc(s["norms"], 1)

            def maxima(n, u):
                dve.wait_ge(s["scores"], n + 2)
                dve.wait_ge(s["probs"], n + 1)
                dve.tensor_reduce(nmax[:, u % 2, :].rearrange("p (a c) -> p c a", a=2),
                                  psS[:, :, 0:2 * KW].rearrange("p c (a k) -> p c a k", a=2),
                                  AX.X, ALU.max, negate=True).then_inc(s["maxes"], 1)

            def halo(n, u):
                dve.wait_ge(s["prT_ps"], n + 3)
                dve.wait_ge(s["pv"], n + 1)
                dve.tensor_copy(prH[P - WIN:P].rearrange("p h c -> p (h c)"), psHalo)\
                    .then_inc(s["prH_sb"], 1)

            def normalize(n, u):
                dve.wait_ge(s["probs"], n + 2)
                dve.reciprocal(rz[:], zsum[:, u % 2, :]).then_inc(s["rz"], 1)
                dve.wait_ge(s["rz"], n + 3)
                dve.wait_ge(s["pv"], n + 2)
                dve.wait_ge(s["oT_ps"], n + 1)
                dve.tensor_tensor(o[:].rearrange("p (h d) -> p h d", h=GH),
                                  psO.rearrange("p (h d) -> p h d", h=GH),
                                  rz[:].rearrange("p (h a) -> p h a", a=1).broadcast_to([P, GH, WD]), ALU.mult).then_inc(s["o_sb"], 1)

            def ffn(F, t, part):
                row = XF[:, bass.ds(t - 1, 1), :].rearrange("p a f -> p (a f)")
                if part == "x1":
                    dve.wait_ge(s["y"], F + 1)
                    dve.tensor_tensor(x1[:], psX[:, P:2 * P], row, ALU.add).then_inc(s["x1_full"], 1)
                elif part == "carry":
                    dve.wait_ge(s["fsT_hi"], F + 1)
                    dve.wait_ge(s["carryF"], F + 1)
                    carry_over(dve, fsT, carryF, psX, position(t), s["fsT_full"], s["carryF"], F + 1)
                elif part == "stats":
                    dve.wait_ge(s["f_tok"], F + 1)
                    dve.bn_stats(st6[:], psX[:, P:2 * P]).then_inc(s["f_stats"], 1)
                    wait_apart(dve, s["f_stats"], F + 1, s["passed_dve"])
                    dve.bn_aggr(mv[:], st6[:]).then_inc(s["f_mv"], 1)
                elif part == "normed":
                    dve.wait_ge(s["f_mv"], F + 1)
                    dve.wait_ge(s["f_rstd"], F + 1)
                    dve.tensor_scalar(fn[:], psX[:, P:2 * P], mv[:, 0:1], rstd[:], ALU.subtract, ALU.mult)\
                        .then_inc(s["fn"], 1)
                elif part == "scaled":
                    dve.wait_ge(s["fnT_ps"], F + 1)
                    dve.tensor_scalar(fnT[:], psX[:, 0:P], lng[:], lnb[:], ALU.mult, ALU.add)\
                        .then_inc(s["fnT_sb"], 1)
                elif part == "hidden":
                    dve.wait_ge(s["gates"], 2 * F + 2)
                    dve.wait_ge(s["gelu"], F + 1)
                    for c, (f0, fw) in enumerate(FC):
                        h = dve.scalar_tensor_tensor(hT[0:fw, c, :], psP[0:fw, c * P:(c + 1) * P],
                                                     b1[0:fw, 0, c:c + 1], gl[0:fw, c, :], ALU.add, ALU.mult)
                    h.then_inc(s["hidden"], 1)
                elif part == "x2":
                    dve.wait_ge(s["y2"], F + 1)
                    dve.tensor_tensor(row, psX[:, P:2 * P], x1[:], ALU.add).then_inc(s["x2_full"], 1)

            def next_x(T, at):
                dve.wait_ge(s["xnT_hi"], T + 1)
                dve.wait_ge(s["carryA"], T + 1)
                carry_over(dve, xnT, carryA, psX, at, s["xnT_full"], s["carryA"], T + 1)

            next_x(0, 1)
            with dve.Fori(0, DEPTH) as l:
                dve.wait_ge(s["weights"], (l + 1) * (NW * 16))
                for j in range(2):
                    for k in range(2):
                        dve.tensor_tensor(rot[:, :, j, k, :], rot0[:, :, j, k, :],
                                          scales[:, j, k:k + 1, :].broadcast_to([P, TB, WD]), ALU.mult)\
                            .then_inc(s["tables"], 1)
                wait_apart(dve, s["tables"], 4 * l + 4, s["passed_dve"])

                def tile(T, t, cur, prev):
                    for k in range(NG):
                        n, (one, two) = T * NG + k, before(k, cur, prev)
                        if k == 3 and prev:
                            ffn(T - 1, t, "normed")
                        if cur:
                            rotate(n, k, position(t))
                        if k == 1 and cur:
                            next_x(T + 1, position(t) + 2)
                        if k == 2 and prev:
                            ffn(T - 1, t, "x1")
                        if k == 3 and prev:
                            ffn(T - 1, t, "scaled")
                        if two:
                            halo(n - 2, (k - 2) % NG)
                        if k == 2 and prev:
                            ffn(T - 1, t, "carry")
                        if k == 3 and prev:
                            ffn(T - 1, t, "hidden")
                        if one:
                            maxima(n - 1, (k - 1) % NG)
                        if two:
                            normalize(n - 2, (k - 2) % NG)
                        if k == 2 and prev:
                            ffn(T - 1, t, "stats")
                        if k == 3 and prev:
                            ffn(T - 1, t, "x2")

                over_tiles(dve, l, tile)

        @block.gpsimd
        def _(pool):
            pool.memset(kT[:], 0.0).then_inc(s["kprev"], 1)
            pool.memset(vprev[:], 0.0).then_inc(s["vprev"], 1)
            pool.wait_ge(s["kprev"], 1)
            pool.sem_inc(s["kprev"], NG - 1)
            pool.wait_ge(s["vprev"], 1)
            pool.sem_inc(s["vprev"], NG - 1)
            pool.sem_inc(s["qk_added"], 1)
            pool.sem_inc(s["rinv_a"], 1)
            pool.sem_inc(s["layer_done"], 1)
            pool.sem_inc(s["x2_full"], NT)

            def load_x(T, t):
                wait_apart(pool, s["x2_full"], T + 1, s["passed_pool"])
                wait_apart(pool, s["xT"], T + 1, s["passed_pool"])
                pool.tensor_copy(xcur[:], XF[:, bass.ds(t % NT, 1), :].rearrange("p a f -> p (a f)"))\
                    .then_inc(s["x_full"], 1)

            def scale_qk(n, u):
                wait_apart(pool, s["norms"], n + 2, s["passed_pool"])
                pool.tensor_scalar(ssm[:], ss[:], 1e-24, None, ALU.max).then_inc(s["rinv_a"], 1)
                pool.wait_ge(s["rinv_a"], n + 2)
                pool.tensor_tensor(rn[:, u % 2, :], ssm[:], half[:], ALU.pow).then_inc(s["rinv"], 1)
                pool.wait_ge(s["qk_free"], 2 * n + 4)
                pool.tensor_tensor(tadd[:], tc[:], tsn[:], ALU.add).then_inc(s["qk_added"], 1)
                pool.wait_ge(s["qk_added"], n + 2)
                pool.wait_ge(s["rinv"], n + 1)
                pool.wait_ge(s["qkT"], n + 1)
                pool.tensor_tensor(qk[:, u % 2, :].rearrange("p (g d) -> p g d", d=WD),
                                   tadd[:].rearrange("p j h d -> p (j h) d"),
                                   rn[:, u % 2, :].rearrange("p (g a) -> p g a", a=1).broadcast_to([P, 2 * GH, WD]),
                                   ALU.mult).then_inc(s["qk_rot"], 1)

            def keep_k(n, u, at):
                wait_apart(pool, s["scores"], n + 2, s["passed_pool"])
                pool.tensor_tensor(kT[:, u, :, P:KW], kT[:, u, :, P - WIN:P],
                                   flag[:, bass.ds(at, 1)].broadcast_to([P, 2 * WIN])
                                   .rearrange("p (a k) -> p a k", a=2), ALU.mult).then_inc(s["kprev"], 1)

            def keep_v(n, u):
                wait_apart(pool, s["pv"], n + 2, s["passed_pool"])
                pool.tensor_copy(vprev[:, u * GW:(u + 1) * GW], vcur[:, u * GW:(u + 1) * GW])\
                    .then_inc(s["vprev"], 1)

            load_x(0, 0)
            with pool.Fori(0, DEPTH) as l:

                def tile(T, t, cur, prev):
                    for k in range(NG):
                        n, (one, two) = T * NG + k, before(k, cur, prev)
                        if cur:
                            scale_qk(n, k)
                        if k == 0 and cur:
                            load_x(T + 1, t + 1)
                        if one:
                            keep_k(n - 1, (k - 1) % NG, position(t) + (1 if k else 0))
                        if two:
                            keep_v(n - 2, (k - 2) % NG)
                        if k == 2 and prev:
                            wait_apart(pool, s["f_mv"], T, s["passed_pool"])
                            pool.tensor_scalar(vr[:], mv[:, 1:2], EPS, None, ALU.add).then_inc(s["f_var"], 1)
                            pool.wait_ge(s["f_var"], T)
                            pool.tensor_tensor(rstd[:], vr[:], half[:, 0:1], ALU.pow).then_inc(s["f_rstd"], 1)

                over_tiles(pool, l, tile)
                wait_apart(pool, s["x2_full"], (l + 1) * NT + NT, s["passed_pool"])
                pool.sem_inc(s["layer_done"], 1)


H, HD = 16, 8
CH = 512
NC_ = B * N // CH
TC = CH // P
SP3 = 3
Q_PARTS = (0, 0, 0, 1, 1, 2)
K_PARTS = (0, 1, 2, 0, 1, 0)
KS = HD * len(Q_PARTS)
KEEP = N // 4
NGLOB = 64
BW = N + (TB - 1) * P


def flipped(tile, tiles):
    a = tile.rearrange("p (t c) -> p t c", c=P)[:, :, P - 1:P]
    return bass.AP(a.tensor, a.offset, [list(a.ap[0]), [P, tiles], [-1, P]])


def project_heads(nc, XN, ident, V, w, pre, qk_parts, scores, flip):
    with ExitStack() as ctx:
        m = Memory(nc, ctx, pre + "p_")
        wq, wk, wv = (m.sb(n, [P, D]) for n in ("wq", "wk", "wv"))
        bq, bqs, bk, bv = m.sb("bq", [P, 1]), m.sb("bqs", [P, 1]), m.sb("bk", [P, 1]), m.sb("bv", [P, D])
        xcur, xT = m.sb("xcur", [P, CH]), m.sb("xT", [P, CH])
        qk, rest = m.sb("qk", [P, 2, CH]), m.sb("rest", [P, 2, CH])
        parts = m.sb("parts", [P, SP3, 2, CH], BF16)
        psX, psQ, psK, psV, psS = (m.ps(n, [P, CH]) for n in ("psX", "psQ", "psK", "psV", "psS"))
        names = """weights bias x xT_ps xT q k v qk_sb high r1 mid low v_sb stored sc sc_sb sc_stored passed"""
        s = {n: m.sem(n) for n in names.split()}
        if scores is not None:
            ws, bs, sc = m.sb("ws", [P, H]), m.sb("bs", [H, 1]), m.sb("sc", [H, CH])
        block = ctx.enter_context(nc.Block())
        scale = 1.0 / float(np.sqrt(np.float32(HD)))
        NWT = 16 * (6 + (2 if scores is not None else 0))

        @block.sync
        def _(sp):
            for dst, name in ((wq, "wq"), (wk, "wk"), (wv, "wv"), (bq, "bq"), (bk, "bk")):
                sp.dma_start(dst[:], w[pre + name]).then_inc(s["weights"], 16)
            sp.dma_start(bv[:], w[pre + "bv"].broadcast_to([P, D])).then_inc(s["weights"], 16)
            if scores is not None:
                sp.dma_start(ws[:], w[pre + "ws"]).then_inc(s["weights"], 16)
                sp.dma_start(bs[:], w[pre + "bs"]).then_inc(s["weights"], 16)
            with sp.Fori(0, NC_) as c:
                sp.wait_ge(s["low"], c + 2)
                for part in range(SP3):
                    sp.dma_start(qk_parts[part, :, :, bass.ds(c * CH, CH)].rearrange("j p t -> p j t"),
                                 parts[:, part]).then_inc(s["stored"], 16)
                if scores is not None:
                    wait_apart(sp, s["sc_sb"], c + 1, s["passed"])
                    sp.dma_start(scores[:, bass.ds(c * CH, CH)], sc[:]).then_inc(s["sc_stored"], 16)
            sp.wait_ge(s["stored"], 48 * (NC_ + 1))
            if scores is not None:
                sp.wait_ge(s["sc_stored"], 16 * (NC_ + 1))

        @block.gpsimd
        def _(pool):
            pool.sem_inc(s["x"], 1)
            with pool.Fori(0, NC_) as c:
                pool.wait_ge(s["xT"], c + 1)
                pool.tensor_copy(xcur[:].rearrange("p (t f) -> p t f", t=TC), XN[:, bass.ds(c * TC, TC), :])\
                    .then_inc(s["x"], 1)

        @block.tensor
        def _(pe):
            pe.wait_ge(s["weights"], NWT)
            with pe.Fori(0, NC_) as c:
                pe.wait_ge(s["x"], c + 2)
                for j in range(TC):
                    mm = pe.transpose(psX[:, j * P:(j + 1) * P], xcur[:, j * P:(j + 1) * P], ident[:])
                mm.then_inc(s["xT_ps"], 1)
                pe.wait_ge(s["xT"], c + 2)
                pe.wait_ge(s["qk_sb"], c + 1)
                pe.matmul(psQ[:], wq[:], xT[:], start=True, stop=True).then_inc(s["q"], 1)
                pe.matmul(psK[:], wk[:], xT[:], start=True, stop=True).then_inc(s["k"], 1)
                if scores is not None:
                    pe.matmul(psS[0:H, :], ws[:], xT[:], start=True, stop=True).then_inc(s["sc"], 1)
                pe.wait_ge(s["v_sb"], c + 1)
                for j in range(TC):
                    mm = pe.matmul(psV[:, j * P:(j + 1) * P], xT[:, j * P:(j + 1) * P], wv[:], start=True, stop=True)
                mm.then_inc(s["v"], 1)

        @block.scalar
        def _(act):
            act.sem_inc(s["xT"], 1)
            act.sem_inc(s["qk_sb"], 1)
            act.wait_ge(s["weights"], NWT)
            act.activation(bqs[:], bq[:], ACT.Copy, scale=scale).then_inc(s["bias"], 1)
            act.wait_ge(s["bias"], 1)
            with act.Fori(0, NC_) as c:
                act.wait_ge(s["xT_ps"], c + 1)
                act.wait_ge(s["v"], c + 1)
                act.activation(xT[:], psX[:], ACT.Copy).then_inc(s["xT"], 1)
                act.wait_ge(s["q"], c + 1)
                act.wait_ge(s["low"], c + 1)
                if flip:
                    act.activation(flipped(qk[:, 0], TC), psQ[:].rearrange("p (t c) -> p t c", c=P), ACT.Identity,
                                   bias=bqs[:], scale=scale)
                else:
                    act.activation(qk[:, 0], psQ[:], ACT.Identity, bias=bqs[:], scale=scale)
                act.wait_ge(s["k"], c + 1)
                act.activation(qk[:, 1], psK[:], ACT.Identity, bias=bk[:]).then_inc(s["qk_sb"], 1)
                if scores is not None:
                    act.wait_ge(s["sc"], c + 1)
                    act.wait_ge(s["sc_stored"], 16 * c + 16)
                    act.activation(sc[:], psS[0:H, :], ACT.Identity, bias=bs[:]).then_inc(s["sc_sb"], 1)

        @block.vector
        def _(dve):
            dve.sem_inc(s["low"], 1)
            dve.sem_inc(s["v_sb"], 1)
            dve.sem_inc(s["v"], 1)
            dve.sem_inc(s["stored"], 48)
            dve.sem_inc(s["sc_stored"], 16)
            dve.wait_ge(s["weights"], NWT)
            with dve.Fori(0, NC_) as c:
                dve.wait_ge(s["qk_sb"], c + 2)
                dve.wait_ge(s["stored"], 48 * c + 48)
                dve.tensor_copy(parts[:, 0], qk[:]).then_inc(s["high"], 1)
                dve.wait_ge(s["high"], c + 1)
                dve.tensor_tensor(rest[:], qk[:], parts[:, 0], ALU.subtract).then_inc(s["r1"], 1)
                dve.wait_ge(s["r1"], c + 1)
                dve.tensor_copy(parts[:, 1], rest[:]).then_inc(s["mid"], 1)
                dve.wait_ge(s["mid"], c + 1)
                dve.tensor_tensor(parts[:, 2], rest[:], parts[:, 1], ALU.subtract).then_inc(s["low"], 1)
                dve.wait_ge(s["v"], c + 2)
                dve.tensor_tensor(V[:, bass.ds(c * TC, TC), :], psV[:].rearrange("p (t f) -> p t f", t=TC),
                                  bv[:].rearrange("p (a f) -> p a f", a=1).broadcast_to([P, TC, D]), ALU.add)\
                    .then_inc(s["v_sb"], 1)


def select_keys(nc, scores, topmask):
    with ExitStack() as ctx:
        m = Memory(nc, ctx, "top_")
        sc, work = m.sb("sc", [B * H, N]), m.sb("work", [B * H, N])
        best = m.sb("best", [B * H, 8])
        left, mask = m.sb("left", [B * H, N]), m.sb("mask", [B * H, N], BF16)
        loaded, s_best, s_work, s_left, s_mask, stored, passed = (
            m.sem(n) for n in ("loaded", "best", "work", "left", "mask", "stored", "passed"))
        block = ctx.enter_context(nc.Block())

        @block.sync
        def _(sp):
            for b in range(B):
                sp.dma_start(sc[b * H:(b + 1) * H, :], scores[:, b * N:(b + 1) * N]).then_inc(loaded, 16)
            sp.wait_ge(s_mask, 1)
            sp.dma_start(topmask, mask[:]).then_inc(stored, 16)
            sp.wait_ge(stored, 16)

        @block.vector
        def _(dve):
            dve.wait_ge(loaded, 16 * B)
            dve.tensor_copy(work[:], sc[:]).then_inc(s_work, 1)
            for k in range(KEEP // 8):
                dve.wait_ge(s_work, k + 1)
                dve.max(best[:], work[:]).then_inc(s_best, 1)
                dve.wait_ge(s_best, k + 1)
                dve.match_replace(work[:], best[:], work[:], -3.0e38).then_inc(s_work, 1)
            dve.wait_ge(s_work, KEEP // 8 + 1)
            dve.tensor_tensor(left[:], work[:], sc[:], ALU.is_equal).then_inc(s_left, 1)
            dve.wait_ge(s_left, 1)
            dve.tensor_scalar(mask[:], left[:], NEG, None, ALU.mult).then_inc(s_mask, 1)


def relative_bias(nc, w, bias):
    R, HID = 2 * N, 32
    with ExitStack() as ctx:
        m = Memory(nc, ctx, "rpe_")
        rel, hid = m.sb("rel", [HID, R]), m.sb("hid", [HID, R])
        w1, b1, w2, b2 = m.sb("w1", [HID, 1]), m.sb("b1", [HID, 1]), m.sb("w2", [HID, H]), m.sb("b2", [H, 1])
        o = m.sb("o", [H, R])
        ps = m.ps("ps", [H, R])
        loaded, hidden, ready, done, stored = (m.sem(n) for n in ("loaded", "hidden", "ready", "done", "stored"))
        block = ctx.enter_context(nc.Block())

        @block.sync
        def _(sp):
            sp.dma_start(rel[:], w["rel"].broadcast_to([HID, R])).then_inc(loaded, 16)
            for dst, name in ((w1, "rpe_w1"), (b1, "rpe_b1"), (w2, "rpe_w2"), (b2, "rpe_b2")):
                sp.dma_start(dst[:], w[name]).then_inc(loaded, 16)
            sp.wait_ge(done, 1)
            sp.dma_start(bias, o[:]).then_inc(stored, 16)
            sp.wait_ge(stored, 16)

        @block.scalar
        def _(act):
            act.wait_ge(loaded, 80)
            act.activation(hid[:], rel[:], ACT.Relu, bias=b1[:], scale=w1[:]).then_inc(hidden, 1)
            act.wait_ge(ready, 1)
            act.activation(o[:], ps[:], ACT.Identity, bias=b2[:]).then_inc(done, 1)

        @block.tensor
        def _(pe):
            pe.wait_ge(loaded, 80)
            pe.wait_ge(hidden, 1)
            for c in range(0, R, 512):
                mm = pe.matmul(ps[:, c:c + 512], w2[:], hid[:, c:c + 512], start=True, stop=True)
            mm.then_inc(ready, 1)


def attend(nc, V, ident, O, qk_parts, pre, bias=None, topmask=None, w=None):
    mixed = topmask is not None
    NR = 3 if mixed else 2
    NTY = 3 if mixed else 1
    KT = 16
    NL = 16 * 13
    with ExitStack() as ctx:
        m = Memory(nc, ctx, pre + "a_")
        qst, kst = m.sb("qst", [64, 2, N], BF16), m.sb("kst", [64, 2, N], BF16)
        vh = m.sb("vh", [P, 2, TB, HD])
        if mixed:
            band = m.sb("band", [P, 3 * P + NGLOB])
        else:
            bt = m.sb("bt", [P, 2, BW])
        z = m.sb("z", [P, 2, 3 * P + NGLOB if mixed else N])
        pr = m.sb("pr", [P, 2, N + (3 * P + NGLOB if mixed else 0)])
        prT = m.sb("prT", [P, 2, NR, 4 * P])
        nmax = m.sb("nmax", [P, 2, 4])
        zs = m.sb("zs", [P, 2, TB, NTY])
        rz = m.sb("rz", [P, TB, NTY])
        ot, osum = m.sb("ot", [P, TB * NTY, HD]), m.sb("osum", [P, TB, HD])
        psS = [m.ps(f"psS{j}", [P, N]) for j in range(2)]
        psG = m.ps("psG", [P, 512]) if mixed else None
        psT = [m.ps(f"psT{j}", [P, 512]) for j in range(2)]
        psO = [m.ps(f"psO{j}", [P, 512]) for j in range(1 if mixed else 2)]
        s = {n: m.sem(n) for n in """const ones load0 load1 vcopy scores scores_g z probs norm rz ot osum passed""".split()}
        turned, turned_sb, pv = ([m.sem(f"{n}{r}") for r in range(NR)] for n in ("turned", "turned_sb", "pv"))
        block = ctx.enter_context(nc.Block())

        def plan(qt, r):
            if not mixed or r < 2:
                return [((4 * r + j) * P, 4 * r + j, P, 0) for j in range(4)]
            lo, hi = max(qt - 1, 0), min(qt + 1, TB - 1)
            return [(N + (j - lo) * P, j, P, 1) for j in range(lo, hi + 1)] + [(N + 3 * P, 0, NGLOB, 2)]

        def band_of(qt):
            lo, hi = max(qt - 1, 0), min(qt + 1, TB - 1)
            return lo * P, (lo - qt + 1) * P, (hi - lo + 1) * P

        @block.sync
        def _(sp):
            if mixed:
                sp.dma_start(band[:], w["band"]).then_inc(s["const"], 16)
            sp.wait_ge(s["ones"], 1)
            with sp.Fori(0, B) as b:
                with sp.Fori(0, H // 2) as hp:
                    for par in range(2):
                        it = b * (H // 2) + hp
                        wait_apart(sp, s["z"], it * KT + (par + 1) * TB, s["passed"])
                        load = s[f"load{par}"]

                        def rows(j, part):
                            return qk_parts[part:part + 1, j, bass.ds(hp * (2 * HD) + par * HD, HD),
                                            bass.ds(b * N, N)]

                        for row, part in enumerate(Q_PARTS):
                            sp.dma_start(qst[row * HD:(row + 1) * HD, par, :],
                                         rows(0, part).rearrange("a d t -> (a d) t")).then_inc(load, 16)
                        for row, part in enumerate(K_PARTS):
                            sp.dma_start(kst[row * HD:(row + 1) * HD, par, :],
                                         rows(1, part).rearrange("a d t -> (a d) t")).then_inc(load, 16)
                        if mixed:
                            sp.dma_start(kst[KS:KS + 1, par, :], topmask[bass.ds(b * H + hp * 2 + par, 1), :])\
                                .then_inc(load, 16)
                        else:
                            a = bias[bass.ds(hp * 2 + par, 1), 0:BW]
                            sp.dma_start(bt[:, par, :], bass.AP(a.tensor, a.offset, [[1, P], [1, BW]]))\
                                .then_inc(load, 16)

        @block.gpsimd
        def _(pool):
            pool.memset(qst[:], 1.0).then_inc(s["ones"], 1)
            with pool.Fori(0, B) as b:
                with pool.Fori(0, H // 2) as hp:
                    for par in range(2):
                        it = b * (H // 2) + hp
                        pool.wait_ge(s["norm"], 2 * it + par + 1)
                        pool.tensor_copy(vh[:, par], V[:, bass.ds(b * TB, TB), bass.ds(hp * (2 * HD) + par * HD, HD)])\
                            .then_inc(s["vcopy"], 1)

        @block.tensor
        def _(pe):
            pe.sem_inc(turned[NR - 1], 2)
            for r in range(NR):
                pe.sem_inc(pv[r], 2)
            pe.wait_ge(s["ones"], 1)
            with pe.Fori(0, B * H // 2) as it:

                def score(k):
                    n, par, qt = it * KT + k, k // TB, k % TB
                    if qt == 0:
                        pe.wait_ge(s[f"load{par}"], NL * it + NL)
                    pe.wait_ge(s["z"], n + 15)
                    if mixed:
                        pe.wait_ge(s["probs"], n + 1)
                    q = slice(qt * P, (qt + 1) * P)
                    rows = KS + 1 if mixed else KS
                    for c in range(2):
                        mm = pe.matmul(psS[k % 2][:, c * 512:(c + 1) * 512], qst[0:rows, par, q],
                                       kst[0:rows, par, c * 512:(c + 1) * 512], start=True, stop=True)
                    mm.then_inc(s["scores"], 1)
                    if mixed:
                        pe.wait_ge(s["z"], n + 16)
                        k0, _, width = band_of(qt)
                        pe.matmul(psG[:, 0:width], qst[0:KS, par, q], kst[0:KS, par, k0:k0 + width],
                                  start=True, stop=True)
                        mm = pe.matmul(psG[:, 3 * P:3 * P + NGLOB], qst[0:KS, par, q], kst[0:KS, par, 0:NGLOB],
                                       start=True, stop=True)
                        mm.then_inc(s["scores_g"], 1)

                def turn(k):
                    n, qt = it * KT + k, k % TB
                    pe.wait_ge(s["probs"], n + 3)
                    for r in range(NR):
                        if r == 2:
                            pe.wait_ge(turned_sb[0], n + 2)
                        else:
                            pe.wait_ge(turned_sb[2 if mixed and r == 0 else r], n + 1)
                        for j, (c0, _, keys, _) in enumerate(plan(qt, r)):
                            mm = pe.transpose(psT[r % 2][0:keys, j * P:(j + 1) * P],
                                              pr[:, k % 2, c0:c0 + keys], ident[:])
                        mm.then_inc(turned[r], 1)

                def times_v(k):
                    n, par, qt = it * KT + k, k // TB, k % TB
                    if qt == 0:
                        pe.wait_ge(s["vcopy"], 2 * it + par + 1)
                        pe.wait_ge(s["norm"], 2 * it + par + (2 if mixed else 1))
                    for r in range(NR):
                        pe.wait_ge(turned_sb[r], n + 2)
                        blocks = plan(qt, r)
                        for j, (_, kb, keys, kind) in enumerate(blocks):
                            c = (qt * NTY + kind) * HD
                            first = kb == 0 if kind == 0 else (kind == 2 or j == 0)
                            last = kb == TB - 1 if kind == 0 else (kind == 2 or blocks[j + 1][3] == 2)
                            mm = pe.matmul(psO[par % len(psO)][:, c:c + HD], prT[0:keys, k % 2, r, j * P:(j + 1) * P],
                                           vh[0:keys, par, kb, :], start=first, stop=last)
                        mm.then_inc(pv[r], 1)

                for k in range(-1, KT + 2):
                    if k + 1 < KT:
                        score(k + 1)
                    if 1 <= k <= KT:
                        turn(k - 1)
                    if k >= 2:
                        times_v(k - 2)

        def copy_round(eng, copy, n, k, r):
            qt, n_par = k % TB, k % 2
            eng.wait_ge(turned[r], n + (3 if r == NR - 1 else 1))
            eng.wait_ge(pv[r], n + 1)
            blocks = plan(qt, r)
            full = sum(keys == P for _, _, keys, _ in blocks)
            c = copy(prT[:, n_par, r, 0:full * P], psT[r % 2][:, 0:full * P])
            if full < len(blocks):
                c = copy(prT[0:NGLOB, n_par, r, full * P:(full + 1) * P], psT[r % 2][0:NGLOB, full * P:(full + 1) * P])
            c.then_inc(turned_sb[r], 1)

        @block.scalar
        def _(act):
            act.sem_inc(s["probs"], 2)
            act.sem_inc(turned_sb[1], 1)
            with act.Fori(0, B * H // 2) as it:
                for k in range(KT + 1):
                    if k < KT:
                        n, par, qt = it * KT + k, k // TB, k % TB
                        act.wait_ge(s["z"], n + 17)
                        act.wait_ge(turned[NR - 1], n + 1)
                        if qt == 0:
                            act.wait_ge(s["norm"], 2 * it + par + 1)
                        nm = nmax[:, k % 2, :]
                        if mixed:
                            _, _, width = band_of(qt)
                            act.activation(pr[:, k % 2, 0:N], psS[k % 2][:], ACT.Exp, bias=nm[:, 0:1],
                                           accum_out=zs[:, par, qt, 0:1])
                            act.activation(pr[:, k % 2, N:N + width], z[:, k % 2, 0:width], ACT.Exp, bias=nm[:, 1:2],
                                           scale=-1.0, accum_out=zs[:, par, qt, 1:2])
                            e = act.activation(pr[:, k % 2, N + 3 * P:N + 3 * P + NGLOB],
                                               z[:, k % 2, 3 * P:3 * P + NGLOB], ACT.Exp, bias=nm[:, 2:3],
                                               scale=-1.0, accum_out=zs[:, par, qt, 2:3])
                        else:
                            e = act.activation(pr[:, k % 2, :], z[:, k % 2, :], ACT.Exp, bias=nm[:, 0:1], scale=-1.0,
                                               accum_out=zs[:, par, qt, 0:1])
                        e.then_inc(s["probs"], 1)
                    if k >= 1:
                        copy_round(act, lambda o, i: act.activation(o, i, ACT.Copy), it * KT + k - 1, k - 1, 1)

        @block.vector
        def _(dve):
            dve.sem_inc(s["z"], 16)
            dve.sem_inc(s["norm"], 2)
            dve.sem_inc(turned_sb[0], 1)
            if mixed:
                dve.sem_inc(turned_sb[2], 1)
                dve.wait_ge(s["const"], 16)
            with dve.Fori(0, B) as b:
                with dve.Fori(0, H // 2) as hp:
                    it = b * (H // 2) + hp

                    def maxima(k):
                        n, par, qt = it * KT + k, k // TB, k % TB
                        dve.wait_ge(s["scores"], n + 1)
                        dve.wait_ge(s["probs"], n + 1)
                        nm = nmax[:, k % 2, :]
                        if mixed:
                            dve.tensor_reduce(nm[:, 0:1], psS[k % 2][:], AX.X, ALU.max, negate=True)
                            if k >= 2:
                                copy_round(dve, dve.tensor_copy, it * KT + k - 2, k - 2, 0)
                            _, c0, width = band_of(qt)
                            wait_apart(dve, s["scores_g"], n + 1, s["passed"])
                            dve.tensor_tensor_reduce(z[:, k % 2, 0:width], psG[:, 0:width],
                                                     band[:, c0:c0 + width], -1.0, 3.0e38, ALU.add, ALU.min, nm[:, 1:2])
                            g = slice(3 * P, 3 * P + NGLOB)
                            dve.tensor_tensor_reduce(z[:, k % 2, g], psG[:, g], band[:, g], -1.0, 3.0e38,
                                                     ALU.add, ALU.min, nm[:, 2:3]).then_inc(s["z"], 1)
                        else:
                            c0 = (TB - 1 - qt) * P
                            wait_apart(dve, s[f"load{par}"], NL * it + NL, s["passed"])
                            dve.tensor_tensor_reduce(z[:, k % 2, :], psS[k % 2][:], bt[:, par, c0:c0 + N], -1.0, 3.0e38,
                                                     ALU.add, ALU.min, nm[:, 0:1]).then_inc(s["z"], 1)

                    def normalize(par):
                        n = it * KT + par * TB + TB - 1
                        nh = 2 * it + par
                        dve.wait_ge(s["probs"], n + 3)
                        dve.reciprocal(rz[:], zs[:, par]).then_inc(s["rz"], 1)
                        dve.wait_ge(pv[NR - 1], n + 3)
                        dve.wait_ge(s["rz"], nh + 1)
                        sums = psO[par % len(psO)][:, 0:TB * NTY * HD].rearrange("p (q d) -> p q d", d=HD)
                        rzb = rz[:].rearrange("p q (k a) -> p (q k) a", a=1).broadcast_to([P, TB * NTY, HD])
                        dst = O[:, bass.ds(b * TB, TB), bass.ds(hp * (2 * HD) + par * HD, HD)]
                        if mixed:
                            dve.tensor_tensor(ot[:], sums, rzb, ALU.mult).then_inc(s["ot"], 1)
                            dve.wait_ge(s["ot"], nh + 1)
                            dve.tensor_reduce(osum[:], ot[:].rearrange("p (q k) d -> p q d k", k=NTY), AX.X, ALU.add)\
                                .then_inc(s["osum"], 1)
                            dve.wait_ge(s["osum"], nh + 1)
                            dve.tensor_scalar(dst, osum[:], 1.0 / 3.0, None, ALU.mult).then_inc(s["norm"], 1)
                        else:
                            dve.tensor_tensor(dst, sums, rzb, ALU.mult).then_inc(s["norm"], 1)

                    for k in range(-1, KT + 3):
                        if k + 1 < KT:
                            maxima(k + 1)
                        if 1 <= k <= KT and not (mixed and k + 1 < KT):
                            copy_round(dve, dve.tensor_copy, it * KT + k - 1, k - 1, 0)
                        if 1 <= k <= KT and mixed:
                            copy_round(dve, dve.tensor_copy, it * KT + k - 1, k - 1, 2)
                        if k >= 3 and (k - 3) % TB == TB - 1:
                            normalize((k - 3) // TB)


def project_out(nc, O, X, ident, w, pre, flip):
    with ExitStack() as ctx:
        m = Memory(nc, ctx, pre + "o_")
        wo, bo, ones = m.sb("wo", [P, D]), m.sb("bo", [1, D]), m.sb("ones", [1, P])
        ocur, oT = m.sb("ocur", [P, D]), m.sb("oT", [P, D])
        psT, psY = m.ps("psT", [P, 512]), m.ps("psY", [P, 512])
        s = {n: m.sem(n) for n in "weights one cur turned oT y added".split()}
        block = ctx.enter_context(nc.Block())

        @block.sync
        def _(sp):
            sp.dma_start(wo[:], w[pre + "wo"]).then_inc(s["weights"], 16)
            sp.dma_start(bo[:], w[pre + "bo"]).then_inc(s["weights"], 16)
            sp.wait_ge(s["weights"], 32)

        @block.gpsimd
        def _(pool):
            pool.memset(ones[:], 1.0).then_inc(s["one"], 1)
            with pool.Fori(0, NT) as t:
                pool.wait_ge(s["turned"], t + 1)
                pool.tensor_copy(ocur[:], O[:, bass.ds(t, 1), :].rearrange("p a f -> p (a f)")).then_inc(s["cur"], 1)

        @block.tensor
        def _(pe):
            pe.sem_inc(s["turned"], 1)
            pe.wait_ge(s["weights"], 32)
            pe.wait_ge(s["one"], 1)
            with pe.Fori(0, NT) as t:
                pe.wait_ge(s["cur"], t + 1)
                pe.wait_ge(s["oT"], t + 1)
                pe.transpose(psT[:, 0:P], ocur[:], ident[:]).then_inc(s["turned"], 1)
                pe.wait_ge(s["oT"], t + 2)
                pe.wait_ge(s["added"], t + 1)
                pe.matmul(psY[:, 0:D], oT[:], wo[:], start=True, stop=False)
                pe.matmul(psY[:, 0:D], ones[:], bo[:], start=False, stop=True).then_inc(s["y"], 1)

        @block.scalar
        def _(act):
            act.sem_inc(s["oT"], 1)
            act.sem_inc(s["y"], 1)
            with act.Fori(0, NT) as t:
                act.wait_ge(s["turned"], t + 2)
                act.wait_ge(s["y"], t + 1)
                if flip:
                    act.activation(flipped(oT[:], 1), psT[:, 0:P].rearrange("p (t c) -> p t c", c=P), ACT.Copy)\
                        .then_inc(s["oT"], 1)
                else:
                    act.activation(oT[:], psT[:, 0:P], ACT.Copy).then_inc(s["oT"], 1)

        @block.vector
        def _(dve):
            dve.sem_inc(s["added"], 1)
            with dve.Fori(0, NT) as t:
                dve.wait_ge(s["y"], t + 2)
                x = X[:, bass.ds(t, 1), :].rearrange("p a f -> p (a f)")
                dve.tensor_tensor(x, psY[:, 0:D], x, ALU.add).then_inc(s["added"], 1)


L, MH = B, 4
MD = D // MH
E, FF = 8, 512
CAP = B * N // E


def cross_attention(nc, XN, Y, ident, w):
    with ExitStack() as ctx:
        m = Memory(nc, ctx, "m_")
        win, bin_ = m.sb("win", [P, 3 * D]), m.sb("bin", [P, 3 * D])
        wout, bout = m.sb("wout", [P, D]), m.sb("bout", [P, D])
        xcur, xT = m.sb("xcur", [P, L, D]), m.sb("xT", [P, L, P])
        qkv = m.sb("qkv", [P, L, 3 * D])
        prod = m.sb("prod", [P, L, L, D])
        sc, sub, ex, pn = (m.sb(n, [P, L * L * MH]) for n in ("sc", "sub", "ex", "pn"))
        mx, zs, rz = (m.sb(n, [P, L * MH]) for n in ("mx", "zs", "rz"))
        o, oT = m.sb("o", [P, L, D]), m.sb("oT", [P, L, P])
        yb = m.sb("yb", [P, L, D])
        psX, psQ, psY = m.ps("psX", [P, 512]), m.ps("psQ", [P, L, 512]), m.ps("psY", [P, 512])
        s = {n: m.sem(n) for n in """weights x xT_ps xT qkv_ps qkv prod sc mx sub ex zs rz pn pv o oT_ps oT
            y_ps yb y""".split()}
        block = ctx.enter_context(nc.Block())
        scale = 1.0 / float(np.sqrt(MD))

        @block.sync
        def _(sp):
            sp.dma_start(win[:], w["m_win"]).then_inc(s["weights"], 16)
            sp.dma_start(bin_[:], w["m_bin"].broadcast_to([P, 3 * D])).then_inc(s["weights"], 16)
            sp.dma_start(wout[:], w["m_wout"]).then_inc(s["weights"], 16)
            sp.dma_start(bout[:], w["m_bout"].broadcast_to([P, D])).then_inc(s["weights"], 16)
            sp.wait_ge(s["weights"], 64)

        @block.gpsimd
        def _(pool):
            with pool.Fori(0, TB) as j:
                pool.wait_ge(s["y"], j + 1)
                pool.tensor_copy(xcur[:], XN[:].rearrange("p (l j) f -> p l j f", l=L)[:, :, bass.ds(j, 1), :]
                                 .rearrange("p l a f -> p l (a f)")).then_inc(s["x"], 1)

        @block.tensor
        def _(pe):
            pe.wait_ge(s["weights"], 64)
            with pe.Fori(0, TB) as j:
                pe.wait_ge(s["x"], j + 1)
                for l in range(L):
                    mm = pe.transpose(psX[:, l * P:(l + 1) * P], xcur[:, l, :], ident[:])
                mm.then_inc(s["xT_ps"], 1)
                pe.wait_ge(s["xT"], j + 1)
                for l in range(L):
                    mm = pe.matmul(psQ[:, l, 0:3 * D], xT[:, l, :], win[:], start=True, stop=True)
                mm.then_inc(s["qkv_ps"], 1)
                pe.wait_ge(s["o"], j + 1)
                for l in range(L):
                    mm = pe.transpose(psX[:, l * P:(l + 1) * P], o[:, l, :], ident[:])
                mm.then_inc(s["oT_ps"], 1)
                pe.wait_ge(s["oT"], j + 1)
                for l in range(L):
                    mm = pe.matmul(psY[:, l * P:(l + 1) * P], oT[:, l, :], wout[:], start=True, stop=True)
                mm.then_inc(s["y_ps"], 1)

        @block.scalar
        def _(act):
            with act.Fori(0, TB) as j:
                act.wait_ge(s["xT_ps"], j + 1)
                act.activation(xT[:].rearrange("p l c -> p (l c)"), psX[:], ACT.Copy).then_inc(s["xT"], 1)
                act.wait_ge(s["sub"], j + 1)
                act.activation(ex[:], sub[:], ACT.Exp, scale=scale).then_inc(s["ex"], 1)
                act.wait_ge(s["oT_ps"], j + 1)
                act.activation(oT[:].rearrange("p l c -> p (l c)"), psX[:], ACT.Copy).then_inc(s["oT"], 1)

        @block.vector
        def _(dve):
            dve.sem_inc(s["y"], 1)
            dve.wait_ge(s["weights"], 64)
            with dve.Fori(0, TB) as j:
                dve.wait_ge(s["qkv_ps"], j + 1)
                dve.tensor_tensor(qkv[:], psQ[:, :, 0:3 * D],
                                  bin_[:].rearrange("p (a f) -> p a f", a=1).broadcast_to([P, L, 3 * D]), ALU.add)\
                    .then_inc(s["qkv"], 1)
                dve.wait_ge(s["qkv"], j + 1)
                for l in range(L):
                    d = dve.tensor_tensor(prod[:, l], qkv[:, l:l + 1, 0:D].broadcast_to([P, L, D]), qkv[:, :, D:2 * D],
                                          ALU.mult)
                d.then_inc(s["prod"], 1)
                dve.wait_ge(s["prod"], j + 1)
                dve.tensor_reduce(sc[:], prod[:].rearrange("p l m (h d) -> p (l m h) d", d=MD), AX.X, ALU.add)\
                    .then_inc(s["sc"], 1)
                dve.wait_ge(s["sc"], j + 1)
                by_key = "p (l m h) -> p l h m"
                dve.tensor_reduce(mx[:].rearrange("p (l h) -> p l h", l=L), sc[:].rearrange(by_key, l=L, m=L), AX.X,
                                  ALU.max).then_inc(s["mx"], 1)
                dve.wait_ge(s["mx"], j + 1)
                over = lambda t: t[:].rearrange("p (l a h) -> p l a h", l=L, a=1).broadcast_to([P, L, L, MH])
                lmh = lambda t: t[:].rearrange("p (l m h) -> p l m h", l=L, m=L)
                dve.tensor_tensor(lmh(sub), lmh(sc), over(mx), ALU.subtract).then_inc(s["sub"], 1)
                dve.wait_ge(s["ex"], j + 1)
                dve.tensor_reduce(zs[:].rearrange("p (l h) -> p l h", l=L), ex[:].rearrange(by_key, l=L, m=L), AX.X,
                                  ALU.add).then_inc(s["zs"], 1)
                dve.wait_ge(s["zs"], j + 1)
                dve.reciprocal(rz[:], zs[:]).then_inc(s["rz"], 1)
                dve.wait_ge(s["rz"], j + 1)
                dve.tensor_tensor(lmh(pn), lmh(ex), over(rz), ALU.mult).then_inc(s["pn"], 1)
                dve.wait_ge(s["pn"], j + 1)
                for l in range(L):
                    d = dve.tensor_tensor(
                        prod[:, l].rearrange("p m (h d) -> p m h d", h=MH),
                        pn[:, l * L * MH:(l + 1) * L * MH].rearrange("p (m h a) -> p m h a", m=L, a=1)
                        .broadcast_to([P, L, MH, MD]),
                        qkv[:, :, 2 * D:3 * D].rearrange("p m (h d) -> p m h d", h=MH), ALU.mult)
                d.then_inc(s["pv"], 1)
                dve.wait_ge(s["pv"], j + 1)
                dve.tensor_reduce(o[:], prod[:].rearrange("p l m f -> p l f m"), AX.X, ALU.add).then_inc(s["o"], 1)
                dve.wait_ge(s["y_ps"], j + 1)
                dve.tensor_tensor(yb[:], psY[:].rearrange("p (l f) -> p l f", l=L),
                                  bout[:].rearrange("p (a f) -> p a f", a=1).broadcast_to([P, L, D]), ALU.add)\
                    .then_inc(s["yb"], 1)
                dve.wait_ge(s["yb"], j + 1)
                dve.tensor_tensor(Y[:].rearrange("p (l j) f -> p l j f", l=L)[:, :, bass.ds(j, 1), :]
                                  .rearrange("p l a f -> p l (a f)"), yb[:], xcur[:], ALU.add).then_inc(s["y"], 1)


def scale_shift(nc, Y, w, g, b, X=None):
    with ExitStack() as ctx:
        m = Memory(nc, ctx, g + "_")
        gb, bb = m.sb("g", [P, D]), m.sb("b", [P, D])
        loaded, scaled, shifted_, = (m.sem(n) for n in ("loaded", "scaled", "shifted"))
        block = ctx.enter_context(nc.Block())

        @block.sync
        def _(sp):
            sp.dma_start(gb[:], w[g].broadcast_to([P, D])).then_inc(loaded, 16)
            sp.dma_start(bb[:], w[b].broadcast_to([P, D])).then_inc(loaded, 16)
            sp.wait_ge(loaded, 32)

        @block.vector
        def _(dve):
            row = lambda t: t[:].rearrange("p (a f) -> p a f", a=1).broadcast_to([P, NT, D])
            dve.wait_ge(loaded, 32)
            dve.tensor_tensor(Y[:], Y[:], row(gb), ALU.mult).then_inc(scaled, 1)
            dve.wait_ge(scaled, 1)
            dve.tensor_tensor(Y[:], Y[:], row(bb), ALU.add).then_inc(shifted_, 1)
            if X is not None:
                dve.wait_ge(shifted_, 1)
                dve.tensor_tensor(X[:], X[:], Y[:], ALU.add)


def experts(nc, Y, YS, ident, w):
    FK = FF // P
    with ExitStack() as ctx:
        m = Memory(nc, ctx, "e_")
        w1T, w2 = m.sb("w1T", [P, E * FK, D]), m.sb("w2", [P, E * FK, D])
        b1 = m.sb("b1", [P, E * FK])
        w12, b12, b2 = m.sb("w12", [P, E * D]), m.sb("b12", [1, E * D]), m.sb("b2", [1, E * D])
        wg, ones, first = m.sb("wg", [P, E]), m.sb("ones", [P, P]), m.sb("first", [P, E])
        upper = m.sb("upper", [P, P])
        ycur, yT = m.sb("ycur", [P, D]), m.sb("yT", [P, P])
        nmx, mx, eq, best, z, ex = (m.sb(n, [P, k]) for n, k in
                                    (("nmx", 1), ("mx", 1), ("eq", E), ("best", 1), ("z", 1), ("ex", E)))
        one = m.sb("one", [P, E])
        prod = m.sb("prod", [P, E, D])
        hot, gate = m.sb("hot", [P, NT, E]), m.sb("gate", [P, NT])
        before = [m.sb(f"before{k}", [P, NT, E]) for k in range(2)]
        rank, mine, keep = m.sb("rank", [P, NT, E]), m.sb("mine", [P, NT]), m.sb("keep", [P, NT])
        psT, psG = m.ps("psT", [P, 512]), m.ps("psG", [P, 512])
        psE, psW = m.ps("psE", [P, E * D]), m.ps("psW", [P, E * D])
        psC, psA = m.ps("psC", [P, 512]), m.ps("psA", [P, 512])
        s = {n: m.sem(n) for n in """weights const w12_ps w12 b12_ps b12 y yT_ps yT logits picked_e nmx mx eq best
            one ex rz prod picked hot counts chain kept""".split()}
        block = ctx.enter_context(nc.Block())
        NW = 16 * 8

        @block.sync
        def _(sp):
            for dst, name in ((w1T, "e_w1T"), (w2, "e_w2"), (b1, "e_b1"), (b2, "e_b2"), (wg, "e_wg"),
                              (first, "first"), (upper, "upper"), (ones, "ones")):
                sp.dma_start(dst[:], w[name]).then_inc(s["weights"], 16)
            sp.wait_ge(s["weights"], NW)

        @block.gpsimd
        def _(pool):
            with pool.Fori(0, NT) as t:
                pool.wait_ge(s["yT_ps"], t + 1)
                pool.tensor_copy(ycur[:], Y[:, bass.ds(t, 1), :].rearrange("p a f -> p (a f)")).then_inc(s["y"], 1)

        @block.tensor
        def _(pe):
            pe.sem_inc(s["yT_ps"], 1)
            pe.wait_ge(s["weights"], NW)
            for e in range(E):
                for k in range(FK):
                    mm = pe.matmul(psW[:, e * D:(e + 1) * D], w1T[:, e * FK + k, :], w2[:, e * FK + k, :],
                                   start=(k == 0), stop=(k == FK - 1))
            mm.then_inc(s["w12_ps"], 1)
            for e in range(E):
                for k in range(FK):
                    mm = pe.matmul(psE[0:1, e * D:(e + 1) * D], b1[:, e * FK + k:e * FK + k + 1],
                                   w2[:, e * FK + k, :], start=(k == 0), stop=(k == FK - 1))
            mm.then_inc(s["b12_ps"], 1)
            pe.wait_ge(s["w12"], 1)
            pe.wait_ge(s["b12"], 1)
            with pe.Fori(0, NT) as t:
                pe.wait_ge(s["y"], t + 1)
                pe.wait_ge(s["yT"], t + 1)
                pe.transpose(psT[:, 0:P], ycur[:], ident[:]).then_inc(s["yT_ps"], 1)
                pe.wait_ge(s["yT"], t + 2)
                pe.wait_ge(s["ex"], t + 1)
                pe.matmul(psG[:, 0:E], yT[:], wg[:], start=True, stop=True).then_inc(s["logits"], 1)
                pe.wait_ge(s["prod"], t + 1)
                for c in range(0, E * D, 512):
                    pe.matmul(psE[:, c:c + 512], yT[:], w12[:, c:c + 512], start=True, stop=False)
                    mm = pe.matmul(psE[:, c:c + 512], ones[0:1, :], b12[:, c:c + 512], start=False, stop=True)
                mm.then_inc(s["picked_e"], 1)
            pe.wait_ge(s["hot"], NT)
            hots = hot[:].rearrange("p t e -> p (t e)")
            pe.matmul(psC[:, 0:NT * E], upper[:], hots, start=True, stop=True)
            pe.matmul(psA[:, 0:NT * E], ones[:], hots, start=True, stop=True).then_inc(s["counts"], 1)

        @block.scalar
        def _(act):
            act.sem_inc(s["yT"], 1)
            act.sem_inc(s["ex"], 1)
            act.wait_ge(s["w12_ps"], 1)
            act.activation(w12[:], psW[:], ACT.Copy).then_inc(s["w12"], 1)
            with act.Fori(0, NT) as t:
                act.wait_ge(s["yT_ps"], t + 2)
                act.wait_ge(s["logits"], t + 1)
                act.activation(yT[:], psT[:, 0:P], ACT.Copy).then_inc(s["yT"], 1)
                act.wait_ge(s["eq"], t + 1)
                act.wait_ge(s["rz"], t + 1)
                act.activation(ex[:], psG[:, 0:E], ACT.Exp, bias=nmx[:], accum_out=z[:]).then_inc(s["ex"], 1)

        @block.vector
        def _(dve):
            dve.sem_inc(s["prod"], 1)
            dve.sem_inc(s["logits"], 1)
            dve.sem_inc(s["rz"], 1)
            dve.wait_ge(s["weights"], NW)
            dve.wait_ge(s["b12_ps"], 1)
            dve.tensor_tensor(b12[:], psE[0:1, :], b2[:], ALU.add).then_inc(s["b12"], 1)
            with dve.Fori(0, NT) as t:
                dve.wait_ge(s["logits"], t + 2)
                dve.tensor_reduce(nmx[:], psG[:, 0:E], AX.X, ALU.max, negate=True)
                dve.tensor_reduce(mx[:], psG[:, 0:E], AX.X, ALU.max).then_inc(s["mx"], 1)
                dve.wait_ge(s["mx"], t + 1)
                dve.scalar_tensor_tensor(eq[:], psG[:, 0:E], mx[:], first[:], ALU.is_equal, ALU.mult)\
                    .then_inc(s["eq"], 1)
                dve.wait_ge(s["eq"], t + 1)
                dve.tensor_reduce(best[:], eq[:], AX.X, ALU.max).then_inc(s["best"], 1)
                dve.wait_ge(s["best"], t + 1)
                dve.tensor_scalar(one[:], eq[:], best[:], None, ALU.is_equal).then_inc(s["one"], 1)
                dve.wait_ge(s["one"], t + 1)
                dve.tensor_copy(hot[:, bass.ds(t, 1), :].rearrange("p a e -> p (a e)"), one[:]).then_inc(s["hot"], 1)
                dve.wait_ge(s["picked_e"], t + 1)
                dve.tensor_tensor(prod[:], psE[:].rearrange("p (e f) -> p e f", e=E),
                                  one[:].rearrange("p (e a) -> p e a", a=1).broadcast_to([P, E, D]), ALU.mult)\
                    .then_inc(s["prod"], 1)
                dve.wait_ge(s["prod"], t + 2)
                dve.tensor_reduce(YS[:, bass.ds(t, 1), :].rearrange("p a f -> p (a f)"),
                                  prod[:].rearrange("p e f -> p f e"), AX.X, ALU.add).then_inc(s["picked"], 1)
                dve.wait_ge(s["ex"], t + 2)
                dve.reciprocal(gate[:, bass.ds(t, 1)], z[:]).then_inc(s["rz"], 1)
            dve.wait_ge(s["counts"], 1)
            n = 0
            dve.memset(before[0][:, 0:1, :], 0.0)
            dve.tensor_copy(before[0][:, 1:NT, :], psA[:, 0:(NT - 1) * E].rearrange("p (t e) -> p t e", e=E))\
                .then_inc(s["chain"], 1)
            for k in range(5):
                a, z_, step = before[k % 2], before[(k + 1) % 2], 1 << k
                dve.wait_ge(s["chain"], k + 1)
                dve.tensor_copy(z_[:, 0:step, :], a[:, 0:step, :])
                dve.tensor_tensor(z_[:, step:NT, :], a[:, step:NT, :], a[:, 0:NT - step, :], ALU.add)\
                    .then_inc(s["chain"], 1)
            dve.wait_ge(s["chain"], 6)
            dve.tensor_tensor(rank[:].rearrange("p t e -> p (t e)"), psC[:, 0:NT * E],
                              before[1][:].rearrange("p t e -> p (t e)"), ALU.add).then_inc(s["chain"], 1)
            dve.wait_ge(s["chain"], 7)
            dve.tensor_tensor(rank[:], rank[:], hot[:], ALU.mult).then_inc(s["chain"], 1)
            dve.wait_ge(s["chain"], 8)
            dve.tensor_reduce(mine[:], rank[:], AX.X, ALU.add).then_inc(s["chain"], 1)
            dve.wait_ge(s["chain"], 9)
            dve.tensor_scalar(mine[:], mine[:], float(CAP), None, ALU.is_le).then_inc(s["chain"], 1)
            dve.wait_ge(s["chain"], 10)
            dve.wait_ge(s["rz"], NT + 1)
            dve.tensor_tensor(keep[:], mine[:], gate[:], ALU.mult).then_inc(s["chain"], 1)
            dve.wait_ge(s["chain"], 11)
            dve.wait_ge(s["picked"], NT)
            dve.tensor_tensor(YS[:], YS[:], keep[:].rearrange("p (t a) -> p t a", a=1).broadcast_to([P, NT, D]),
                              ALU.mult).then_inc(s["chain"], 1)
            dve.wait_ge(s["chain"], 12)
            dve.tensor_tensor(Y[:], Y[:], YS[:], ALU.add).then_inc(s["kept"], 1)


def constants():
    bf16 = np.dtype("bfloat16")
    c = {}
    c["ident"] = np.eye(P, dtype=np.float32)
    c["identb"] = np.eye(P).astype(bf16)
    hd = np.arange(0, WD, 2, dtype=np.float32)
    inv_freq = (1.0 / np.float32(10000.0) ** (hd / np.float32(WD))).astype(np.float32)
    pos = np.arange(N, dtype=np.float32)
    freqs = (pos[:, None] * inv_freq[None, :]).astype(np.float32)
    freqs = np.concatenate([freqs, freqs], -1).astype(np.float64)
    base = (hd + 0.4 * WD) / (1.4 * WD)
    power = (pos - N // 2) / (WIN // 2)
    scale = base.astype(np.float64)[None, :] ** power.astype(np.float64)[:, None]
    scale = np.concatenate([scale, scale], -1)
    sign = np.where(np.arange(WD) < WD // 2, -1.0, 1.0)[None, :]
    rot = np.empty((N, 2, 2, WD), np.float64)
    rot[:, 0, 0], rot[:, 0, 1] = 8 * np.cos(freqs) * scale, 8 * np.sin(freqs) * scale * sign
    rot[:, 1, 0], rot[:, 1, 1] = np.cos(freqs) / scale, np.sin(freqs) / scale * sign
    c["rot"] = rot.reshape(TB, P, 2, 2, WD).transpose(1, 0, 2, 3, 4).astype(np.float32)
    key = np.concatenate([np.arange(P), np.arange(-WIN, 0)])
    back = np.arange(P)[:, None] - key[None, :]
    m = np.where((back >= 0) & (back <= WIN), 0.0, NEG)
    m = np.repeat(m[:, None, None, :], TB, 1).repeat(2, 2)
    m[:, 0, :, P:] = NEG
    f = np.ones((P, TB), np.float32)
    f[:, TB - 1] = 0.0
    around = np.arange(-1, TB + 1) % TB
    c["wmask"] = m[:, around].astype(bf16)
    c["flag"] = f[:, around]
    off = np.arange(3 * P)[None, :] - P - np.arange(P)[:, None]
    c["band"] = np.concatenate([np.where(np.abs(off) <= P, 0.0, NEG), np.zeros((P, NGLOB))], 1).astype(np.float32)
    c["first"] = np.tile(np.arange(E, 0, -1, dtype=np.float32), (P, 1))
    c["upper"] = np.triu(np.ones((P, P), np.float32))
    c["ones"] = np.ones((P, P), np.float32)
    d = (N - 1 - np.arange(2 * N)).astype(np.float32)
    c["rel"] = (np.sign(d) * np.log1p(np.abs(d))).astype(np.float32)[None, :]
    return c

def layout(inputs):
    a = {k: np.asarray(v) for k, v in inputs.items()}
    w = {"x": a["L0_attn_x"]}
    pre = "L1_ffn_"
    for name in ("Wo", "W1", "W2", "b1", "b2", "ln_g", "ln_b", "q_scale", "k_scale"):
        w[name] = a[pre + name]
    w["Wqkv"] = a[pre + "Wqkv"].reshape(DEPTH, D, 3, NG, GW).transpose(0, 1, 3, 2, 4).reshape(DEPTH, D, NG, 3 * GW)
    pre = "L0_attn_"
    for n in "qkv":
        w["A" + "w" + n] = a[pre + "W" + n].T
    w["Awo"], w["Aws"] = a[pre + "Wo"].T, a[pre + "Ws"].T
    w["Abq"], w["Abk"], w["Abs"] = (a[pre + n].reshape(-1, 1) for n in ("bq", "bk", "bs"))
    w["Abv"], w["Abo"] = a[pre + "bv"].reshape(1, -1), a[pre + "bo"].reshape(1, -1)
    pre = "L1_attn_"
    for j, n in enumerate("qkv"):
        w["Cw" + n] = a[pre + "w_qkv"][:, j * D:(j + 1) * D]
        w["Cb" + n] = a[pre + "b_qkv"][j * D:(j + 1) * D].reshape((1, -1) if n == "v" else (-1, 1))
    w["Cwo"], w["Cbo"] = a[pre + "w_out"], a[pre + "b_out"].reshape(1, -1)
    w["rpe_w1"], w["rpe_b1"] = a[pre + "w1_rpe"].reshape(-1, 1), a[pre + "b1_rpe"].reshape(-1, 1)
    w["rpe_w2"], w["rpe_b2"] = a[pre + "w2_rpe"], a[pre + "b2_rpe"].reshape(-1, 1)
    pre = "L0_ffn_"
    w["m_win"], w["m_bin"] = a[pre + "in_proj_w"].T, a[pre + "in_proj_b"].reshape(1, -1)
    w["m_wout"], w["m_bout"] = a[pre + "out_proj_w"].T, a[pre + "out_proj_b"].reshape(1, -1)
    for n in ("ln1_g", "ln1_b", "ln2_g", "ln2_b"):
        w[n] = a[pre + n].reshape(1, -1)
    w["e_w1T"] = a[pre + "w1"].reshape(E, D, FF // P, P).transpose(3, 0, 2, 1).reshape(P, -1, D)
    w["e_w2"] = a[pre + "w2"].reshape(E, FF // P, P, D).transpose(2, 0, 1, 3).reshape(P, -1, D)
    w["e_b1"] = a[pre + "b1"].reshape(E * (FF // P), P).T
    w["e_b2"], w["e_wg"] = a[pre + "b2"].reshape(1, -1), a[pre + "wg"]
    w.update(constants())
    return {k: np.ascontiguousarray(v) for k, v in w.items()}


def build(nc, w, out):
    with ExitStack() as ctx:
        X = ctx.enter_context(nc.sbuf_tensor("X", [P, NT, D], F32))
        XN = ctx.enter_context(nc.sbuf_tensor("XN", [P, NT, D], F32))
        ident = ctx.enter_context(nc.sbuf_tensor("ident", [P, P], F32))
        qk_parts = nc.dram_tensor("qk_parts", (SP3, 2, P, B * N), BF16, kind="Internal").ap()
        scores = nc.dram_tensor("scores", (H, B * N), F32, kind="Internal").ap()
        topmask = nc.dram_tensor("topmask", (B * H, N), BF16, kind="Internal").ap()
        bias = nc.dram_tensor("bias", (H, 2 * N), F32, kind="Internal").ap()
        load_and_normalize(nc, w["x"], w["ident"], X, XN, ident)
        with ExitStack() as inner:
            V = inner.enter_context(nc.sbuf_tensor("V", [P, NT, D], F32))
            O = inner.enter_context(nc.sbuf_tensor("O", [P, NT, D], F32))
            project_heads(nc, XN, ident, V, w, "A", qk_parts, scores, False)
            select_keys(nc, scores, topmask)
            attend(nc, V, ident, O, qk_parts, "A", topmask=topmask, w=w)
            project_out(nc, O, X, ident, w, "A", False)
            cross_attention(nc, XN, V, ident, w)
            layer_norm(nc, V, V, "ln1_")
            scale_shift(nc, V, w, "ln1_g", "ln1_b")
            experts(nc, V, O, ident, w)
            layer_norm(nc, V, V, "ln2_")
            scale_shift(nc, V, w, "ln2_g", "ln2_b", X)
            layer_norm(nc, X, XN, "ln3_")
            relative_bias(nc, w, bias)
            project_heads(nc, XN, ident, V, w, "C", qk_parts, None, True)
            attend(nc, V, ident, O, qk_parts, "C", bias=bias)
            project_out(nc, O, X, ident, w, "C", True)
        windowed_layers(nc, XN, ident, w)
        add_into(nc, X, XN)
        stored = ctx.enter_context(nc.semaphore("stored"))
        block = ctx.enter_context(nc.Block())

        @block.sync
        def _(sp):
            sp.dma_start(tokens(out), X[:]).then_inc(stored, 16)
            sp.wait_ge(stored, 16)


def kernel(**inputs):
    import concourse.bacc as _bacc
    from concourse import mybir as _mybir
    from concourse.bass_utils import run_bass_kernel_spmd as _run
    nc = _bacc.Bacc("TRN2", target_bir_lowering=False, num_devices=1)
    arrays = layout(inputs)
    w = {k: nc.dram_tensor(k + "_dram", v.shape, _mybir.dt.from_np(v.dtype), kind="ExternalInput").ap()
         for k, v in arrays.items()}
    o = nc.dram_tensor("out", (B, N, D), F32, kind="ExternalOutput").ap()
    build(nc, w, o)
    r = _run(nc, [{k + "_dram": v for k, v in arrays.items()}], core_ids=[0])
    return r.results[0]["out"]
```
